# Optimizing a Trainium2 kernel written in Bass

```python
import numpy as np
import jax
import jax.numpy as jnp

def _softmax(x, axis=-1):
    return jax.nn.softmax(x, axis=axis)

def _gelu(x):
    return jax.nn.gelu(x, approximate=True)

def _silu(x):
    return jax.nn.silu(x)

def _sigmoid(x):
    return jax.nn.sigmoid(x)

def _layernorm(x, axis=-1, eps=1e-05):
    m = jnp.mean(x, axis=axis, keepdims=True)
    v = jnp.var(x, axis=axis, keepdims=True)
    return (x - m) / jnp.sqrt(v + eps)

def _scatter_add(tgt, idx, src, axis=0):
    return tgt.at[idx].add(src)

def _segment_sum(src, seg, n):
    return jax.ops.segment_sum(src, seg, n)
kernel_name = 'mk_prb_d4_jaxref_r8_629be7'

def setup_inputs(seed: int=0):
    np.random.seed(seed)
    _w = jnp.asarray

    def _L0_attn_setup():
        import math
        import jax, jax.numpy as jnp
        import numpy as np

        def _rope_tables(T, h, dtype):
            pos = jnp.arange(T, dtype=jnp.float32)
            thetas = 1.0 / 10000.0 ** (jnp.arange(0, h, 2, dtype=jnp.float32) / h)
            pt = jnp.outer(pos, thetas)
            pt = jnp.concatenate([pt, pt], axis=-1)
            return (jnp.sin(pt).astype(dtype), jnp.cos(pt).astype(dtype))

        def _apply_rope(x, sin, cos):
            h = x.shape[-1]
            rot = jnp.concatenate([-x[..., h // 2:], x[..., :h // 2]], axis=-1)
            return x * cos + rot * sin
        key = jax.random.key(seed)
        ks = jax.random.split(key, 5)
        B, T, C = (2, 256, 512)
        s = 1.0 / math.sqrt(C)
        return {'x': jax.random.normal(ks[0], (B, T, C), dtype=jnp.float32), 'wq': jax.random.normal(ks[1], (C, C), dtype=jnp.float32) * s, 'wk': jax.random.normal(ks[2], (C, C), dtype=jnp.float32) * s, 'wv': jax.random.normal(ks[3], (C, C), dtype=jnp.float32) * s, 'wo': jax.random.normal(ks[4], (C, C), dtype=jnp.float32) * s}
    _L0_attn_in = _L0_attn_setup()

    def _L0_ffn_setup():
        import jax, jax.numpy as jnp
        import numpy as np
        HID = 512
        INTER = 1376
        BITS = 4
        PACK = 8
        MAXQ = 15
        GROUP = 128

        def _dequant(qweight, scales, qzeros, g_idx):
            shifts = jnp.arange(PACK, dtype=jnp.uint32) * BITS
            qw = qweight.astype(jnp.uint32)
            w = (qw[:, None, :] >> shifts[None, :, None] & MAXQ).reshape(-1, qweight.shape[1])
            qz = qzeros.astype(jnp.uint32)
            z = ((qz[:, :, None] >> shifts[None, None, :] & MAXQ) + 1).reshape(qzeros.shape[0], -1)
            s = scales[g_idx]
            return (w.astype(scales.dtype) - z[g_idx].astype(scales.dtype)) * s
        key = jax.random.key(seed)
        ks = jax.random.split(key, 16)

        def qw(k, K, N):
            return jax.random.randint(k, (K // PACK, N), 0, 2147483647, dtype=jnp.int32)

        def qz(k, G, N):
            return jax.random.randint(k, (G, N // PACK), 0, 2147483647, dtype=jnp.int32)

        def sc(k, G, N):
            return jax.random.uniform(k, (G, N), jnp.float32, 0.001, 0.01)
        Gk = HID // GROUP
        Gd = INTER // GROUP
        return {'x': jax.random.normal(ks[0], (4, 256, HID), jnp.float32), 'gate_qweight': qw(ks[1], HID, INTER), 'gate_scales': sc(ks[2], Gk, INTER), 'gate_qzeros': qz(ks[3], Gk, INTER), 'gate_g_idx': (jnp.arange(HID) // GROUP).astype(jnp.int32), 'up_qweight': qw(ks[4], HID, INTER), 'up_scales': sc(ks[5], Gk, INTER), 'up_qzeros': qz(ks[6], Gk, INTER), 'up_g_idx': (jnp.arange(HID) // GROUP).astype(jnp.int32), 'down_qweight': qw(ks[7], INTER, HID), 'down_scales': sc(ks[8], Gd, HID), 'down_qzeros': qz(ks[9], Gd, HID), 'down_g_idx': (jnp.arange(INTER) // GROUP).astype(jnp.int32)}
    _L0_ffn_in = _L0_ffn_setup()

    def _L1_attn_setup():
        import jax, jax.numpy as jnp
        import numpy as np
        import math
        D_MODEL = 512
        NUM_HEADS = 32
        NUM_KV_HEADS = 8
        HEAD_DIM = D_MODEL // NUM_HEADS
        GROUP = NUM_HEADS // NUM_KV_HEADS
        SEQ_LEN = 256
        BATCH = 2
        ROPE_THETA = 10000.0

        def apply_rope(x, start_pos=0):
            b, h, s, hd = x.shape
            inv_freq = 1.0 / ROPE_THETA ** (jnp.arange(0, hd, 2, dtype=jnp.float32) / hd)
            pos = jnp.arange(start_pos, start_pos + s, dtype=jnp.float32)
            ang = pos[:, None] * inv_freq[None, :]
            cos = jnp.cos(ang).astype(x.dtype)
            sin = jnp.sin(ang).astype(x.dtype)
            xr = x[..., 0::2]
            xi = x[..., 1::2]
            out_r = xr * cos - xi * sin
            out_i = xr * sin + xi * cos
            return jnp.stack([out_r, out_i], axis=-1).reshape(b, h, s, hd)
        key = jax.random.key(seed)
        ks = jax.random.split(key, 5)
        qkv_dim = HEAD_DIM * (NUM_HEADS + 2 * NUM_KV_HEADS)
        scale = 1.0 / math.sqrt(D_MODEL)
        return {'x': jax.random.normal(ks[0], (BATCH, SEQ_LEN, D_MODEL), jnp.float32), 'w_qkv': jax.random.normal(ks[1], (qkv_dim, D_MODEL), jnp.float32) * scale, 'b_qkv': jax.random.normal(ks[2], (qkv_dim,), jnp.float32) * 0.01, 'w_o': jax.random.normal(ks[3], (D_MODEL, D_MODEL), jnp.float32) * scale, 'b_o': jax.random.normal(ks[4], (D_MODEL,), jnp.float32) * 0.01}
    _L1_attn_in = _L1_attn_setup()

    def _L1_ffn_setup():
        import jax, jax.numpy as jnp
        import numpy as np
        D_MODEL = 512
        D_FF = 1376
        key = jax.random.key(seed)
        k1, k2, k3, k4 = jax.random.split(key, 4)
        x = jax.random.normal(k1, (2, 256, D_MODEL), dtype=jnp.float32)
        W_gate = jax.random.normal(k2, (D_FF, D_MODEL), dtype=jnp.float32) * D_MODEL ** (-0.5)
        W_up = jax.random.normal(k3, (D_FF, D_MODEL), dtype=jnp.float32) * D_MODEL ** (-0.5)
        W_down = jax.random.normal(k4, (D_MODEL, D_FF), dtype=jnp.float32) * D_FF ** (-0.5)
        return {'x': x, 'W_gate': W_gate, 'W_up': W_up, 'W_down': W_down}
    _L1_ffn_in = _L1_ffn_setup()

    def _L2_attn_setup():
        import jax, jax.numpy as jnp
        import numpy as np
        Q_DIM = 512
        N_HEADS = 32
        HEAD_DIM = 128
        INNER = N_HEADS * HEAD_DIM
        EPS = 1e-06

        def rms_norm(x, w):
            xf = x.astype(jnp.float32)
            var = jnp.mean(xf * xf, axis=-1, keepdims=True)
            return (w.astype(jnp.float32) * xf * jax.lax.rsqrt(var + EPS)).astype(x.dtype)
        key = jax.random.key(seed)
        ks = jax.random.split(key, 12)
        s = 1.0 / np.sqrt(Q_DIM)
        return {'hidden_states': jax.random.normal(ks[0], (2, 256, Q_DIM), dtype=jnp.float32), 'Wq': jax.random.normal(ks[1], (Q_DIM, INNER), dtype=jnp.float32) * s, 'bq': jnp.zeros((INNER,), dtype=jnp.float32), 'Wk': jax.random.normal(ks[2], (Q_DIM, INNER), dtype=jnp.float32) * s, 'bk': jnp.zeros((INNER,), dtype=jnp.float32), 'Wv': jax.random.normal(ks[3], (Q_DIM, INNER), dtype=jnp.float32) * s, 'bv': jnp.zeros((INNER,), dtype=jnp.float32), 'Wo': jax.random.normal(ks[4], (INNER, Q_DIM), dtype=jnp.float32) * s, 'bo': jnp.zeros((Q_DIM,), dtype=jnp.float32), 'gq': jnp.ones((INNER,), dtype=jnp.float32), 'gk': jnp.ones((INNER,), dtype=jnp.float32)}
    _L2_attn_in = _L2_attn_setup()

    def _L2_ffn_setup():
        import jax, jax.numpy as jnp
        import numpy as np
        DIM = 512
        HID = 1376
        R = 16
        SCALING = 32.0 / 16.0

        def _lora_linear(x, w, a, b):
            base = jnp.einsum('bsd,od->bso', x, w)
            low = jnp.einsum('bsr,or->bso', jnp.einsum('bsd,rd->bsr', x, a), b)
            return base + low * SCALING
        key = jax.random.key(seed)
        ks = jax.random.split(key, 10)
        s_in = 1.0 / np.sqrt(DIM)
        s_hid = 1.0 / np.sqrt(HID)
        return {'x': jax.random.normal(ks[0], (4, 256, DIM), jnp.float32), 'w1': jax.random.normal(ks[1], (HID, DIM), jnp.float32) * s_in, 'w3': jax.random.normal(ks[2], (HID, DIM), jnp.float32) * s_in, 'w2': jax.random.normal(ks[3], (DIM, HID), jnp.float32) * s_hid, 'lora_A1': jax.random.normal(ks[4], (R, DIM), jnp.float32) * s_in, 'lora_B1': jax.random.normal(ks[5], (HID, R), jnp.float32) * 0.02, 'lora_A3': jax.random.normal(ks[6], (R, DIM), jnp.float32) * s_in, 'lora_B3': jax.random.normal(ks[7], (HID, R), jnp.float32) * 0.02, 'lora_A2': jax.random.normal(ks[8], (R, HID), jnp.float32) * s_hid, 'lora_B2': jax.random.normal(ks[9], (DIM, R), jnp.float32) * 0.02}
    _L2_ffn_in = _L2_ffn_setup()

    def _L3_attn_setup():
        import jax, jax.numpy as jnp
        import numpy as np
        B, T, D = (2, 256, 512)
        H = 32
        HKV = 1
        HD = D // H
        key = jax.random.key(seed)
        ks = jax.random.split(key, 9)
        s = lambda fan_in: 1.0 / np.sqrt(fan_in)
        return {'x': jax.random.normal(ks[0], (B, T, D), dtype=jnp.float32), 'wq_w': jax.random.normal(ks[1], (H * HD, D), dtype=jnp.float32) * s(D), 'wq_b': jax.random.normal(ks[2], (H * HD,), dtype=jnp.float32) * 0.02, 'wk_w': jax.random.normal(ks[3], (HKV * HD, D), dtype=jnp.float32) * s(D), 'wk_b': jax.random.normal(ks[4], (HKV * HD,), dtype=jnp.float32) * 0.02, 'wv_w': jax.random.normal(ks[5], (HKV * HD, D), dtype=jnp.float32) * s(D), 'wv_b': jax.random.normal(ks[6], (HKV * HD,), dtype=jnp.float32) * 0.02, 'wo_w': jax.random.normal(ks[7], (D, H * HD), dtype=jnp.float32) * s(H * HD), 'wo_b': jax.random.normal(ks[8], (D,), dtype=jnp.float32) * 0.02}
    _L3_attn_in = _L3_attn_setup()

    def _L3_ffn_setup():
        import jax, jax.numpy as jnp
        import numpy as np
        BS = 128
        FP8_MAX = 448.0

        def act_quant(x):
            T, K = x.shape
            xb = x.reshape(T, K // BS, BS)
            amax = jnp.max(jnp.abs(xb), axis=-1)
            scale = amax / FP8_MAX + 1e-12
            xq = (xb / scale[:, :, None]).reshape(T, K)
            return (xq, scale)

        def linear_dsv3(x, wq, w_scale):
            T, K = x.shape
            N = wq.shape[0]
            xq, xs = act_quant(x)
            xdq = (xq.reshape(T, K // BS, BS) * xs[:, :, None]).reshape(T, K)
            wdq = (wq.reshape(N // BS, BS, K // BS, BS) * w_scale[:, None, :, None]).reshape(N, K)
            return xdq @ wdq.T
        key = jax.random.key(seed)
        ks = jax.random.split(key, 4)
        DIM, INTER = (512, 1792)

        def make_qweight(k, n, m):
            w = jax.random.normal(k, (n, m), dtype=jnp.float32) * 0.02
            wb = w.reshape(n // BS, BS, m // BS, BS)
            amax = jnp.max(jnp.abs(wb), axis=(1, 3))
            scale = amax / FP8_MAX + 1e-12
            wq = (wb / scale[:, None, :, None]).reshape(n, m)
            return (wq, scale)
        x = jax.random.normal(ks[0], (2, 128, DIM), dtype=jnp.float32)
        w1, w1_scale = make_qweight(ks[1], INTER, DIM)
        w3, w3_scale = make_qweight(ks[2], INTER, DIM)
        w2, w2_scale = make_qweight(ks[3], DIM, INTER)
        return {'x': x, 'w1': w1, 'w1_scale': w1_scale, 'w3': w3, 'w3_scale': w3_scale, 'w2': w2, 'w2_scale': w2_scale}
    _L3_ffn_in = _L3_ffn_setup()
    _d = {'L0_attn_x': _L0_attn_in['x'], 'L0_attn_wq': _L0_attn_in['wq'], 'L0_attn_wk': _L0_attn_in['wk'], 'L0_attn_wv': _L0_attn_in['wv'], 'L0_attn_wo': _L0_attn_in['wo'], 'L0_ffn_gate_qweight': _L0_ffn_in['gate_qweight'], 'L0_ffn_gate_scales': _L0_ffn_in['gate_scales'], 'L0_ffn_gate_qzeros': _L0_ffn_in['gate_qzeros'], 'L0_ffn_gate_g_idx': _L0_ffn_in['gate_g_idx'], 'L0_ffn_up_qweight': _L0_ffn_in['up_qweight'], 'L0_ffn_up_scales': _L0_ffn_in['up_scales'], 'L0_ffn_up_qzeros': _L0_ffn_in['up_qzeros'], 'L0_ffn_up_g_idx': _L0_ffn_in['up_g_idx'], 'L0_ffn_down_qweight': _L0_ffn_in['down_qweight'], 'L0_ffn_down_scales': _L0_ffn_in['down_scales'], 'L0_ffn_down_qzeros': _L0_ffn_in['down_qzeros'], 'L0_ffn_down_g_idx': _L0_ffn_in['down_g_idx'], 'L1_attn_w_qkv': _L1_attn_in['w_qkv'], 'L1_attn_b_qkv': _L1_attn_in['b_qkv'], 'L1_attn_w_o': _L1_attn_in['w_o'], 'L1_attn_b_o': _L1_attn_in['b_o'], 'L1_ffn_W_gate': _L1_ffn_in['W_gate'], 'L1_ffn_W_up': _L1_ffn_in['W_up'], 'L1_ffn_W_down': _L1_ffn_in['W_down'], 'L2_attn_Wq': _L2_attn_in['Wq'], 'L2_attn_bq': _L2_attn_in['bq'], 'L2_attn_Wk': _L2_attn_in['Wk'], 'L2_attn_bk': _L2_attn_in['bk'], 'L2_attn_Wv': _L2_attn_in['Wv'], 'L2_attn_bv': _L2_attn_in['bv'], 'L2_attn_Wo': _L2_attn_in['Wo'], 'L2_attn_bo': _L2_attn_in['bo'], 'L2_attn_gq': _L2_attn_in['gq'], 'L2_attn_gk': _L2_attn_in['gk'], 'L2_ffn_w1': _L2_ffn_in['w1'], 'L2_ffn_w3': _L2_ffn_in['w3'], 'L2_ffn_w2': _L2_ffn_in['w2'], 'L2_ffn_lora_A1': _L2_ffn_in['lora_A1'], 'L2_ffn_lora_B1': _L2_ffn_in['lora_B1'], 'L2_ffn_lora_A3': _L2_ffn_in['lora_A3'], 'L2_ffn_lora_B3': _L2_ffn_in['lora_B3'], 'L2_ffn_lora_A2': _L2_ffn_in['lora_A2'], 'L2_ffn_lora_B2': _L2_ffn_in['lora_B2'], 'L3_attn_wq_w': _L3_attn_in['wq_w'], 'L3_attn_wq_b': _L3_attn_in['wq_b'], 'L3_attn_wk_w': _L3_attn_in['wk_w'], 'L3_attn_wk_b': _L3_attn_in['wk_b'], 'L3_attn_wv_w': _L3_attn_in['wv_w'], 'L3_attn_wv_b': _L3_attn_in['wv_b'], 'L3_attn_wo_w': _L3_attn_in['wo_w'], 'L3_attn_wo_b': _L3_attn_in['wo_b'], 'L3_ffn_w1': _L3_ffn_in['w1'], 'L3_ffn_w1_scale': _L3_ffn_in['w1_scale'], 'L3_ffn_w3': _L3_ffn_in['w3'], 'L3_ffn_w3_scale': _L3_ffn_in['w3_scale'], 'L3_ffn_w2': _L3_ffn_in['w2'], 'L3_ffn_w2_scale': _L3_ffn_in['w2_scale']}
    _x0 = _d['L0_attn_x']
    _d['L0_attn_x'] = jax.random.normal(jax.random.fold_in(jax.random.key(seed), 1), (4, 256, 512), dtype=_x0.dtype)
    del _x0
    return _d

def reference(L0_attn_x, L0_attn_wq, L0_attn_wk, L0_attn_wv, L0_attn_wo, L0_ffn_gate_qweight, L0_ffn_gate_scales, L0_ffn_gate_qzeros, L0_ffn_gate_g_idx, L0_ffn_up_qweight, L0_ffn_up_scales, L0_ffn_up_qzeros, L0_ffn_up_g_idx, L0_ffn_down_qweight, L0_ffn_down_scales, L0_ffn_down_qzeros, L0_ffn_down_g_idx, L1_attn_w_qkv, L1_attn_b_qkv, L1_attn_w_o, L1_attn_b_o, L1_ffn_W_gate, L1_ffn_W_up, L1_ffn_W_down, L2_attn_Wq, L2_attn_bq, L2_attn_Wk, L2_attn_bk, L2_attn_Wv, L2_attn_bv, L2_attn_Wo, L2_attn_bo, L2_attn_gq, L2_attn_gk, L2_ffn_w1, L2_ffn_w3, L2_ffn_w2, L2_ffn_lora_A1, L2_ffn_lora_B1, L2_ffn_lora_A3, L2_ffn_lora_B3, L2_ffn_lora_A2, L2_ffn_lora_B2, L3_attn_wq_w, L3_attn_wq_b, L3_attn_wk_w, L3_attn_wk_b, L3_attn_wv_w, L3_attn_wv_b, L3_attn_wo_w, L3_attn_wo_b, L3_ffn_w1, L3_ffn_w1_scale, L3_ffn_w3, L3_ffn_w3_scale, L3_ffn_w2, L3_ffn_w2_scale):

    def _L0_attn_ref(x, wq, wk, wv, wo):
        import math
        import jax, jax.numpy as jnp
        import numpy as np

        def _rope_tables(T, h, dtype):
            pos = jnp.arange(T, dtype=jnp.float32)
            thetas = 1.0 / 10000.0 ** (jnp.arange(0, h, 2, dtype=jnp.float32) / h)
            pt = jnp.outer(pos, thetas)
            pt = jnp.concatenate([pt, pt], axis=-1)
            return (jnp.sin(pt).astype(dtype), jnp.cos(pt).astype(dtype))

        def _apply_rope(x, sin, cos):
            h = x.shape[-1]
            rot = jnp.concatenate([-x[..., h // 2:], x[..., :h // 2]], axis=-1)
            return x * cos + rot * sin
        B, T, C = x.shape
        n_head = 32
        h = C // n_head

        def proj(w):
            y = jnp.einsum('btc,dc->btd', x, w)
            return y.reshape(B, T, n_head, h).transpose(0, 2, 1, 3)
        q, k, v = (proj(wq), proj(wk), proj(wv))
        sin, cos = _rope_tables(T, h, x.dtype)
        q = _apply_rope(q, sin, cos)
        k = _apply_rope(k, sin, cos)
        scores = jnp.einsum('bnth,bnsh->bnts', q, k) * (1.0 / math.sqrt(h))
        causal = jnp.tril(jnp.ones((T, T), dtype=bool))
        scores = jnp.where(causal, scores, -jnp.inf)
        attn = jax.nn.softmax(scores, axis=-1)
        out = jnp.einsum('bnts,bnsh->bnth', attn, v)
        out = out.transpose(0, 2, 1, 3).reshape(B, T, C)
        return jnp.einsum('btc,dc->btd', out, wo)

    def _L0_ffn_ref(x, gate_qweight, gate_scales, gate_qzeros, gate_g_idx, up_qweight, up_scales, up_qzeros, up_g_idx, down_qweight, down_scales, down_qzeros, down_g_idx):
        import jax, jax.numpy as jnp
        import numpy as np
        HID = 512
        INTER = 1376
        BITS = 4
        PACK = 8
        MAXQ = 15
        GROUP = 128

        def _dequant(qweight, scales, qzeros, g_idx):
            shifts = jnp.arange(PACK, dtype=jnp.uint32) * BITS
            qw = qweight.astype(jnp.uint32)
            w = (qw[:, None, :] >> shifts[None, :, None] & MAXQ).reshape(-1, qweight.shape[1])
            qz = qzeros.astype(jnp.uint32)
            z = ((qz[:, :, None] >> shifts[None, None, :] & MAXQ) + 1).reshape(qzeros.shape[0], -1)
            s = scales[g_idx]
            return (w.astype(scales.dtype) - z[g_idx].astype(scales.dtype)) * s
        Wg = _dequant(gate_qweight, gate_scales, gate_qzeros, gate_g_idx)
        Wu = _dequant(up_qweight, up_scales, up_qzeros, up_g_idx)
        Wd = _dequant(down_qweight, down_scales, down_qzeros, down_g_idx)
        xf = x.reshape(-1, x.shape[-1])
        h = jax.nn.silu(xf @ Wg) * (xf @ Wu)
        out = h @ Wd
        return out.reshape(x.shape[:-1] + (Wd.shape[1],))

    def _L1_attn_ref(x, w_qkv, b_qkv, w_o, b_o):
        import jax, jax.numpy as jnp
        import numpy as np
        import math
        D_MODEL = 512
        NUM_HEADS = 32
        NUM_KV_HEADS = 8
        HEAD_DIM = D_MODEL // NUM_HEADS
        GROUP = NUM_HEADS // NUM_KV_HEADS
        SEQ_LEN = 256
        BATCH = 2
        ROPE_THETA = 10000.0

        def apply_rope(x, start_pos=0):
            b, h, s, hd = x.shape
            inv_freq = 1.0 / ROPE_THETA ** (jnp.arange(0, hd, 2, dtype=jnp.float32) / hd)
            pos = jnp.arange(start_pos, start_pos + s, dtype=jnp.float32)
            ang = pos[:, None] * inv_freq[None, :]
            cos = jnp.cos(ang).astype(x.dtype)
            sin = jnp.sin(ang).astype(x.dtype)
            xr = x[..., 0::2]
            xi = x[..., 1::2]
            out_r = xr * cos - xi * sin
            out_i = xr * sin + xi * cos
            return jnp.stack([out_r, out_i], axis=-1).reshape(b, h, s, hd)
        bs, seq_len, d_model = x.shape
        qkv = x @ w_qkv.T + b_qkv
        q_dim = NUM_HEADS * HEAD_DIM
        kv_dim = NUM_KV_HEADS * HEAD_DIM
        q, k, v = jnp.split(qkv, [q_dim, q_dim + kv_dim], axis=-1)
        q = q.reshape(bs, seq_len, NUM_HEADS, HEAD_DIM).transpose(0, 2, 1, 3)
        k = k.reshape(bs, seq_len, NUM_KV_HEADS, HEAD_DIM).transpose(0, 2, 1, 3)
        v = v.reshape(bs, seq_len, NUM_KV_HEADS, HEAD_DIM).transpose(0, 2, 1, 3)
        q = apply_rope(q, 0)
        k = apply_rope(k, 0)
        k = jnp.repeat(k, GROUP, axis=1)
        v = jnp.repeat(v, GROUP, axis=1)
        scores = jnp.einsum('bhqd,bhkd->bhqk', q, k) / math.sqrt(HEAD_DIM)
        causal = jnp.tril(jnp.ones((seq_len, seq_len), dtype=bool))
        scores = jnp.where(causal[None, None, :, :], scores, jnp.float32(-1e+20))
        attn = jax.nn.softmax(scores, axis=-1)
        out = jnp.einsum('bhqk,bhkd->bhqd', attn, v)
        out = out.transpose(0, 2, 1, 3).reshape(bs, seq_len, d_model)
        return out @ w_o.T + b_o

    def _L1_ffn_ref(x, W_gate, W_up, W_down):
        import jax, jax.numpy as jnp
        import numpy as np
        D_MODEL = 512
        D_FF = 1376
        out_shape = x.shape[:-1] + (W_down.shape[0],)
        xf = x.reshape(-1, x.shape[-1])
        up = jnp.einsum('td,fd->tf', xf, W_up)
        gate = jax.nn.silu(jnp.einsum('td,fd->tf', xf, W_gate))
        h = gate * up
        y = jnp.einsum('tf,df->td', h, W_down)
        return y.reshape(out_shape)

    def _L2_attn_ref(hidden_states, Wq, bq, Wk, bk, Wv, bv, Wo, bo, gq, gk):
        import jax, jax.numpy as jnp
        import numpy as np
        Q_DIM = 512
        N_HEADS = 32
        HEAD_DIM = 128
        INNER = N_HEADS * HEAD_DIM
        EPS = 1e-06

        def rms_norm(x, w):
            xf = x.astype(jnp.float32)
            var = jnp.mean(xf * xf, axis=-1, keepdims=True)
            return (w.astype(jnp.float32) * xf * jax.lax.rsqrt(var + EPS)).astype(x.dtype)
        B, S, _ = hidden_states.shape
        q = hidden_states @ Wq + bq
        k = hidden_states @ Wk + bk
        v = hidden_states @ Wv + bv
        q = rms_norm(q, gq)
        k = rms_norm(k, gk)
        q = q.reshape(B, S, N_HEADS, HEAD_DIM).transpose(0, 2, 1, 3)
        k = k.reshape(B, S, N_HEADS, HEAD_DIM).transpose(0, 2, 1, 3)
        v = v.reshape(B, S, N_HEADS, HEAD_DIM).transpose(0, 2, 1, 3)
        scale = 1.0 / np.sqrt(HEAD_DIM)
        attn = jnp.einsum('bhqd,bhkd->bhqk', q.astype(jnp.float32), k.astype(jnp.float32)) * scale
        attn = jax.nn.softmax(attn, axis=-1)
        out = jnp.einsum('bhqk,bhkd->bhqd', attn, v.astype(jnp.float32))
        out = out.transpose(0, 2, 1, 3).reshape(B, S, INNER).astype(hidden_states.dtype)
        return out @ Wo + bo

    def _L2_ffn_ref(x, w1, w3, w2, lora_A1, lora_B1, lora_A3, lora_B3, lora_A2, lora_B2):
        import jax, jax.numpy as jnp
        import numpy as np
        DIM = 512
        HID = 1376
        R = 16
        SCALING = 32.0 / 16.0

        def _lora_linear(x, w, a, b):
            base = jnp.einsum('bsd,od->bso', x, w)
            low = jnp.einsum('bsr,or->bso', jnp.einsum('bsd,rd->bsr', x, a), b)
            return base + low * SCALING
        h1 = _lora_linear(x, w1, lora_A1, lora_B1)
        h3 = _lora_linear(x, w3, lora_A3, lora_B3)
        g = jax.nn.silu(h1) * h3
        return _lora_linear(g, w2, lora_A2, lora_B2)

    def _L3_attn_ref(x, wq_w, wq_b, wk_w, wk_b, wv_w, wv_b, wo_w, wo_b):
        import jax, jax.numpy as jnp
        import numpy as np
        B, T, D = (2, 256, 512)
        H = 32
        HKV = 1
        HD = D // H
        b, t, d = x.shape
        q = (x @ wq_w.T + wq_b).reshape(b, t, H, HD)
        k = (x @ wk_w.T + wk_b).reshape(b, t, HKV, HD)
        v = (x @ wv_w.T + wv_b).reshape(b, t, HKV, HD)
        k1 = k[:, :, 0, :]
        v1 = v[:, :, 0, :]
        scores = jnp.einsum('bqhd,bkd->bhqk', q, k1) / jnp.sqrt(jnp.float32(HD))
        causal = jnp.tril(jnp.ones((t, t), dtype=bool))
        scores = jnp.where(causal, scores, -jnp.inf)
        weights = jax.nn.softmax(scores, axis=-1)
        attn = jnp.einsum('bhqk,bkd->bqhd', weights, v1)
        attn = attn.reshape(b, t, H * HD)
        return attn @ wo_w.T + wo_b

    def _L3_ffn_ref(x, w1, w1_scale, w3, w3_scale, w2, w2_scale):
        import jax, jax.numpy as jnp
        import numpy as np
        BS = 128
        FP8_MAX = 448.0

        def act_quant(x):
            T, K = x.shape
            xb = x.reshape(T, K // BS, BS)
            amax = jnp.max(jnp.abs(xb), axis=-1)
            scale = amax / FP8_MAX + 1e-12
            xq = (xb / scale[:, :, None]).reshape(T, K)
            return (xq, scale)

        def linear_dsv3(x, wq, w_scale):
            T, K = x.shape
            N = wq.shape[0]
            xq, xs = act_quant(x)
            xdq = (xq.reshape(T, K // BS, BS) * xs[:, :, None]).reshape(T, K)
            wdq = (wq.reshape(N // BS, BS, K // BS, BS) * w_scale[:, None, :, None]).reshape(N, K)
            return xdq @ wdq.T
        B, S, D = x.shape
        xf = x.reshape(-1, D)
        g = linear_dsv3(xf, w1, w1_scale)
        u = linear_dsv3(xf, w3, w3_scale)
        h = jax.nn.silu(g) * u
        y = linear_dsv3(h, w2, w2_scale)
        return y.reshape(B, S, D)
    x = L0_attn_x
    xn = _layernorm(x, axis=-1)
    x = x + _L0_attn_ref(xn, L0_attn_wq, L0_attn_wk, L0_attn_wv, L0_attn_wo) + _L0_ffn_ref(xn, L0_ffn_gate_qweight, L0_ffn_gate_scales, L0_ffn_gate_qzeros, L0_ffn_gate_g_idx, L0_ffn_up_qweight, L0_ffn_up_scales, L0_ffn_up_qzeros, L0_ffn_up_g_idx, L0_ffn_down_qweight, L0_ffn_down_scales, L0_ffn_down_qzeros, L0_ffn_down_g_idx)
    xn = _layernorm(x, axis=-1)
    x = x + _L1_attn_ref(xn, L1_attn_w_qkv, L1_attn_b_qkv, L1_attn_w_o, L1_attn_b_o) + _L1_ffn_ref(xn, L1_ffn_W_gate, L1_ffn_W_up, L1_ffn_W_down)
    xn = _layernorm(x, axis=-1)
    x = x + _L2_attn_ref(xn, L2_attn_Wq, L2_attn_bq, L2_attn_Wk, L2_attn_bk, L2_attn_Wv, L2_attn_bv, L2_attn_Wo, L2_attn_bo, L2_attn_gq, L2_attn_gk) + _L2_ffn_ref(xn, L2_ffn_w1, L2_ffn_w3, L2_ffn_w2, L2_ffn_lora_A1, L2_ffn_lora_B1, L2_ffn_lora_A3, L2_ffn_lora_B3, L2_ffn_lora_A2, L2_ffn_lora_B2)
    xn = _layernorm(x, axis=-1)
    x = x + _L3_attn_ref(xn, L3_attn_wq_w, L3_attn_wq_b, L3_attn_wk_w, L3_attn_wk_b, L3_attn_wv_w, L3_attn_wv_b, L3_attn_wo_w, L3_attn_wo_b) + _L3_ffn_ref(xn, L3_ffn_w1, L3_ffn_w1_scale, L3_ffn_w3, L3_ffn_w3_scale, L3_ffn_w2, L3_ffn_w2_scale)
    return x

_drawn_inputs = setup_inputs


def setup_inputs(seed=0):
    import zlib

    import numpy as np

    out = dict(_drawn_inputs(seed))
    spreads = {'L2_attn_bq': (0.0, 0.424),
     'L2_attn_bk': (0.0, 0.8),
     'L2_attn_bv': (0.0, 0.1),
     'L2_attn_bo': (0.0, 0.1),
     'L2_attn_gq': (1.0, 0.2),
     'L2_attn_gk': (1.0, 0.2)}
    factors = {'L1_attn_b_qkv': 4.784,
     'L1_attn_b_o': 4.665,
     'L3_attn_wq_b': 64.0,
     'L3_attn_wk_b': 200.0,
     'L3_attn_wv_b': 51.464,
     'L3_attn_wo_b': 200.0,
     'L3_ffn_w1_scale': 8.0,
     'L3_ffn_w3_scale': 8.0,
     'L3_ffn_w2_scale': 8.0,
     'L3_attn_wq_w': 8.0,
     'L3_attn_wk_w': 8.0,
     'L3_attn_wv_w': 7.074,
     'L3_attn_wo_w': 6.659}
    for name, (base, spread) in spreads.items():
        noise = np.random.default_rng([zlib.crc32(name.encode()), seed]).standard_normal(out[name].shape)
        drawn = base * np.exp(spread * noise) if base else spread * noise
        out[name] = jnp.asarray(drawn.astype(out[name].dtype))
    for name, factor in factors.items():
        out[name] = (out[name] * factor).astype(out[name].dtype)
    return out
```

```python
from contextlib import ExitStack

import numpy as np

import concourse.bass as bass
from concourse import mybir

P = 128
BATCH, SEQ, D = 4, 256, 512
TOK = BATCH * SEQ
HALF = 512
NH = TOK // HALF
KT = D // P
SLOTS = 4

HEADS, HD = 32, 16
HPC = P // HD
QC = HEADS // HPC
VW = HD + 1
KV1 = 8
PACK = 8
F0 = 1376
F3 = 1792
GROUPS_UP, GROUPS_DOWN = 4, 10
H2, HD2 = 32, 128
INNER2 = H2 * HD2
GRP2 = 4
LORA = 2.0
RANK = 16
LN_EPS, RMS_EPS = 1e-5, 1e-6
MASKED = -1e30

F32 = mybir.dt.float32
F32R = mybir.dt.float32r
BF16 = mybir.dt.bfloat16
I32 = mybir.dt.int32
ALU = mybir.AluOpType
ACT = mybir.ActivationFunctionType
AX = mybir.AxisListType

C_ID, C_MEAN, C_MEAN2, C_ROT0, C_ROT1 = 0, 128, 256, 384, 512
C_MASK, C_HEAD = 640, 768
C_COS0, C_SIN0, C_COS1, C_SIN1 = 776, 1032, 1288, 1544
C_IDX = 1800
C_WIDTH = 1802


def constants():
    c = np.zeros((P, C_WIDTH), np.float32)
    c[:, C_ID:C_ID + P] = np.eye(P)
    c[:, C_MEAN:C_MEAN + P] = 1.0 / D
    c[:, C_MEAN2:C_MEAN2 + P] = 1.0 / INNER2
    for p in range(P):
        h, d = p - p % HD, p % HD
        if d < HD // 2:
            c[h + d + HD // 2, C_ROT0 + p] = -1.0
        else:
            c[h + d - HD // 2, C_ROT0 + p] = 1.0
        if d % 2 == 0:
            c[p + 1, C_ROT1 + p] = -1.0
        else:
            c[p - 1, C_ROT1 + p] = 1.0
    c[:, C_MASK:C_MASK + P] = np.where(np.arange(P)[:, None] >= np.arange(P)[None], 0.0, MASKED)
    c[np.arange(P), C_HEAD + np.arange(P) // HD] = 1.0 / np.sqrt(np.float32(HD))
    freq = (1.0 / 10000.0 ** (np.arange(0, HD, 2, dtype=np.float32) / HD)).astype(np.float32)
    ang = np.outer(np.arange(SEQ, dtype=np.float32), freq).astype(np.float32)
    half = ang[:, np.arange(P) % (HD // 2)].T
    pair = ang[:, (np.arange(P) % HD) // 2].T
    c[:, C_COS0:C_COS0 + SEQ], c[:, C_SIN0:C_SIN0 + SEQ] = np.cos(half), np.sin(half)
    c[:, C_COS1:C_COS1 + SEQ], c[:, C_SIN1:C_SIN1 + SEQ] = np.cos(pair), np.sin(pair)
    c[:, C_IDX] = np.arange(P)
    shift = np.zeros((P, 1), np.int32)
    shift[:, 0] = (np.arange(P) % PACK) * (32 // PACK)
    return c, shift


class Signal:

    def __init__(self, sem):
        self.sem = sem
        self.count = 0

    def reserve(self, n):
        base = self.count
        self.count += n
        return base




class Stage:
    pass


def build(nc, t, out):
    ctx = ExitStack()
    with ctx:
        def sb(name, shape, dt=F32):
            return ctx.enter_context(nc.sbuf_tensor(name, shape, dt))

        def sig(name):
            return Signal(ctx.enter_context(nc.semaphore(name)))

        cst = sb("cst", [P, C_WIDTH])
        shift = sb("shift", [P, 1], I32)
        ident = cst[:, C_ID:C_ID + P]
        ident16 = sb("ident16", [P, P], BF16)
        mask16 = sb("mask16", [P, P], BF16)
        eps = sb("eps", [P, 2])
        bias1 = sb("bias1", [P, QC + 2 + KT])
        bias3 = sb("bias3", [P, QC + 2 + KT])
        cols2 = sb("cols2", [P, 5, H2])
        bo2 = sb("bo2", [P, KT])
        wscale = sb("wscale", [P, 2, F3 // P, KT])
        wscale2 = sb("wscale2", [P, KT, F3 // P])
        xT = sb("xT", [P, KT, TOK])
        xn_hi = sb("xn_hi", [P, KT, TOK], F32R)
        xn_lo = sb("xn_lo", [P, KT, TOK], F32R)
        nat = sb("nat", [P, SLOTS, D])
        w_hi = sb("w_hi", [P, SLOTS, D], F32R)
        w_lo = sb("w_lo", [P, SLOTS, D], F32R)
        arena_at = nc.sbuf_base

        def arena(*tensors):
            with ExitStack() as own:
                made = [own.enter_context(nc.sbuf_tensor(n, s, *(dt or [F32]))) for n, s, *dt in tensors]
            assert nc.sbuf_base == arena_at
            return made

        F11, F14 = -(-F0 // P), F3 // P
        x_nat, = arena(("x_nat", [P, TOK // P, D]))
        cen, sq, inv = arena(("cen", [P, KT, TOK]), ("sq", [P, KT, TOK]), ("inv", [P, TOK]))
        h0_hi, h0_lo, sgf0, hot, packed, zero, scale, deq = arena(
            ("h0_hi", [P, F11, TOK], F32R), ("h0_lo", [P, F11, TOK], F32R), ("sgf0", [P, 2, NH, HALF]),
            ("hot", [P, F0]), ("packed", [48, F0 // PACK], I32),
            ("zero", [P, F0]), ("scale", [P, F0]), ("deq", [P, 2, D]))
        h1_hi, h1_lo, sgf1 = arena(
            ("h1_hi", [P, F11, TOK], F32R), ("h1_lo", [P, F11, TOK], F32R), ("sgf1", [P, 2, NH, HALF]))
        h2_hi, h2_lo, sgf2, b13, b13s, low, b2 = arena(
            ("h2_hi", [P, F11, TOK], F32R), ("h2_lo", [P, F11, TOK], F32R), ("sgf2", [P, 2, NH, HALF]),
            ("b13", [48, F11 * P]), ("b13s", [48, SLOTS, P]), ("low", [48, TOK]), ("b2", [RANK, D]))
        h3_hi, h3_lo, sgf3 = arena(
            ("h3_hi", [P, F14, TOK], F32R), ("h3_lo", [P, F14, TOK], F32R), ("sgf3", [P, 2, NH, HALF]))
        at_q, at_k, at_v, at_val, at_km, at_qs, at_p, at_pt, at_on, at_lo, at_small = arena(
            ("at_q", [P, QC, TOK]), ("at_k", [P, QC, TOK]), ("at_v", [P, QC, TOK]),
            ("at_val", [P, TOK // P, QC, HPC, VW]), ("at_km", [P, 2, HPC, SEQ]), ("at_qs", [P, QC, SEQ]),
            ("at_p", [P, 3, 512]), ("at_pt", [P, 2, 512]), ("at_on", [P, 2, 2, P]),
            ("at_lo", [P, QC, TOK], F32R), ("at_small", [P, 64]))
        at_q2, at_k2, at_hi = arena(
            ("at_q2", [P, QC, TOK]), ("at_k2", [P, QC, TOK]), ("at_hi", [P, QC, TOK], F32R))
        rms_q, rms_k, ssq, raw2, sq2, b2s = arena(
            ("rms_q", [P, TOK]), ("rms_k", [P, TOK]), ("ssq", [P, 2, TOK]),
            ("raw2", [P, SLOTS, TOK]), ("sq2", [P, SLOTS, TOK]), ("b2s", [P, SLOTS]))
        (rms_q_, rms_k_, qk_raw, qk_hi, qk_lo, val2, p2, pt2, bv2, o2_hi, o2_lo, small2) = arena(
            ("rms_q_", [P, TOK]), ("rms_k_", [P, TOK]), ("qk_raw", [P, 2, TOK]),
            ("qk_hi", [P, 2, 2, TOK], F32R), ("qk_lo", [P, 2, 2, TOK], F32R),
            ("val2", [P, 2, TOK // P, P]), ("p2", [P, 2, 2, SEQ]), ("pt2", [P, 2, 2, SEQ]),
            ("bv2", [P, GRP2]), ("o2_hi", [P, GRP2, TOK], F32R), ("o2_lo", [P, GRP2, TOK], F32R),
            ("small2", [P, 2, 8]))
        bank = [ctx.enter_context(nc.psum_tensor(f"bank{i}", [P, 512], F32)) for i in range(8)]
        turn_bank = [bank[0], bank[1]]
        acc = [[bank[2], bank[3]], [bank[4], bank[5]]]
        qk_dram = nc.dram_tensor("qk_scratch", (H2, 2, P, TOK), F32).ap()

        phase = sig("phase")
        cst_in = sig("cst_in")
        cst_made = sig("cst_made")
        loaded = [sig(f"loaded{j}") for j in range(SLOTS)]
        scaled = sig("scaled")
        turned = sig("turned")
        unpacked = sig("unpacked")
        centred = sig("centred")
        dequant = sig("dequant")
        hi = sig("hi")
        lo = sig("lo")
        half0 = sig("half0")
        used = sig("used")
        gate_read = sig("gate_read")
        up_read = sig("up_read")
        h_hi_done = sig("h_hi_done")
        h_lo_done = sig("h_lo_done")
        out_read = sig("out_read")
        step_a = sig("step_a")
        step_b = sig("step_b")
        step_c = sig("step_c")
        step_d = sig("step_d")
        step_e = sig("step_e")
        io = sig("io")
        s_ready = sig("s_ready")
        max_done = sig("max_done")
        exp_done = sig("exp_done")
        pt_ready = sig("pt_ready")
        pt_copied = sig("pt_copied")
        pv_done = sig("pv_done")
        o_normed = sig("o_normed")
        ot_ready = sig("ot_ready")
        ot_hi = sig("ot_hi")
        ot_lo = sig("ot_lo")
        km_made = sig("km_made")
        qs_made = sig("qs_made")
        stored = [sig(f"stored{j}") for j in range(SLOTS)]
        norm_done = sig("norm_done")
        v_ready = sig("v_ready")
        v_copied = sig("v_copied")
        small = sig("small")
        sq_done = sig("sq_done")
        raw_done = [sig("raw_q_done"), sig("raw_k_done")]
        ssq_done = sig("ssq_done")
        qk_in = sig("qk_in")
        qk_scaled = sig("qk_scaled")
        qk_hi_done = sig("qk_hi_done")
        qk_lo_done = sig("qk_lo_done")
        bias_in = sig("bias_in")
        o_hi_done = sig("o_hi_done")
        o_lo_done = sig("o_lo_done")

        def loop(eng, n, body):
            if n > 2:
                with eng.Fori(0, n) as it:
                    body(it)
            else:
                for it in range(n):
                    body(it)

        stage_no = {}

        def barrier(eng):
            k = stage_no[id(eng)] = stage_no.get(id(eng), 0) + 1
            eng.drain().then_inc(phase.sem, 1)
            eng.wait_ge(phase.sem, 5 * k)

        def bcast(ap, n):
            return ap.unsqueeze(1).broadcast_to([ap.shape[0], n, ap.shape[1]])

        def tail_bcast(ap, n):
            return ap.unsqueeze(2).broadcast_to([ap.shape[0], ap.shape[1], n])

        def at(half):
            return slice(half * HALF, (half + 1) * HALF)

        def plan_chunks(n, mode, per_slot):
            s = Stage()
            s.n, s.mode = n, mode
            s.lo0, s.hi0, s.used0 = lo.reserve(n), hi.reserve(n), used.reserve(n)
            s.turned0 = turned.reserve(n if mode != "direct" else 0)
            s.scaled0 = scaled.reserve(n if mode == "scaled" else 0)
            m = n if mode == "dequant" else 0
            s.un0, s.cen0, s.deq0 = unpacked.reserve(m), centred.reserve(m), dequant.reserve(m)
            dmas = per_slot if isinstance(per_slot, list) else [per_slot] * n
            s.dmas = dmas
            s.load0 = [loaded[j].reserve(16 * sum(dmas[j::SLOTS])) for j in range(SLOTS)]
            return s

        def loaded_count(s, i, j):
            if isinstance(i, int):
                return s.load0[j] + 16 * sum(s.dmas[j:i + 1:SLOTS])
            return s.load0[j] + 4 * s.dmas[j] * (i - j) + 16 * s.dmas[j]

        def later(i):
            return not isinstance(i, int) or i >= SLOTS

        def sp_slot(sp, s, i):
            if later(i):
                if s.mode == "direct":
                    sp.wait_ge(lo.sem, s.lo0 + i - 3)
                elif s.mode == "dequant":
                    sp.wait_ge(centred.sem, s.cen0 + i - 3)
                else:
                    sp.wait_ge(turned.sem, s.turned0 + i - 3)

        def pool_scale(pool, s, i, j, w, factors):
            pool.wait_ge(loaded[j].sem, loaded_count(s, i, j))
            v = nat[:, j, 0:w].rearrange("p (k c) -> p k c", c=P)
            nc.gpsimd.tensor_tensor(v, v, tail_bcast(factors, P), ALU.mult).then_inc(scaled.sem, 1)

        def pe_turn(pe, s, i, j, views):
            if s.mode == "scaled":
                pe.wait_ge(scaled.sem, s.scaled0 + i + 1)
            else:
                pe.wait_ge(loaded[j].sem, loaded_count(s, i, j))
            if not isinstance(i, int) or i >= 2:
                pe.wait_ge(lo.sem, s.lo0 + i - 1)
            for k, v in enumerate(views):
                rows, width = v.shape[0], v.free_size()
                mm = nc.tensor.transpose(turn_bank[j % 2][0:width, k * P:k * P + rows], v, ident[0:rows, 0:rows])
            mm.then_inc(turned.sem, 1)

        def pe_spread(pe, s, i, j, rows_used, at_hot, kts, cols):
            if not isinstance(i, int) or i >= 2:
                pe.wait_ge(dequant.sem, s.deq0 + i - 1)
            g = slice(0, rows_used)
            for k, (kt, rows) in enumerate(kts):
                for b, table in ((turn_bank[j % 2], zero), (bank[6 + j % 2], scale)):
                    n = cols.stop - cols.start if isinstance(cols, slice) else P
                    mm = nc.tensor.matmul(b[0:rows, k * P:k * P + n], hot[g, at_hot + kt * P:at_hot + kt * P + rows],
                                          table[g, cols], start=True, stop=True)
            mm.then_inc(turned.sem, 1)

        def dve_dequant(dve, s, i, j, parts):
            dve.wait_ge(loaded[j].sem, loaded_count(s, i, j))
            for n, (r, c) in enumerate(parts):
                v = nat[r, j, c].bitcast(I32)
                ins = nc.vector.tensor_scalar(v, v, shift[r, 0:1], 15, ALU.logical_shift_right, ALU.bitwise_and)
            ins.then_inc(unpacked.sem, 1)
            dve.wait_ge(unpacked.sem, s.un0 + i + 1)
            dve.wait_ge(turned.sem, s.turned0 + i + 1)
            if not isinstance(i, int) or i >= 2:
                dve.wait_ge(lo.sem, s.lo0 + i - 1)
            for r, c in parts:
                ins = nc.vector.tensor_tensor(deq[r, j % 2, c], nat[r, j, c].bitcast(I32),
                                              turn_bank[j % 2][r, c], ALU.subtract)
            ins.then_inc(centred.sem, 1)
            dve.wait_ge(centred.sem, s.cen0 + i + 1)
            for r, c in parts:
                ins = nc.vector.tensor_tensor(deq[r, j % 2, c], deq[r, j % 2, c],
                                              bank[6 + j % 2][r, c], ALU.mult)
            ins.then_inc(dequant.sem, 1)

        def chunk_source(s, j):
            if s.mode == "direct":
                return nat[:, j, :]
            if s.mode == "dequant":
                return deq[:, j % 2, :]
            return turn_bank[j % 2]

        def act_hi(act, s, i, j, parts):
            if s.mode == "direct":
                act.wait_ge(loaded[j].sem, loaded_count(s, i, j))
                if later(i):
                    act.wait_ge(used.sem, s.used0 + i - 3)
            elif s.mode == "dequant":
                act.wait_ge(dequant.sem, s.deq0 + i + 1)
            else:
                act.wait_ge(turned.sem, s.turned0 + i + 1)
            src = chunk_source(s, j)
            for r, c in parts:
                ins = nc.scalar.activation(w_hi[r, j, c], src[r, c], ACT.Copy)
            ins.then_inc(hi.sem, 1)

        def dve_lo(dve, s, i, j, parts):
            dve.wait_ge(hi.sem, s.hi0 + i + 1)
            src = chunk_source(s, j)
            for r, c in parts:
                ins = nc.vector.tensor_tensor(w_lo[r, j, c], src[r, c], w_hi[r, j, c].bitcast(F32), ALU.subtract)
            ins.then_inc(lo.sem, 1)

        def pe_chunk(pe, s, i, j, rows, rhs, to, first=True, last=True, more=None):
            pe.wait_ge(lo.sem, s.lo0 + i + 1)
            for half in range(NH):
                for k, n in enumerate(rows):
                    r_hi, r_lo = rhs(k, half)
                    for x, (w, r) in enumerate(((w_hi, r_hi), (w_hi, r_lo), (w_lo, r_hi))):
                        mm = nc.tensor.matmul(to[half][:, :], w[0:n, j, k * P:(k + 1) * P], r,
                                              start=first and k == 0 and x == 0,
                                              stop=last and more is None and k == len(rows) - 1 and x == 2)
                if more is not None:
                    mm = nc.tensor.matmul(to[half][:, :], *more(half), start=False, stop=True)
                if last and half == 0:
                    mm.then_inc(half0.sem, 1)
            mm.then_inc(used.sem, 1)

        ALL = [(slice(0, P), slice(0, D))]

        def whole(nkt, last_rows=P):
            if last_rows == P:
                return [(slice(0, P), slice(0, nkt * P))]
            return [(slice(0, P), slice(0, (nkt - 1) * P)), (slice(0, last_rows), slice((nkt - 1) * P, nkt * P))]

        def xn(k, half):
            return xn_hi[:, k, at(half)], xn_lo[:, k, at(half)]

        x_rows = t["L0_attn_x"].rearrange("b s d -> (b s) d").rearrange("(n p) d -> p n d", p=P)
        out_rows = out.rearrange("b s d -> (b s) d").rearrange("(n p) d -> p n d", p=P)
        DUP = P // HD

        def sp_start(sp):
            def get(dst, src):
                sp.dma_start(dst, src, allow_slow_non_contiguous=True).then_inc(cst_in.sem, 16)
                cst_in.count += 16

            get(cst[:, :], t["cst"])
            get(x_nat[:, :, :], x_rows)
            get(shift[:, :], t["shift"])
            b = t["L1_attn_b_qkv"]
            for kv in range(KV1):
                rows = slice(kv * HD, (kv + 1) * HD)
                get(bias1[rows, 0:QC], b[kv * QC * HD:(kv + 1) * QC * HD].rearrange("(c d) -> d c", d=HD))
            for n in range(2):
                get(bias1[:, QC + n:QC + n + 1], b[D + n * P:D + (n + 1) * P].rearrange("(d o) -> d o", o=1))
            get(bias1[:, QC + 2:], t["L1_attn_b_o"].rearrange("(c d) -> d c", d=P))
            get(bias3[:, 0:QC], t["L3_attn_wq_b"].rearrange("(c d) -> d c", d=P))
            for n, name in enumerate(("wk", "wv")):
                for r in range(DUP):
                    get(bias3[r * HD:(r + 1) * HD, QC + n:QC + n + 1],
                        t[f"L3_attn_{name}_b"].rearrange("(d o) -> d o", o=1))
            get(bias3[:, QC + 2:], t["L3_attn_wo_b"].rearrange("(c d) -> d c", d=P))
            for n, name in enumerate(("bq", "bk", "bv", "gq", "gk")):
                get(cols2[:, n, :], t[f"L2_attn_{name}"].rearrange("(h d) -> d h", d=P))
            get(bo2[:, :], t["L2_attn_bo"].rearrange("(c d) -> d c", d=P))
            for n, name in enumerate(("w1", "w3")):
                get(wscale[:, n, :, :], t[f"L3_ffn_{name}_scale"].rearrange("(o n) k -> o n k", o=1)
                    .broadcast_to([P, F14, KT]))
            get(wscale2[:, :, :], t["L3_ffn_w2_scale"].rearrange("(o n) k -> o n k", o=1)
                .broadcast_to([P, KT, F14]))
            sp.wait_ge(cst_in.sem, cst_in.count)
            barrier(sp)
            barrier(sp)

        def pe_start(pe, s):
            barrier(pe)
            for k in range(KT):
                for half in range(NH):
                    n = NH * k + half
                    if n >= 2:
                        pe.wait_ge(out_read.sem, s.out0 + n - 1)
                    for j in range(4):
                        mm = nc.tensor.transpose(turn_bank[n % 2][:, j * P:(j + 1) * P],
                                                 x_nat[:, 4 * half + j, k * P:(k + 1) * P], ident)
                    mm.then_inc(step_a.sem, 1)
            barrier(pe)

        def dve_start(dve, s):
            nc.vector.memset(eps[:, 0:1], LN_EPS)
            nc.vector.memset(eps[:, 1:2], RMS_EPS)
            for x in (hot, zero, scale):
                nc.vector.memset(x[:, :], 0.0)
            barrier(dve)
            for k in range(KT):
                for half in range(NH):
                    n = NH * k + half
                    dve.wait_ge(step_a.sem, s.a0 + n + 1)
                    nc.vector.tensor_copy(xT[:, k, at(half)], turn_bank[n % 2][:, :]).then_inc(out_read.sem, 1)
            barrier(dve)

        def act_start(act):
            barrier(act)
            nc.scalar.activation(ident16[:, :], ident, ACT.Copy)
            nc.scalar.activation(mask16[:, :], cst[:, C_MASK:C_MASK + P], ACT.Copy)
            barrier(act)

        def plan_start():
            s = Stage()
            s.out0, s.a0 = out_read.reserve(KT * NH), step_a.reserve(KT * NH)
            return s

        def pe_end(pe, s):
            for n in range(TOK // P):
                if n >= 2:
                    pe.wait_ge(out_read.sem, s.out0 + n - 1)
                for k in range(KT):
                    mm = nc.tensor.transpose(turn_bank[n % 2][:, k * P:(k + 1) * P],
                                             xT[:, k, n * P:(n + 1) * P], ident)
                mm.then_inc(step_a.sem, 1)
            barrier(pe)

        def dve_end(dve, s):
            for n in range(TOK // P):
                dve.wait_ge(step_a.sem, s.a0 + n + 1)
                nc.vector.tensor_copy(x_nat[:, n, :], turn_bank[n % 2][:, :]).then_inc(out_read.sem, 1)
            barrier(dve)

        def sp_end(sp, s):
            for n in range(TOK // P):
                sp.wait_ge(out_read.sem, s.out0 + n + 1)
                sp.dma_start(out_rows[:, n, :], x_nat[:, n, :]).then_inc(io.sem, 16)
            sp.wait_ge(io.sem, 16 * (TOK // P))
            barrier(sp)

        def plan_end():
            s = Stage()
            s.out0, s.a0 = out_read.reserve(TOK // P), step_a.reserve(TOK // P)
            return s

        def plan_norm():
            s = Stage()
            s.a0, s.b0, s.c0, s.d0, s.e0 = (x.reserve(n) for x, n in (
                (step_a, 4), (step_b, 2), (step_c, 4), (step_d, 4), (step_e, 2)))
            return s

        def pe_norm(pe, s):
            mean = cst[:, C_MEAN:C_MEAN + P]
            for half in range(NH):
                for k in range(KT):
                    mm = nc.tensor.matmul(acc[0][half][:, :], mean, xT[:, k, at(half)], start=k == 0, stop=k == KT - 1)
                mm.then_inc(step_a.sem, 1)
            for half in range(NH):
                pe.wait_ge(step_c.sem, s.c0 + half + 1)
                for k in range(KT):
                    mm = nc.tensor.matmul(acc[1][half][:, :], mean, sq[:, k, at(half)], start=k == 0, stop=k == KT - 1)
                mm.then_inc(step_a.sem, 1)
            barrier(pe)

        def dve_norm(dve, s):
            for half in range(NH):
                dve.wait_ge(step_a.sem, s.a0 + half + 1)
                nc.vector.tensor_tensor(cen[:, :, at(half)], xT[:, :, at(half)], bcast(acc[0][half][:, :], KT),
                                        ALU.subtract).then_inc(step_b.sem, 1)
            for half in range(NH):
                dve.wait_ge(step_c.sem, s.c0 + 2 + half + 1)
                nc.vector.reciprocal(inv[:, at(half)], inv[:, at(half)]).then_inc(step_d.sem, 1)
                dve.wait_ge(step_d.sem, s.d0 + 2 * half + 1)
                nc.vector.tensor_tensor(cen[:, :, at(half)], cen[:, :, at(half)], bcast(inv[:, at(half)], KT),
                                        ALU.mult).then_inc(step_d.sem, 1)
            barrier(dve)

        def act_norm(act, s):
            for half in range(NH):
                act.wait_ge(step_b.sem, s.b0 + half + 1)
                nc.scalar.activation(sq[:, :, at(half)], cen[:, :, at(half)], ACT.Square).then_inc(step_c.sem, 1)
            for half in range(NH):
                act.wait_ge(step_a.sem, s.a0 + 2 + half + 1)
                nc.scalar.activation(inv[:, at(half)], acc[1][half][:, :], ACT.Sqrt, bias=eps[:, 0:1])\
                  .then_inc(step_c.sem, 1)
            for half in range(NH):
                act.wait_ge(step_d.sem, s.d0 + 2 * half + 2)
                nc.scalar.activation(xn_hi[:, :, at(half)], cen[:, :, at(half)], ACT.Copy).then_inc(step_e.sem, 1)
            barrier(act)

        def pool_norm(pool, s):
            for half in range(NH):
                pool.wait_ge(step_e.sem, s.e0 + half + 1)
                nc.gpsimd.tensor_tensor(xn_lo[:, :, at(half)], cen[:, :, at(half)], xn_hi[:, :, at(half)].bitcast(F32),
                                        ALU.subtract)
            barrier(pool)

        def plan_up(width, mode, dmas, gate, up, h, sgf, spread=None, adapters=False, scales=None):
            nf = -(-width // P)
            s = plan_chunks(2 * nf, mode, dmas)
            s.nf, s.width, s.gate, s.up, s.h, s.sg, s.hf = nf, width, gate, up, h, sgf[:, 0], sgf[:, 1]
            s.spread, s.adapters, s.scales = spread, adapters, scales
            s.half00 = half0.reserve(2 * nf)
            s.gate0, s.up0 = gate_read.reserve(2 * nf), up_read.reserve(2 * nf)
            s.hhi0, s.hlo0 = h_hi_done.reserve(2 * nf), h_lo_done.reserve(2 * nf)
            s.small0 = small.reserve(2 * nf if adapters else 0)
            s.rounds, s.tail = nf // 2, nf % 2
            return s

        def up_rounds(eng, s, ahead, work):
            def body(it, n, n_next):
                for j in range(n):
                    work(4 * it + j, j, 2 * it + j // 2)
                    if j < n_next:
                        ahead(4 * it + 4 + j, j, 2 * it + 2 + j // 2)

            for j in range(SLOTS):
                ahead(j, j, j // 2)
            loop(eng, s.rounds - 1, lambda it: body(it, 4, 4))
            body(s.rounds - 1, 4, 2 * s.tail)
            if s.tail:
                body(s.rounds, 2, 0)

        def up_cols(s, ft):
            if isinstance(ft, int):
                return slice(ft * P, min((ft + 1) * P, s.width))
            return bass.ds(ft * P, P)

        def sp_up(sp, s):
            def load(i, j, ft):
                sp_slot(sp, s, i)
                w = (s.gate, s.up)[j % 2]
                if s.mode == "dequant":
                    cols = up_cols(s, ft)
                    n = cols.stop - cols.start if isinstance(cols, slice) else P
                    words = P // PACK
                    v = nat[:, j, :].bitcast(I32).rearrange("p (k c) -> p k c", c=P)
                    for x in range(PACK):
                        sp.dma_start(v[x:P:PACK, :, 0:n], w.rearrange("(k r) c -> r k c", r=words)[:, :, cols])\
                          .then_inc(loaded[j].sem, 16)
                else:
                    rows = up_cols(s, ft)
                    n = rows.stop - rows.start if isinstance(rows, slice) else P
                    sp.dma_start(nat[0:n, j, :], w[rows, :]).then_inc(loaded[j].sem, 16)

            up_rounds(sp, s, load, lambda i, j, ft: None)
            barrier(sp)

        def pe_up(pe, s):
            def ahead(i, j, ft):
                if s.mode == "dequant":
                    pe_spread(pe, s, i, j, P, D * (j % 2), [(k, P) for k in range(KT)],
                              up_cols(s, ft))
                else:
                    pe_turn(pe, s, i, j, [nat[:, j, k * P:(k + 1) * P] for k in range(KT)])

            def work(i, j, ft):
                pe.wait_ge((gate_read, up_read)[j % 2].sem, (s.gate0, s.up0)[j % 2] + 2 * ft)
                more = None
                if s.adapters:
                    pe.wait_ge(small.sem, s.small0 + i + 1)
                    r = slice(32 * (j % 2), 32 * (j % 2) + RANK)
                    more = lambda half: (b13s[r, j, :], low[r, at(half)])
                pe_chunk(pe, s, i, j, [P] * KT, xn, acc[j % 2], more=more)

            up_rounds(pe, s, ahead, work)
            barrier(pe)

        def act_up(act, s):
            def work(i, j, ft):
                for half in range(NH):
                    if j % 2 == 0:
                        if half == 0:
                            act.wait_ge(half0.sem, s.half00 + i + 1)
                            act.wait_ge(up_read.sem, s.up0 + 2 * ft)
                        else:
                            act.wait_ge(used.sem, s.used0 + i + 1)
                        nc.scalar.activation(s.sg[:, half, :], acc[0][half][:, :], ACT.Silu).then_inc(gate_read.sem, 1)
                    else:
                        act.wait_ge(up_read.sem, s.up0 + 2 * ft + half + 1)
                        nc.scalar.activation(s.h[0][:, bass.ds(ft, 1), at(half)].rearrange("p o c -> p (o c)"),
                                             s.hf[:, half, :], ACT.Copy).then_inc(h_hi_done.sem, 1)

            up_rounds(act, s, lambda i, j, ft: act_hi(act, s, i, j, ALL), work)
            barrier(act)

        def dve_up(dve, s):
            def ahead(i, j, ft):
                if s.mode == "dequant":
                    dve_dequant(dve, s, i, j, ALL)
                dve_lo(dve, s, i, j, ALL)
                if s.adapters:
                    nc.vector.tensor_scalar(b13s[0:48, j, :], b13[0:48, bass.ds(ft * P, P)], LORA, None, ALU.mult)\
                      .then_inc(small.sem, 1)

            def work(i, j, ft):
                if j % 2 == 0:
                    return
                for half in range(NH):
                    if half == 0:
                        dve.wait_ge(half0.sem, s.half00 + i + 1)
                        dve.wait_ge(h_lo_done.sem, s.hlo0 + 2 * ft)
                    else:
                        dve.wait_ge(used.sem, s.used0 + i + 1)
                    dve.wait_ge(gate_read.sem, s.gate0 + 2 * ft + half + 1)
                    nc.vector.tensor_tensor(s.hf[:, half, :], s.sg[:, half, :], acc[1][half][:, :], ALU.mult)\
                      .then_inc(up_read.sem, 1)

            up_rounds(dve, s, ahead, work)
            barrier(dve)

        def pool_up(pool, s):
            def ahead(i, j, ft):
                if s.scales is not None:
                    pool_scale(pool, s, i, j, D, s.scales[:, j % 2, bass.ds(ft, 1), :].rearrange("p o k -> p (o k)"))

            def work(i, j, ft):
                if j % 2 == 0:
                    return
                for half in range(NH):
                    pool.wait_ge(h_hi_done.sem, s.hhi0 + 2 * ft + half + 1)
                    o = [x[:, bass.ds(ft, 1), at(half)].rearrange("p o c -> p (o c)") for x in s.h]
                    nc.gpsimd.tensor_tensor(o[1], s.hf[:, half, :], o[0].bitcast(F32), ALU.subtract)\
                      .then_inc(h_lo_done.sem, 1)

            up_rounds(pool, s, ahead, work)
            barrier(pool)

        def plan_proj(chunks, mode, n_tiles, rhs, engine):
            s = plan_chunks(len(chunks), mode, [len(c["loads"]) for c in chunks])
            s.chunks, s.n_tiles, s.rhs, s.engine = chunks, n_tiles, rhs, engine
            s.half00 = half0.reserve(n_tiles)
            s.out0 = out_read.reserve(2 * n_tiles)
            return s

        def proj_order(s, ahead, work):
            for i in range(min(SLOTS, s.n)):
                ahead(i, i % SLOTS, s.chunks[i])
            for i in range(s.n):
                work(i, i % SLOTS, s.chunks[i])
                if i + SLOTS < s.n:
                    ahead(i + SLOTS, i % SLOTS, s.chunks[i + SLOTS])

        def sp_proj(sp, s):
            def load(i, j, c):
                sp_slot(sp, s, i)
                for dst, src in c["loads"]:
                    sp.dma_start(dst(j), src).then_inc(loaded[j].sem, 16)

            proj_order(s, load, lambda i, j, c: None)
            barrier(sp)

        def pe_proj(pe, s):
            def ahead(i, j, c):
                if s.mode == "dequant":
                    pe_spread(pe, s, i, j, GROUPS_DOWN, 0, c["kts"], c["cols"])
                elif s.mode != "direct":
                    pe_turn(pe, s, i, j, c["views"](j))

            def work(i, j, c):
                if c["first"] and c["tile"] >= 2:
                    pe.wait_ge(out_read.sem, s.out0 + 2 * (c["tile"] - 1))
                pe_chunk(pe, s, i, j, c["rows"], lambda k, half: s.rhs(c["k0"] + k, half, c["rows"][k]),
                         acc[c["tile"] % 2], c["first"], c["last"], c.get("more"))

            proj_order(s, ahead, work)
            barrier(pe)

        def sums_ready(eng, s, i, tile, half):
            if half == 0:
                eng.wait_ge(half0.sem, s.half00 + tile + 1)
            else:
                eng.wait_ge(used.sem, s.used0 + i + 1)

        def act_proj(act, s):
            def work(i, j, c):
                if s.engine != "act" or not c["last"]:
                    return
                for half in range(NH):
                    sums_ready(act, s, i, c["tile"], half)
                    dst, b, factor = c["to"](half)
                    n = dst.shape[0]
                    nc.scalar.activation(dst, acc[c["tile"] % 2][half][0:n, :], ACT.Identity,
                                         bias=0.0 if b is None else b, scale=factor).then_inc(out_read.sem, 1)

            proj_order(s, lambda i, j, c: act_hi(act, s, i, j, c["parts"]), work)
            barrier(act)

        def dve_proj(dve, s):
            def ahead(i, j, c):
                if s.mode == "dequant":
                    dve_dequant(dve, s, i, j, c["parts"])
                dve_lo(dve, s, i, j, c["parts"])

            def work(i, j, c):
                if s.engine != "dve" or not c["last"]:
                    return
                for half in range(NH):
                    sums_ready(dve, s, i, c["tile"], half)
                    x = xT[:, c["tile"], at(half)]
                    a = acc[c["tile"] % 2][half][:, :]
                    if c.get("bias") is None:
                        ins = nc.vector.tensor_tensor(x, a, x, ALU.add)
                    else:
                        ins = nc.vector.scalar_tensor_tensor(x, a, c["bias"], x, ALU.add, ALU.add)
                    ins.then_inc(out_read.sem, 1)

            proj_order(s, ahead, work)
            barrier(dve)

        def pool_proj(pool, s):
            if s.mode == "scaled":
                proj_order(s, lambda i, j, c: pool_scale(pool, s, i, j, len(c["rows"]) * P, c["scales"]),
                           lambda i, j, c: None)
            barrier(pool)

        def nat_views(n, rows=P, last=P):
            return lambda j: [nat[0:rows, j, k * P:k * P + (P if k < n - 1 else last)] for k in range(n)]

        def slot(*index):
            return lambda j: nat[(index[0], j) + tuple(index[1:])]

        def rows_chunk(w, r0, k0=0, **more):
            return dict(loads=[(slot(slice(0, P), slice(0, D)), w[r0:r0 + P, :])], parts=ALL, rows=[P] * KT,
                        views=nat_views(KT), first=True, last=True, k0=k0, **more)

        def split_kts(nf):
            q = -(-nf // 4)
            return [list(range(a, min(a + q, nf))) for a in range(0, nf, q)]

        def h_of(h):
            return lambda k, half, rows: (h[0][0:rows, k, at(half)], h[1][0:rows, k, at(half)])

        def down_chunks(w, width, scales=None, more=None):
            found = []
            nf = -(-width // P)
            for m in range(-(-w.shape[0] // P)):
                for kts in split_kts(nf):
                    a, b = kts[0] * P, min((kts[-1] + 1) * P, width)
                    last = b - kts[-1] * P
                    n = len(kts)
                    r = min(P, w.shape[0] - m * P)
                    c = dict(loads=[(slot(slice(0, r), slice(0, b - a)), w[m * P:m * P + r, a:b])],
                             parts=whole(n, last), rows=[P] * (n - 1) + [last], views=nat_views(n, last=last),
                             first=a == 0, last=b == width, k0=kts[0], tile=m)
                    if scales is not None:
                        c["scales"] = scales[:, m, kts[0]:kts[0] + n]
                    if more is not None and b == width:
                        c["more"] = more(m)
                    found.append(c)
            return found

        def packed_down_chunks(w, width):
            found = []
            nf = -(-width // P)
            words = P // PACK
            for m in range(KT):
                for kts in split_kts(nf):
                    n = len(kts)
                    last = min(P, width - kts[-1] * P)
                    loads = []
                    for x in range(PACK):
                        for k0, n_k, rows in ((0, n if last == P else n - 1, P), (n - 1, 1 if last < P else 0, last)):
                            if n_k:
                                r0 = (kts[0] + k0) * words
                                r1 = r0 + n_k * words if rows == P else r0 + rows // PACK
                                dst = (lambda j, x=x, k0=k0, n_k=n_k, rows=rows:
                                       nat[x:rows:PACK, j, k0 * P:(k0 + n_k) * P].bitcast(I32)
                                       .rearrange("r (k c) -> r k c", c=P))
                                src = w[r0:r1, m * P:(m + 1) * P].rearrange("(k r) c -> r k c", k=n_k)
                                loads.append((dst, src))
                    found.append(dict(loads=loads, parts=whole(n, last), rows=[P] * (n - 1) + [last],
                                      kts=[(k, P if k < kts[-1] else last) for k in kts],
                                      cols=slice(m * P, (m + 1) * P), first=kts[0] == 0,
                                      last=kts[-1] == nf - 1, k0=kts[0], tile=m))
            return found

        def sp_tables(sp, s):
            for base, name, groups, n_in, width in s.which:
                g = slice(base, base + groups)
                for dst, src in (
                    (zero[g, 0:n_in].bitcast(I32), t[f"L0_ffn_{name}_g_idx"].rearrange("(o k) -> o k", o=1)
                     .broadcast_to([groups, n_in])),
                    (packed[g, 0:width // PACK], t[f"L0_ffn_{name}_qzeros"]),
                    (scale[g, 0:width], t[f"L0_ffn_{name}_scales"])):
                    sp.dma_start(dst, src).then_inc(cst_in.sem, 16)
                    cst_in.count += 16
            sp.wait_ge(cst_in.sem, cst_in.count)
            barrier(sp)
            barrier(sp)

        def dve_tables(dve, s):
            barrier(dve)

            def chain(ins):
                s.count += 1
                ins.then_inc(step_b.sem, 1)
                dve.wait_ge(step_b.sem, s.count)

            for base, name, groups, n_in, width in s.which:
                g = slice(base, base + groups)
                h, n = hot[g, D * (base // 32):D * (base // 32) + n_in], sgf0[g, :, :, :].rearrange("p a b c -> p (a b c)")[:, 0:n_in]
                chain(nc.vector.tensor_copy(h, zero[g, 0:n_in].bitcast(I32)))
                chain(nc.vector.tensor_scalar(n, h, 0.0, float(groups), ALU.is_lt, ALU.mult))
                chain(nc.vector.tensor_tensor(h, h, n, ALU.add))
                chain(nc.vector.tensor_scalar(h, h, 0.0, groups - 1.0, ALU.max, ALU.min))
                chain(nc.vector.tensor_scalar(n, h, cst[g, C_IDX:C_IDX + 1], float(-base), ALU.subtract, ALU.subtract))
                chain(nc.vector.tensor_scalar(h, n, 0.0, None, ALU.is_equal))
                z = zero[g, 0:width]
                for x in range(PACK):
                    zi = z.bitcast(I32).rearrange("p (n x) -> p n x", x=PACK)[:, :, x]
                    chain(nc.vector.tensor_scalar(zi, packed[g, 0:width // PACK], 32 // PACK * x, 15,
                                                  ALU.logical_shift_right, ALU.bitwise_and))
                chain(nc.vector.tensor_scalar(z, z.bitcast(I32), 1.0, None, ALU.add))
            barrier(dve)

        def plan_tables(which):
            s = Stage()
            s.which = which
            s.count = step_b.count
            step_b.count += len(which) * (7 + PACK)
            return s

        def plan_prep(rope, n_k, n_v):
            s = Stage()
            s.rope, s.n_v = rope, n_v
            s.tiles = [(x, c, half) for x, n in ((at_q, QC), (at_k, n_k)) for c in range(n) for half in range(NH)]
            s.tiles = s.tiles if rope else []
            n = len(s.tiles)
            s.a0, s.b0, s.c0, s.d0 = (x.reserve(n) for x in (step_a, step_b, step_c, step_d))
            s.vr0, s.vc0 = v_ready.reserve(2 * n_v), v_copied.reserve(2 * n_v)
            return s

        def pe_prep(pe, s):
            for n, (x, c, half) in enumerate(s.tiles):
                if n >= 2:
                    pe.wait_ge(step_b.sem, s.b0 + n - 1)
                r = s.rope[2]
                nc.tensor.matmul(turn_bank[n % 2][:, :], cst[:, r:r + P], x[:, c, at(half)], start=True, stop=True)\
                  .then_inc(step_a.sem, 1)
            for n in range(2 * s.n_v):
                if n >= 2:
                    pe.wait_ge(v_copied.sem, s.vc0 + n - 1)
                for j in range(4):
                    tt = 4 * (n % 2) + j
                    mm = nc.tensor.transpose(bank[2 + n % 2][:, j * P:(j + 1) * P],
                                             at_v[:, n // 2, tt * P:(tt + 1) * P], ident)
                mm.then_inc(v_ready.sem, 1)
            barrier(pe)

        def seqs(ap):
            return ap.rearrange("p (b s) -> p b s", s=SEQ)

        def dve_prep(dve, s):
            for n, (x, c, half) in enumerate(s.tiles):
                rot = at_km[:, n % 2, 0:2, :]
                dve.wait_ge(step_a.sem, s.a0 + n + 1)
                if n >= 2:
                    dve.wait_ge(step_d.sem, s.d0 + n - 1)
                nc.vector.tensor_tensor(rot, seqs(turn_bank[n % 2][:, :]),
                                        bcast(cst[:, s.rope[1]:s.rope[1] + SEQ], 2), ALU.mult).then_inc(step_b.sem, 1)
                dve.wait_ge(step_b.sem, s.b0 + n + 1)
                dve.wait_ge(step_c.sem, s.c0 + n + 1)
                nc.vector.tensor_tensor(seqs(x[:, c, at(half)]), seqs(x[:, c, at(half)]), rot, ALU.add)\
                  .then_inc(step_d.sem, 1)
            for n in range(2 * s.n_v):
                dve.wait_ge(v_ready.sem, s.vr0 + n + 1)
                tt = 4 * (n % 2)
                nc.vector.tensor_copy(at_val[:, tt:tt + 4, n // 2, :, 0:HD],
                                      bank[2 + n % 2][:, :].rearrange("p (t h d) -> p t h d", t=4, h=HPC))\
                  .then_inc(v_copied.sem, 1)
            barrier(dve)

        def pool_prep(pool, s):
            nc.gpsimd.memset(at_val[:, :, 0:s.n_v, :, HD:VW].rearrange("p t c h o -> p t (c h o)"), 1.0)
            for n, (x, c, half) in enumerate(s.tiles):
                pool.wait_ge(step_a.sem, s.a0 + n + 1)
                v = seqs(x[:, c, at(half)])
                nc.gpsimd.tensor_tensor(v, v, bcast(cst[:, s.rope[0]:s.rope[0] + SEQ], 2), ALU.mult)\
                  .then_inc(step_c.sem, 1)
            barrier(pool)

        STEPS = 6
        ALL_STEPS = STEPS * QC

        def plan_att(n_k, n_v):
            s = Stage()
            n = BATCH * ALL_STEPS
            s.n_k, s.n_v = n_k, n_v
            s.sr, s.mx, s.ex, s.pr, s.pc, s.pv = (x.reserve(n) for x in (
                s_ready, max_done, exp_done, pt_ready, pt_copied, pv_done))
            s.on, s.tr, s.th, s.tl, s.sm = (x.reserve(BATCH * QC) for x in (o_normed, ot_ready, ot_hi, ot_lo, small))
            s.km, s.qs = km_made.reserve(BATCH * n_k), qs_made.reserve(BATCH)
            return s

        def step_heads(part):
            return (0, 4 * part, 4) if part < 2 else (1, 2 * (part - 2), 2)

        def pe_att(pe, s):
            def body(b):
                def scores(n):
                    c, part = divmod(n, STEPS)
                    qt, h, nh = step_heads(part)
                    if n == 0:
                        pe.wait_ge(qs_made.sem, s.qs + b + 1)
                    if part == 0 and c < s.n_k:
                        pe.wait_ge(km_made.sem, s.km + s.n_k * b + c + 1)
                    if n >= 3:
                        pe.wait_ge(exp_done.sem, s.ex + ALL_STEPS * b + n - 2)
                    o = bank[n % 3][:, :].rearrange("p (h k) -> p h k", h=nh)
                    keys = (qt + 1) * P
                    nc.tensor.matmul(o, at_qs[:, c, qt * P:(qt + 1) * P],
                                     at_km[:, c % 2 if s.n_k > 1 else 0, h:h + nh, 0:keys], start=True, stop=False)
                    nc.tensor.matmul(o[:, :, qt * P:keys], ident16[:, :], bcast(mask16[:, :], nh), start=False, stop=True)\
                      .then_inc(s_ready.sem, 1)

                def turns(n):
                    pe.wait_ge(exp_done.sem, s.ex + ALL_STEPS * b + n + 1)
                    if n >= 2:
                        pe.wait_ge(pt_copied.sem, s.pc + ALL_STEPS * b + n - 1)
                    for j in range(4):
                        mm = nc.tensor.transpose(bank[3 + n % 2][:, j * P:(j + 1) * P],
                                                 at_p[:, n % 3, j * P:(j + 1) * P], ident)
                    mm.then_inc(pt_ready.sem, 1)

                def values(n):
                    c, part = divmod(n, STEPS)
                    qt, h, nh = step_heads(part)
                    pe.wait_ge(pt_copied.sem, s.pc + ALL_STEPS * b + n + 1)
                    if part == 0 and c >= 2:
                        pe.wait_ge(o_normed.sem, s.on + QC * b + c - 1)
                    o = bank[5 + c % 2][:, 0:2 * HPC * VW].rearrange("p (q h d) -> p q h d", q=2, h=HPC)
                    for x in range(nh):
                        for kb in range(qt + 1):
                            j = x * (qt + 1) + kb
                            v = at_val[:, bass.ds(2 * b + kb, 1), c if s.n_v > 1 else 0, h + x, :]
                            mm = nc.tensor.matmul(o[:, qt, h + x, :], at_pt[:, n % 2, j * P:(j + 1) * P],
                                                  v.rearrange("p o d -> p (o d)"), start=kb == 0, stop=kb == qt)
                    mm.then_inc(pv_done.sem, 1)

                def turn_out(c):
                    pe.wait_ge(o_normed.sem, s.on + QC * b + c + 1)
                    pe.wait_ge(ot_lo.sem, s.tl + QC * b + c)
                    for qt in range(2):
                        mm = nc.tensor.transpose(bank[7][:, qt * P:(qt + 1) * P], at_on[:, c % 2, qt, :], ident)
                    mm.then_inc(ot_ready.sem, 1)

                scores(0)
                scores(1)
                for n in range(ALL_STEPS):
                    if n + 2 < ALL_STEPS:
                        scores(n + 2)
                    turns(n)
                    if n >= 1:
                        values(n - 1)
                    if n >= 8 and n % STEPS == 2:
                        turn_out(n // STEPS - 1)
                values(ALL_STEPS - 1)
                turn_out(QC - 1)

            loop(pe, BATCH, body)
            barrier(pe)

        def dve_att(dve, s):
            def body(b):
                def top(n):
                    qt, h, nh = step_heads(n % STEPS)
                    dve.wait_ge(s_ready.sem, s.sr + ALL_STEPS * b + n + 1)
                    nc.vector.tensor_reduce(at_small[:, 4 * (n % 3):4 * (n % 3) + nh],
                                            bank[n % 3][:, :].rearrange("p (h k) -> p h k", h=nh), AX.X, ALU.max,
                                            negate=True).then_inc(max_done.sem, 1)

                def copy(n):
                    dve.wait_ge(pt_ready.sem, s.pr + ALL_STEPS * b + n + 1)
                    if n >= 2:
                        dve.wait_ge(pv_done.sem, s.pv + ALL_STEPS * b + n - 1)
                    nc.vector.tensor_copy(at_pt[:, n % 2, :], bank[3 + n % 2][:, :]).then_inc(pt_copied.sem, 1)

                def norm(c):
                    dve.wait_ge(pv_done.sem, s.pv + ALL_STEPS * b + STEPS * (c + 1))
                    o = bank[5 + c % 2][:, 0:2 * HPC * VW].rearrange("p (q h d) -> p q h d", q=2, h=HPC)
                    r = at_small[:, 16 + 16 * (c % 2):32 + 16 * (c % 2)].rearrange("p (q h o) -> p q h o", q=2, o=1)
                    nc.vector.reciprocal(r, o[:, :, :, HD:VW]).then_inc(small.sem, 1)
                    dve.wait_ge(small.sem, s.sm + QC * b + c + 1)
                    if c >= 2:
                        dve.wait_ge(ot_ready.sem, s.tr + QC * b + c - 1)
                    nc.vector.tensor_tensor(at_on[:, c % 2, :, :].rearrange("p q (h d) -> p q h d", d=HD),
                                            o[:, :, :, 0:HD], r.broadcast_to([P, 2, HPC, HD]), ALU.mult)\
                      .then_inc(o_normed.sem, 1)

                def low_part(c):
                    dve.wait_ge(ot_hi.sem, s.th + QC * b + c + 1)
                    nc.vector.tensor_tensor(at_lo[:, c, bass.ds(b * SEQ, SEQ)], bank[7][:, 0:SEQ],
                                            at_hi[:, c, bass.ds(b * SEQ, SEQ)].bitcast(F32), ALU.subtract)\
                      .then_inc(ot_lo.sem, 1)

                top(0)
                for n in range(ALL_STEPS):
                    if n + 1 < ALL_STEPS:
                        top(n + 1)
                    copy(n)
                    if n >= STEPS and n % STEPS == 0:
                        norm(n // STEPS - 1)
                    if n >= 9 and n % STEPS == 3:
                        low_part(n // STEPS - 1)
                norm(QC - 1)
                low_part(QC - 1)

            loop(dve, BATCH, body)
            barrier(dve)

        def act_att(act, s):
            def body(b):
                def high_part(c):
                    act.wait_ge(ot_ready.sem, s.tr + QC * b + c + 1)
                    nc.scalar.activation(at_hi[:, c, bass.ds(b * SEQ, SEQ)], bank[7][:, 0:SEQ], ACT.Copy)\
                      .then_inc(ot_hi.sem, 1)

                for n in range(ALL_STEPS):
                    qt, h, nh = step_heads(n % STEPS)
                    act.wait_ge(max_done.sem, s.mx + ALL_STEPS * b + n + 1)
                    if n >= 3:
                        act.wait_ge(pt_ready.sem, s.pr + ALL_STEPS * b + n - 2)
                    w = 512 // nh
                    for x in range(nh):
                        ins = nc.scalar.activation(at_p[:, n % 3, x * w:(x + 1) * w], bank[n % 3][:, x * w:(x + 1) * w],
                                                   ACT.Exp, bias=at_small[:, 4 * (n % 3) + x:4 * (n % 3) + x + 1])
                    ins.then_inc(exp_done.sem, 1)
                    if n >= 9 and n % STEPS == 3:
                        high_part(n // STEPS - 1)
                high_part(QC - 1)

            loop(act, BATCH, body)
            barrier(act)

        def pool_att(pool, s):
            def body(b):
                pool.wait_ge(s_ready.sem, s.sr + ALL_STEPS * b)
                nc.gpsimd.tensor_copy(at_qs[:, :, :], at_q[:, :, bass.ds(b * SEQ, SEQ)]).then_inc(qs_made.sem, 1)
                for c in range(s.n_k):
                    if c >= 2:
                        pool.wait_ge(s_ready.sem, s.sr + ALL_STEPS * b + STEPS * (c - 1))
                    nc.gpsimd.tensor_tensor(at_km[:, c % 2, :, :], bcast(at_k[:, c, bass.ds(b * SEQ, SEQ)], HPC),
                                            tail_bcast(cst[:, C_HEAD:C_HEAD + HPC], SEQ), ALU.mult)\
                      .then_inc(km_made.sem, 1)

            loop(pool, BATCH, body)
            barrier(pool)

        def plan_qk2():
            s = plan_chunks(2 * H2, "direct", 1)
            n = 4 * H2
            s.half00, s.sq0, s.ssq0 = half0.reserve(2 * H2), sq_done.reserve(n), ssq_done.reserve(n)
            s.small0 = small.reserve(2 * H2)
            s.raw0 = [x.reserve(2 * H2) for x in raw_done]
            s.st0 = [x.reserve(16 * H2 // 2) for x in stored]
            s.rounds, s.tail = H2 // 2, 0
            return s

        def sp_qk2(sp, s):
            def load(i, j, h):
                sp_slot(sp, s, i)
                w = t["L2_attn_W" + "qk"[j % 2]].rearrange("(k p) n -> p k n", p=P)
                sp.dma_start(nat[:, j, :].rearrange("p (k c) -> p k c", c=P), w[:, :, bass.ds(h * P, P)])\
                  .then_inc(loaded[j].sem, 16)

            def store(i, j, h):
                sp.wait_ge(raw_done[j % 2].sem, s.raw0[j % 2] + 2 * h + 2)
                sp.dma_start(qk_dram[bass.ds(h, 1), j % 2, :, :].rearrange("o p c -> (o p) c"), raw2[:, j, :])\
                  .then_inc(stored[j].sem, 16)

            up_rounds(sp, s, load, store)
            for j in range(SLOTS):
                sp.wait_ge(stored[j].sem, stored[j].count)
            barrier(sp)

        def pe_qk2(pe, s):
            def work(i, j, h):
                pe.wait_ge(raw_done[j % 2].sem, s.raw0[j % 2] + 2 * h)
                pe_chunk(pe, s, i, j, [P] * KT, xn, acc[j % 2])

            barrier(pe)
            up_rounds(pe, s, lambda i, j, h: None, work)
            barrier(pe)

        def act_qk2(act, s):
            def work(i, j, h):
                for half in range(NH):
                    if half == 0:
                        act.wait_ge(half0.sem, s.half00 + i + 1)
                        act.wait_ge(small.sem, s.small0 + i + 1)
                        act.wait_ge(ssq_done.sem, s.ssq0 + 2 * (i - j))
                    else:
                        act.wait_ge(used.sem, s.used0 + i + 1)
                    nc.scalar.activation(sq2[:, j, at(half)], acc[j % 2][half][:, :], ACT.Square,
                                         bias=b2s[:, j:j + 1]).then_inc(sq_done.sem, 1)

            barrier(act)
            up_rounds(act, s, lambda i, j, h: act_hi(act, s, i, j, ALL), work)
            barrier(act)

        def dve_qk2(dve, s):
            def ahead(i, j, h):
                nc.vector.tensor_scalar(b2s[:, j:j + 1], cols2[:, j % 2, bass.ds(h, 1)], 0.0, None, ALU.add)\
                  .then_inc(small.sem, 1)
                dve_lo(dve, s, i, j, ALL)

            def work(i, j, h):
                for half in range(NH):
                    dve.wait_ge(sq_done.sem, s.sq0 + 2 * i + half + 1)
                    if half == 0:
                        dve.wait_ge(stored[j].sem, s.st0[j] + 4 * (i - j))
                    nc.vector.tensor_scalar(raw2[:, j, at(half)], acc[j % 2][half][:, :],
                                            cols2[:, j % 2, bass.ds(h, 1)], cols2[:, 3 + j % 2, bass.ds(h, 1)],
                                            ALU.add, ALU.mult).then_inc(raw_done[j % 2].sem, 1)

            barrier(dve)
            up_rounds(dve, s, ahead, work)
            barrier(dve)

        def pool_qk2(pool, s):
            def work(i, j, h):
                for half in range(NH):
                    pool.wait_ge(sq_done.sem, s.sq0 + 2 * i + half + 1)
                    pool.wait_ge(ssq_done.sem, s.ssq0 + 2 * i + half)
                    v = ssq[:, j % 2, at(half)]
                    nc.gpsimd.tensor_tensor(v, v, sq2[:, j, at(half)], ALU.add).then_inc(ssq_done.sem, 1)

            nc.gpsimd.memset(ssq[:, :, :], 0.0)
            barrier(pool)
            up_rounds(pool, s, lambda i, j, h: None, work)
            barrier(pool)

        def plan_rms():
            s = Stage()
            s.a0, s.b0, s.c0 = step_a.reserve(4), step_b.reserve(4), step_c.reserve(4)
            return s

        def pe_rms(pe, s):
            for n in range(2):
                for half in range(NH):
                    nc.tensor.matmul(acc[n][half][:, :], cst[:, C_MEAN2:C_MEAN2 + P], ssq[:, n, at(half)],
                                     start=True, stop=True).then_inc(step_a.sem, 1)
            barrier(pe)

        def act_rms(act, s):
            for n in range(2):
                for half in range(NH):
                    act.wait_ge(step_a.sem, s.a0 + 2 * n + half + 1)
                    nc.scalar.activation((rms_q, rms_k)[n][:, at(half)], acc[n][half][:, :], ACT.Sqrt, bias=eps[:, 1:2])\
                      .then_inc(step_b.sem, 1)
            barrier(act)

        def dve_rms(dve, s):
            for m in range(KT):
                nc.vector.tensor_scalar(xT[:, m, :], xT[:, m, :], bo2[:, m:m + 1], None, ALU.add)
            for n in range(2):
                for half in range(NH):
                    dve.wait_ge(step_b.sem, s.b0 + 2 * n + half + 1)
                    v = (rms_q, rms_k)[n][:, at(half)]
                    nc.vector.reciprocal(v, v).then_inc(step_c.sem, 1)
            dve.wait_ge(step_c.sem, s.c0 + 2)
            nc.vector.tensor_scalar(rms_q[:, :], rms_q[:, :], float(1.0 / np.sqrt(HD2)), None, ALU.mult)
            barrier(dve)

        GSTEPS = GRP2 * BATCH

        def plan_att2():
            groups = H2 // GRP2
            s = plan_chunks(groups * 2 * SLOTS, "direct", 1)
            used.count -= groups * SLOTS
            n = groups * GSTEPS
            s.groups = groups
            s.sr, s.mx, s.ex, s.nd, s.pr, s.pc, s.pv, s.sm, s.oh, s.ol = (x.reserve(n) for x in (
                s_ready, max_done, exp_done, norm_done, pt_ready, pt_copied, pv_done, small, o_hi_done, o_lo_done))
            s.bv = bias_in.reserve(groups)
            s.qi, s.qs, s.qh, s.ql = (qk_in.reserve(16 * H2), qk_scaled.reserve(2 * H2), qk_hi_done.reserve(H2),
                                      qk_lo_done.reserve(H2))
            s.vr, s.vc = v_ready.reserve(2 * H2), v_copied.reserve(2 * H2)
            s.half00, s.out0 = half0.reserve(groups * KT), out_read.reserve(groups * 2 * KT)
            return s

        def sp_att2(sp, s):
            wv = t["L2_attn_Wv"].rearrange("(k p) n -> p k n", p=P)

            def body(g):
                for x in range(GRP2):
                    h = GRP2 * g + x
                    sp.wait_ge(lo.sem, s.lo0 + 8 * g + x - 3 if x >= 3 else s.lo0 + 8 * g)
                    sp.dma_start(nat[:, x, :].rearrange("p (k c) -> p k c", c=P), wv[:, :, bass.ds(h * P, P)])\
                      .then_inc(loaded[x].sem, 16)
                for x in range(GRP2):
                    h = GRP2 * g + x
                    sp.wait_ge(qk_lo_done.sem, s.ql + h)
                    sp.dma_start(qk_raw[:, :, :], qk_dram[bass.ds(h, 1), :, :, :].rearrange("o n p c -> (o p) n c"))\
                      .then_inc(qk_in.sem, 16)
                    sp.wait_ge(lo.sem, s.lo0 + 8 * g + x + 1)
                    sp.dma_start(nat[:, x, :].rearrange("p (k c) -> p k c", c=P),
                                 t["L2_attn_Wo"].rearrange("(h p) n -> p h n", p=P)
                                 [:, bass.ds(GRP2 * g, GRP2), x * P:(x + 1) * P]).then_inc(loaded[x].sem, 16)

            loop(sp, s.groups, body)
            barrier(sp)

        def pe_att2(pe, s):
            def body(g):
                base = GSTEPS * g

                def values_of(x):
                    i = 8 * g + x
                    h = GRP2 * g + x
                    pe.wait_ge(lo.sem, s.lo0 + i + 1)
                    for n in range(2):
                        pe.wait_ge(v_copied.sem, s.vc + 2 * h)
                        for tt in range(4 * n, 4 * n + 4):
                            for k in range(KT):
                                for y, (a, w) in enumerate(((xn_hi, w_hi), (xn_lo, w_hi), (xn_hi, w_lo))):
                                    mm = nc.tensor.matmul(bank[6 + n][:, tt % 4 * P:(tt % 4 + 1) * P],
                                                          a[:, k, tt * P:(tt + 1) * P], w[:, x, k * P:(k + 1) * P],
                                                          start=k == 0 and y == 0, stop=k == KT - 1 and y == 2)
                        mm.then_inc(v_ready.sem, 1)

                def scores(n):
                    x, b = divmod(n, BATCH)
                    if b == 0:
                        pe.wait_ge(qk_lo_done.sem, s.ql + GRP2 * g + x + 1)
                    if n >= 2:
                        pe.wait_ge(exp_done.sem, s.ex + base + n - 1)
                    for qt in range(2):
                        q = slice(b * SEQ + qt * P, b * SEQ + (qt + 1) * P)
                        for y, (a, c) in enumerate(((qk_hi, qk_hi), (qk_hi, qk_lo), (qk_lo, qk_hi))):
                            mm = nc.tensor.matmul(bank[n % 2][:, qt * SEQ:(qt + 1) * SEQ], a[:, x % 2, 0, q],
                                                  c[:, x % 2, 1, b * SEQ:(b + 1) * SEQ], start=y == 0, stop=y == 2)
                    mm.then_inc(s_ready.sem, 1)

                def turns(n):
                    pe.wait_ge(norm_done.sem, s.nd + base + n + 1)
                    if n >= 2:
                        pe.wait_ge(pt_copied.sem, s.pc + base + n - 1)
                    else:
                        pe.wait_ge(out_read.sem, s.out0 + 2 * KT * g)
                    for kb in range(2):
                        for qt in range(2):
                            mm = nc.tensor.transpose(bank[2 + n % 2][:, kb * SEQ + qt * P:kb * SEQ + (qt + 1) * P],
                                                     p2[:, n % 2, qt, kb * P:(kb + 1) * P], ident)
                    mm.then_inc(pt_ready.sem, 1)

                def outputs(n):
                    x, b = divmod(n, BATCH)
                    pe.wait_ge(pt_copied.sem, s.pc + base + n + 1)
                    if b == 0:
                        pe.wait_ge(v_copied.sem, s.vc + 2 * (GRP2 * g + x) + 2)
                    if n >= 2:
                        pe.wait_ge(o_lo_done.sem, s.ol + base + n - 1)
                    for kb in range(2):
                        mm = nc.tensor.matmul(bank[4 + n % 2][:, 0:SEQ], val2[:, x % 2, 2 * b + kb, :],
                                              pt2[:, n % 2, kb, :], start=kb == 0, stop=kb == 1)
                    mm.then_inc(pv_done.sem, 1)

                values_of(0)
                scores(0)
                scores(1)
                for n in range(GSTEPS):
                    if n + 2 < GSTEPS:
                        if (n + 2) % BATCH == 0:
                            values_of((n + 2) // BATCH)
                        scores(n + 2)
                    turns(n)
                    if n >= 1:
                        outputs(n - 1)
                outputs(GSTEPS - 1)
                pe.wait_ge(o_lo_done.sem, s.ol + base + GSTEPS)
                for m in range(KT):
                    if m >= 2:
                        pe.wait_ge(out_read.sem, s.out0 + 2 * KT * g + 2 * (m - 1))
                    pe_chunk(pe, s, 8 * g + 4 + m, m, [P] * GRP2,
                             lambda k, half: (o2_hi[:, k, at(half)], o2_lo[:, k, at(half)]), acc[m % 2])

            loop(pe, s.groups, body)
            barrier(pe)

        def act_att2(act, s):
            def body(g):
                base = GSTEPS * g

                def split_w(x):
                    if x < 4:
                        act.wait_ge(used.sem, s.used0 + 4 * g)
                    else:
                        act.wait_ge(v_ready.sem, s.vr + 2 * (GRP2 * g + x - 3))
                    act.wait_ge(loaded[x % 4].sem, s.load0[x % 4] + 32 * g + 16 * (x // 4 + 1))
                    nc.scalar.activation(w_hi[:, x % 4, :], nat[:, x % 4, :], ACT.Copy).then_inc(hi.sem, 1)

                def split_qk(x):
                    h = GRP2 * g + x
                    act.wait_ge(qk_scaled.sem, s.qs + 2 * h + 2)
                    if x >= 2:
                        act.wait_ge(s_ready.sem, s.sr + base + BATCH * (x - 1))
                    nc.scalar.activation(qk_hi[:, x % 2, :, :], qk_raw[:, :, :], ACT.Copy).then_inc(qk_hi_done.sem, 1)

                def copy_values(x):
                    h = GRP2 * g + x
                    for n in range(2):
                        act.wait_ge(v_ready.sem, s.vr + 2 * h + n + 1)
                        if x >= 2:
                            act.wait_ge(pv_done.sem, s.pv + base + BATCH * (x - 1))
                        nc.scalar.activation(val2[:, x % 2, 4 * n:4 * n + 4, :],
                                             bank[6 + n][:, :].rearrange("p (t d) -> p t d", d=P), ACT.Copy)\
                          .then_inc(v_copied.sem, 1)

                def high_part(n):
                    x, b = divmod(n, BATCH)
                    act.wait_ge(pv_done.sem, s.pv + base + n + 1)
                    if n == 0:
                        act.wait_ge(bias_in.sem, s.bv + g + 1)
                        act.wait_ge(used.sem, s.used0 + 4 * g)
                    nc.scalar.activation(o2_hi[:, x, b * SEQ:(b + 1) * SEQ], bank[4 + n % 2][:, 0:SEQ], ACT.Identity,
                                         bias=bv2[:, x:x + 1]).then_inc(o_hi_done.sem, 1)

                for x in range(GRP2):
                    split_w(x)
                split_qk(0)
                copy_values(0)
                for n in range(GSTEPS):
                    x, b = divmod(n, BATCH)
                    if b == 2 and x + 1 < GRP2:
                        split_qk(x + 1)
                    act.wait_ge(max_done.sem, s.mx + base + n + 1)
                    if n >= 2:
                        act.wait_ge(pt_ready.sem, s.pr + base + n - 1)
                    for qt in range(2):
                        ins = nc.scalar.activation(p2[:, n % 2, qt, :], bank[n % 2][:, qt * SEQ:(qt + 1) * SEQ], ACT.Exp,
                                                   bias=small2[:, n % 2, qt:qt + 1],
                                                   accum_out=small2[:, n % 2, 2 + qt:3 + qt])
                    ins.then_inc(exp_done.sem, 1)
                    if b == 2 and x + 1 < GRP2:
                        copy_values(x + 1)
                        split_w(4 + x)
                    if n >= 2:
                        high_part(n - 2)
                high_part(GSTEPS - 2)
                high_part(GSTEPS - 1)
                split_w(7)

            loop(act, s.groups, body)
            barrier(act)

        def dve_att2(dve, s):
            def body(g):
                base = GSTEPS * g

                def split_w(x):
                    dve.wait_ge(hi.sem, s.hi0 + 8 * g + x + 1)
                    nc.vector.tensor_tensor(w_lo[:, x % 4, :], nat[:, x % 4, :], w_hi[:, x % 4, :].bitcast(F32),
                                            ALU.subtract).then_inc(lo.sem, 1)

                def scale_qk(x):
                    h = GRP2 * g + x
                    dve.wait_ge(qk_in.sem, s.qi + 16 * h + 16)
                    for n, r in enumerate((rms_q, rms_k)):
                        nc.vector.tensor_tensor(qk_raw[:, n, :], qk_raw[:, n, :], r[:, :], ALU.mult)\
                          .then_inc(qk_scaled.sem, 1)

                def top(n):
                    dve.wait_ge(s_ready.sem, s.sr + base + n + 1)
                    nc.vector.tensor_reduce(small2[:, n % 2, 0:2], bank[n % 2][:, :].rearrange("p (q k) -> p q k", q=2),
                                            AX.X, ALU.max, negate=True).then_inc(max_done.sem, 1)

                def norm(n):
                    dve.wait_ge(exp_done.sem, s.ex + base + n + 1)
                    nc.vector.reciprocal(small2[:, n % 2, 4:6], small2[:, n % 2, 2:4]).then_inc(small.sem, 1)
                    dve.wait_ge(small.sem, s.sm + base + n + 1)
                    nc.vector.tensor_tensor(p2[:, n % 2, :, :], p2[:, n % 2, :, :], tail_bcast(small2[:, n % 2, 4:6], SEQ),
                                            ALU.mult).then_inc(norm_done.sem, 1)

                def copy(n):
                    dve.wait_ge(pt_ready.sem, s.pr + base + n + 1)
                    if n >= 2:
                        dve.wait_ge(pv_done.sem, s.pv + base + n - 1)
                    nc.vector.tensor_copy(pt2[:, n % 2, :, :], bank[2 + n % 2][:, :].rearrange("p (k q) -> p k q", k=2))\
                      .then_inc(pt_copied.sem, 1)

                def low_part(n):
                    x, b = divmod(n, BATCH)
                    dve.wait_ge(o_hi_done.sem, s.oh + base + n + 1)
                    v = slice(b * SEQ, (b + 1) * SEQ)
                    nc.vector.scalar_tensor_tensor(o2_lo[:, x, v], bank[4 + n % 2][:, 0:SEQ], bv2[:, x:x + 1],
                                                   o2_hi[:, x, v].bitcast(F32), ALU.add, ALU.subtract)\
                      .then_inc(o_lo_done.sem, 1)

                scale_qk(0)
                nc.vector.tensor_scalar(bv2[:, :], cols2[:, 2, bass.ds(GRP2 * g, GRP2)], 0.0, None, ALU.add)\
                  .then_inc(bias_in.sem, 1)
                dve.wait_ge(bias_in.sem, s.bv + g + 1)
                for x in range(GRP2):
                    split_w(x)
                top(0)
                for n in range(GSTEPS):
                    x, b = divmod(n, BATCH)
                    norm(n)
                    if b == 1 and x + 1 < GRP2:
                        scale_qk(x + 1)
                    if n + 1 < GSTEPS:
                        top(n + 1)
                    copy(n)
                    if b == 2 and x + 1 < GRP2:
                        split_w(4 + x)
                    if n >= 2:
                        low_part(n - 2)
                low_part(GSTEPS - 2)
                low_part(GSTEPS - 1)
                split_w(7)
                for m in range(KT):
                    for half in range(NH):
                        if half == 0:
                            dve.wait_ge(half0.sem, s.half00 + KT * g + m + 1)
                        else:
                            dve.wait_ge(used.sem, s.used0 + 4 * g + m + 1)
                        nc.vector.tensor_tensor(xT[:, m, at(half)], acc[m % 2][half][:, :], xT[:, m, at(half)], ALU.add)\
                          .then_inc(out_read.sem, 1)

            loop(dve, s.groups, body)
            barrier(dve)

        def pool_att2(pool, s):
            def body(g):
                def split_qk(x):
                    pool.wait_ge(qk_hi_done.sem, s.qh + GRP2 * g + x + 1)
                    nc.gpsimd.tensor_tensor(qk_lo[:, x % 2, :, :], qk_raw[:, :, :], qk_hi[:, x % 2, :, :].bitcast(F32),
                                            ALU.subtract).then_inc(qk_lo_done.sem, 1)

                for x in range(GRP2):
                    split_qk(x)

            loop(pool, s.groups, body)
            barrier(pool)

        def sp_adapters(sp):
            barrier(sp)
            with nc.allow_non_contiguous_dma(reason="small transposed adapters"):
                for r, name in ((0, "B1"), (32, "B3")):
                    sp.dma_start(b13[r:r + RANK, 0:F0], t[f"L2_ffn_lora_{name}"].rearrange("o r -> r o"))\
                      .then_inc(cst_in.sem, 16)
                sp.dma_start(b2[:, :], t["L2_ffn_lora_B2"].rearrange("o r -> r o")).then_inc(cst_in.sem, 16)
            cst_in.count += 48
            sp.wait_ge(cst_in.sem, cst_in.count)
            barrier(sp)

        def pool_adapters(pool):
            nc.gpsimd.memset(b13[:, :], 0.0)
            barrier(pool)
            barrier(pool)

        def idle(eng, n=1):
            for _ in range(n):
                barrier(eng)

        def rhs_xn(k, half, rows):
            return xn_hi[:, k, at(half)], xn_lo[:, k, at(half)]

        def rhs_out(k, half, rows):
            return at_hi[:, k, at(half)], at_lo[:, k, at(half)]

        def dest(x, c, b=None, factor=1.0):
            return lambda half: (x[:, c, at(half)], b, factor)

        def qkv0():
            found = []
            for x, name in ((at_q, "wq"), (at_k, "wk"), (at_v, "wv")):
                for c in range(QC):
                    found.append(rows_chunk(t[f"L0_attn_{name}"], c * P, tile=len(found), to=dest(x, c)))
            return found

        def qkv1():
            w = t["L1_attn_w_qkv"]
            found = []
            for c in range(QC):
                q = rows_chunk(w, 0, tile=c, to=dest(at_q, c, bias1[:, c:c + 1]))
                q["loads"] = [(slot(slice(kv * HD, (kv + 1) * HD), slice(0, D)),
                               w[(kv * QC + c) * HD:(kv * QC + c + 1) * HD, :]) for kv in range(KV1)]
                found.append(q)
            for n, x in enumerate((at_k, at_v)):
                found.append(rows_chunk(w, D + n * P, tile=QC + n, to=dest(x, 0, bias1[:, QC + n:QC + n + 1])))
            return found

        def qkv3():
            found = [rows_chunk(t["L3_attn_wq_w"], c * P, tile=c, to=dest(at_q, c, bias3[:, c:c + 1])) for c in range(QC)]
            for n, (x, name) in enumerate(((at_k, "wk"), (at_v, "wv"))):
                c = rows_chunk(t["L3_attn_wq_w"], 0, tile=QC + n, to=dest(x, 0, bias3[:, QC + n:QC + n + 1]))
                c["loads"] = [(slot(slice(r * HD, (r + 1) * HD), slice(0, D)), t[f"L3_attn_{name}_w"]) for r in range(DUP)]
                found.append(c)
            return found

        def wo(w, b=None, by_key_head=False):
            found = []
            for m in range(KT):
                c = rows_chunk(w, m * P, tile=m)
                if b is not None:
                    c["bias"] = b[:, QC + 2 + m:QC + 3 + m]
                if by_key_head:
                    src = w[m * P:(m + 1) * P, :].rearrange("p (v c d) -> p c v d", c=QC, d=HD)
                    c["loads"] = [(lambda j, n=n: nat[:, j, n * P:(n + 1) * P].rearrange("p (v d) -> p v d", d=HD),
                                   src[:, n, :, :]) for n in range(QC)]
                found.append(c)
            return found

        def adapters_in():
            c = rows_chunk(t["L2_ffn_w1"], 0, tile=0)
            c["loads"] = [(slot(slice(r, r + RANK), slice(0, D)), t[f"L2_ffn_lora_{n}"]) for r, n in ((0, "A1"), (32, "A3"))]
            c["to"] = lambda half: (low[0:48, at(half)], None, 1.0)
            return [c]

        def adapters_down():
            found = down_chunks(t["L2_ffn_lora_A2"], F0)
            for c in found:
                c["to"] = lambda half: (low[0:RANK, at(half)], None, LORA)
            return found

        start = plan_start()
        norms = []
        norms.append(plan_norm())
        tables_up = plan_tables([(0, "gate", GROUPS_UP, D, F0), (32, "up", GROUPS_UP, D, F0)])
        up0 = plan_up(F0, "dequant", PACK, t["L0_ffn_gate_qweight"], t["L0_ffn_up_qweight"], (h0_hi, h0_lo), sgf0)
        tables_down = plan_tables([(0, "down", GROUPS_DOWN, F0, D)])
        down0 = plan_proj(packed_down_chunks(t["L0_ffn_down_qweight"], F0), "dequant", KT, h_of((h0_hi, h0_lo)), "dve")
        in0 = plan_proj(qkv0(), "turn", 3 * QC, rhs_xn, "act")
        prep0 = plan_prep((C_COS0, C_SIN0, C_ROT0), QC, QC)
        att0 = plan_att(QC, QC)
        wo0 = plan_proj(wo(t["L0_attn_wo"]), "turn", KT, rhs_out, "dve")

        norms.append(plan_norm())
        up1 = plan_up(F0, "turn", 1, t["L1_ffn_W_gate"], t["L1_ffn_W_up"], (h1_hi, h1_lo), sgf1)
        down1 = plan_proj(down_chunks(t["L1_ffn_W_down"], F0), "turn", KT, h_of((h1_hi, h1_lo)), "dve")
        in1 = plan_proj(qkv1(), "turn", QC + 2, rhs_xn, "act")
        prep1 = plan_prep((C_COS1, C_SIN1, C_ROT1), 1, 1)
        att1 = plan_att(1, 1)
        wo1 = plan_proj(wo(t["L1_attn_w_o"], bias1, True), "turn", KT, rhs_out, "dve")

        norms.append(plan_norm())
        low_in = plan_proj(adapters_in(), "turn", 1, rhs_xn, "act")
        up2 = plan_up(F0, "turn", 1, t["L2_ffn_w1"], t["L2_ffn_w3"], (h2_hi, h2_lo), sgf2, adapters=True)
        low_down = plan_proj(adapters_down(), "turn", 1, h_of((h2_hi, h2_lo)), "act")
        down2 = plan_proj(down_chunks(t["L2_ffn_w2"], F0, more=lambda m: lambda half: (
            b2[:, m * P:(m + 1) * P], low[0:RANK, at(half)])), "turn", KT, h_of((h2_hi, h2_lo)), "dve")
        qk2 = plan_qk2()
        rms2 = plan_rms()
        att2 = plan_att2()

        norms.append(plan_norm())
        up3 = plan_up(F3, "scaled", 1, t["L3_ffn_w1"], t["L3_ffn_w3"], (h3_hi, h3_lo), sgf3, scales=wscale)
        down3 = plan_proj(down_chunks(t["L3_ffn_w2"], F3, scales=wscale2), "scaled", KT, h_of((h3_hi, h3_lo)), "dve")
        in3 = plan_proj(qkv3(), "turn", QC + 2, rhs_xn, "act")
        prep3 = plan_prep(None, 1, 1)
        att3 = plan_att(1, 1)
        wo3 = plan_proj(wo(t["L3_attn_wo_w"], bias3), "turn", KT, rhs_out, "dve")
        end = plan_end()

        block = ctx.enter_context(nc.Block())

        @block.sync
        def _(sp):
            sp_start(sp)
            idle(sp)
            sp_tables(sp, tables_up)
            sp_up(sp, up0)
            sp_tables(sp, tables_down)
            sp_proj(sp, down0)
            sp_proj(sp, in0)
            idle(sp, 2)
            sp_proj(sp, wo0)
            idle(sp)
            sp_up(sp, up1)
            sp_proj(sp, down1)
            sp_proj(sp, in1)
            idle(sp, 2)
            sp_proj(sp, wo1)
            idle(sp)
            sp_adapters(sp)
            sp_proj(sp, low_in)
            sp_up(sp, up2)
            sp_proj(sp, low_down)
            sp_proj(sp, down2)
            idle(sp)
            sp_qk2(sp, qk2)
            idle(sp)
            sp_att2(sp, att2)
            idle(sp)
            sp_up(sp, up3)
            sp_proj(sp, down3)
            sp_proj(sp, in3)
            idle(sp, 2)
            sp_proj(sp, wo3)
            sp_end(sp, end)

        @block.tensor
        def _(pe):
            pe_start(pe, start)
            pe_norm(pe, norms[0])
            idle(pe, 2)
            pe_up(pe, up0)
            idle(pe, 2)
            pe_proj(pe, down0)
            pe_proj(pe, in0)
            pe_prep(pe, prep0)
            pe_att(pe, att0)
            pe_proj(pe, wo0)
            pe_norm(pe, norms[1])
            pe_up(pe, up1)
            pe_proj(pe, down1)
            pe_proj(pe, in1)
            pe_prep(pe, prep1)
            pe_att(pe, att1)
            pe_proj(pe, wo1)
            pe_norm(pe, norms[2])
            idle(pe, 2)
            pe_proj(pe, low_in)
            pe_up(pe, up2)
            pe_proj(pe, low_down)
            pe_proj(pe, down2)
            pe_qk2(pe, qk2)
            pe_rms(pe, rms2)
            pe_att2(pe, att2)
            pe_norm(pe, norms[3])
            pe_up(pe, up3)
            pe_proj(pe, down3)
            pe_proj(pe, in3)
            pe_prep(pe, prep3)
            pe_att(pe, att3)
            pe_proj(pe, wo3)
            pe_end(pe, end)

        @block.scalar
        def _(act):
            act_start(act)
            act_norm(act, norms[0])
            idle(act, 2)
            act_up(act, up0)
            idle(act, 2)
            act_proj(act, down0)
            act_proj(act, in0)
            idle(act)
            act_att(act, att0)
            act_proj(act, wo0)
            act_norm(act, norms[1])
            act_up(act, up1)
            act_proj(act, down1)
            act_proj(act, in1)
            idle(act)
            act_att(act, att1)
            act_proj(act, wo1)
            act_norm(act, norms[2])
            idle(act, 2)
            act_proj(act, low_in)
            act_up(act, up2)
            act_proj(act, low_down)
            act_proj(act, down2)
            act_qk2(act, qk2)
            act_rms(act, rms2)
            act_att2(act, att2)
            act_norm(act, norms[3])
            act_up(act, up3)
            act_proj(act, down3)
            act_proj(act, in3)
            idle(act)
            act_att(act, att3)
            act_proj(act, wo3)
            idle(act)

        @block.vector
        def _(dve):
            dve_start(dve, start)
            dve_norm(dve, norms[0])
            dve_tables(dve, tables_up)
            dve_up(dve, up0)
            dve_tables(dve, tables_down)
            dve_proj(dve, down0)
            dve_proj(dve, in0)
            dve_prep(dve, prep0)
            dve_att(dve, att0)
            dve_proj(dve, wo0)
            dve_norm(dve, norms[1])
            dve_up(dve, up1)
            dve_proj(dve, down1)
            dve_proj(dve, in1)
            dve_prep(dve, prep1)
            dve_att(dve, att1)
            dve_proj(dve, wo1)
            dve_norm(dve, norms[2])
            idle(dve, 2)
            dve_proj(dve, low_in)
            dve_up(dve, up2)
            dve_proj(dve, low_down)
            dve_proj(dve, down2)
            dve_qk2(dve, qk2)
            dve_rms(dve, rms2)
            dve_att2(dve, att2)
            dve_norm(dve, norms[3])
            dve_up(dve, up3)
            dve_proj(dve, down3)
            dve_proj(dve, in3)
            dve_prep(dve, prep3)
            dve_att(dve, att3)
            dve_proj(dve, wo3)
            dve_end(dve, end)

        @block.gpsimd
        def _(pool):
            idle(pool, 2)
            pool_norm(pool, norms[0])
            idle(pool, 2)
            pool_up(pool, up0)
            idle(pool, 2)
            pool_proj(pool, down0)
            pool_proj(pool, in0)
            pool_prep(pool, prep0)
            pool_att(pool, att0)
            pool_proj(pool, wo0)
            pool_norm(pool, norms[1])
            pool_up(pool, up1)
            pool_proj(pool, down1)
            pool_proj(pool, in1)
            pool_prep(pool, prep1)
            pool_att(pool, att1)
            pool_proj(pool, wo1)
            pool_norm(pool, norms[2])
            pool_adapters(pool)
            pool_proj(pool, low_in)
            pool_up(pool, up2)
            pool_proj(pool, low_down)
            pool_proj(pool, down2)
            pool_qk2(pool, qk2)
            idle(pool)
            pool_att2(pool, att2)
            pool_norm(pool, norms[3])
            pool_up(pool, up3)
            pool_proj(pool, down3)
            pool_proj(pool, in3)
            pool_prep(pool, prep3)
            pool_att(pool, att3)
            pool_proj(pool, wo3)
            idle(pool)


def kernel(**inputs):
    import concourse.bacc as bacc
    from concourse.bass_utils import run_bass_kernel_spmd

    nc = bacc.Bacc("TRN2", target_bir_lowering=False, num_devices=1)
    arrays, t = {}, {}
    cst, shift = constants()
    for name, a in (*inputs.items(), ("cst", cst), ("shift", shift)):
        arrays[f"in_{name}"] = a = np.ascontiguousarray(a)
        t[name] = nc.dram_tensor(f"in_{name}", a.shape, mybir.dt.from_np(a.dtype), kind="ExternalInput").ap()
    out = nc.dram_tensor("out", (BATCH, SEQ, D), F32, kind="ExternalOutput").ap()
    build(nc, t, out)
    return run_bass_kernel_spmd(nc, [arrays], core_ids=[0]).results[0]["out"]
```

```python
from contextlib import ExitStack

import numpy as np

import concourse.bass as bass
from concourse import mybir

P = 128
BATCH, SEQ, D = 4, 256, 512
TOK = BATCH * SEQ
HALF = 512
NH = TOK // HALF
KT = D // P
SLOTS = 4

HEADS, HD = 32, 16
HPC = P // HD
QC = HEADS // HPC
VW = HD + 1
KV1 = 8
PACK = 8
F0 = 1376
F3 = 1792
GROUPS_UP, GROUPS_DOWN = 4, 10
H2, HD2 = 32, 128
INNER2 = H2 * HD2
GRP2 = 4
LORA = 2.0
RANK = 16
LEAD = 3
LEAD_SCALE = 5
LEAD_LOAD = 6
LN_EPS, RMS_EPS = 1e-5, 1e-6
MASKED = -1e30

F32 = mybir.dt.float32
F32R = mybir.dt.float32r
BF16 = mybir.dt.bfloat16
I32 = mybir.dt.int32
ALU = mybir.AluOpType
ACT = mybir.ActivationFunctionType
AX = mybir.AxisListType

C_ID, C_MEAN, C_MEAN2, C_ROT0, C_ROT1 = 0, 128, 256, 384, 512
C_MASK, C_HEAD = 640, 768
C_COS0, C_SIN0, C_COS1, C_SIN1 = 776, 1032, 1288, 1544
C_IDX = 1800
C_WIDTH = 1802


def constants():
    c = np.zeros((P, C_WIDTH), np.float32)
    c[:, C_ID:C_ID + P] = np.eye(P)
    c[:, C_MEAN:C_MEAN + P] = 1.0 / D
    c[:, C_MEAN2:C_MEAN2 + P] = 1.0 / INNER2
    for p in range(P):
        h, d = p - p % HD, p % HD
        if d < HD // 2:
            c[h + d + HD // 2, C_ROT0 + p] = -1.0
        else:
            c[h + d - HD // 2, C_ROT0 + p] = 1.0
        if d % 2 == 0:
            c[p + 1, C_ROT1 + p] = -1.0
        else:
            c[p - 1, C_ROT1 + p] = 1.0
    c[:, C_MASK:C_MASK + P] = np.where(np.arange(P)[:, None] >= np.arange(P)[None], 0.0, MASKED)
    c[np.arange(P), C_HEAD + np.arange(P) // HD] = 1.0 / np.sqrt(np.float32(HD))
    freq = (1.0 / 10000.0 ** (np.arange(0, HD, 2, dtype=np.float32) / HD)).astype(np.float32)
    ang = np.outer(np.arange(SEQ, dtype=np.float32), freq).astype(np.float32)
    half = ang[:, np.arange(P) % (HD // 2)].T
    pair = ang[:, (np.arange(P) % HD) // 2].T
    c[:, C_COS0:C_COS0 + SEQ], c[:, C_SIN0:C_SIN0 + SEQ] = np.cos(half), np.sin(half)
    c[:, C_COS1:C_COS1 + SEQ], c[:, C_SIN1:C_SIN1 + SEQ] = np.cos(pair), np.sin(pair)
    c[:, C_IDX] = np.arange(P)
    shift = np.zeros((P, 1), np.int32)
    shift[:, 0] = (np.arange(P) % PACK) * (32 // PACK)
    return c, shift


class Signal:

    def __init__(self, sem):
        self.sem = sem
        self.count = 1

    def reserve(self, n):
        base = self.count
        self.count += n
        return base




class Stage:

    norm = None


def build(nc, t, out):
    ctx = ExitStack()
    with ctx:
        def sb(name, shape, dt=F32):
            return ctx.enter_context(nc.sbuf_tensor(name, shape, dt))

        signals = []

        def sig(name):
            signals.append(Signal(ctx.enter_context(nc.semaphore(name))))
            return signals[-1]

        cst = sb("cst", [P, C_WIDTH])
        shift = sb("shift", [P, 1], I32)
        ident = cst[:, C_ID:C_ID + P]
        ident16 = sb("ident16", [P, P], BF16)
        mask16 = sb("mask16", [P, P], BF16)
        eps = sb("eps", [P, 2])
        bias1 = sb("bias1", [P, QC + 2 + KT])
        bias3 = sb("bias3", [P, QC + 2 + KT])
        cols2 = sb("cols2", [P, 5, H2])
        bo2 = sb("bo2", [P, KT])
        b2s = sb("b2s", [P, SLOTS])
        wscale = sb("wscale", [P, 2, F3 // P, KT])
        wscale2 = sb("wscale2", [P, KT, F3 // P])
        xT = sb("xT", [P, KT, TOK])
        xn_hi = sb("xn_hi", [P, KT, TOK], F32R)
        xn_lo = sb("xn_lo", [P, KT, TOK], F32R)
        nat = sb("nat", [P, SLOTS, D])
        w_hi = sb("w_hi", [P, SLOTS, D], F32R)
        w_lo = sb("w_lo", [P, SLOTS, D], F32R)
        arena_at = nc.sbuf_base

        def arena(*tensors):
            with ExitStack() as own:
                made = [own.enter_context(nc.sbuf_tensor(n, s, *(dt or [F32]))) for n, s, *dt in tensors]
            assert nc.sbuf_base == arena_at
            return made

        F11, F14 = -(-F0 // P), F3 // P
        x_nat, = arena(("x_nat", [P, TOK // P, D]))
        cen, sq, inv = arena(("cen", [P, KT, TOK]), ("sq", [P, KT, TOK]), ("inv", [P, TOK]))
        ROWS_DOWN = slice(64, 64 + GROUPS_DOWN)
        h0_hi, h0_lo, sgf0, hot, hot_d, packed, zero, scale, deq = arena(
            ("h0_hi", [P, F11, TOK], F32R), ("h0_lo", [P, F11, TOK], F32R), ("sgf0", [P, 2, NH, HALF]),
            ("hot", [P, F0]), ("hot_d", [P, F0]), ("packed", [P, F0 // PACK], I32),
            ("zero", [P, F0]), ("scale", [P, F0]), ("deq", [P, 2, D]))
        h1_hi, h1_lo, sgf1 = arena(
            ("h1_hi", [P, F11, TOK], F32R), ("h1_lo", [P, F11, TOK], F32R), ("sgf1", [P, 2, NH, HALF]))
        h2_hi, h2_lo, sgf2, b13s, low, _, b13, b2 = arena(
            ("h2_hi", [P, F11, TOK], F32R), ("h2_lo", [P, F11, TOK], F32R), ("sgf2", [P, 2, NH, HALF]),
            ("b13s", [48, SLOTS, P]), ("low", [48, TOK]), ("pad2", [P, 3 * TOK]), ("b13", [48, F11 * P]), ("b2", [RANK, D]))
        h3_hi, h3_lo, sgf3 = arena(
            ("h3_hi", [P, F14, TOK], F32R), ("h3_lo", [P, F14, TOK], F32R), ("sgf3", [P, 2, NH, HALF]))
        at_q, at_k, at_v, at_val, at_km, at_qs, at_p, at_pt, at_on, at_lo, at_small = arena(
            ("at_q", [P, QC, TOK]), ("at_k", [P, QC, TOK]), ("at_v", [P, QC, TOK]),
            ("at_val", [P, TOK // P, QC, HPC, VW]), ("at_km", [P, 2, HPC, SEQ]), ("at_qs", [P, QC, SEQ]),
            ("at_p", [P, 3, 512]), ("at_pt", [P, 2, 512]), ("at_on", [P, 2, 2, P]),
            ("at_lo", [P, QC, TOK], F32R), ("at_small", [P, 64]))
        at_q2, at_k2, at_hi = arena(
            ("at_q2", [P, QC, TOK]), ("at_k2", [P, QC, TOK]), ("at_hi", [P, QC, TOK], F32R))
        rms, ssq, raw2, sq2 = arena(
            ("rms", [P, 2, TOK]), ("ssq", [P, 2, TOK]), ("raw2", [P, SLOTS, TOK]), ("sq2", [P, SLOTS, TOK]))
        (rms_, qk_raw, qk_hi, qk_lo, val2, p2, pt2, bv2, o2_hi, o2_lo, wo_nat, wo_hi, wo_lo, small2) = arena(
            ("rms_", [P, 2, TOK]), ("qk_raw", [P, 2, 2, HALF]),
            ("qk_hi", [P, 2, 2, HALF], F32R), ("qk_lo", [P, 2, 2, HALF], F32R),
            ("val2", [P, NH, HALF // P, GRP2 * HD2]), ("p2", [P, 4, 2, SEQ]), ("pt2", [P, 2, 2, SEQ]),
            ("bv2", [P, GRP2]), ("o2_hi", [P, NH, GRP2, HALF], F32R), ("o2_lo", [P, NH, GRP2, HALF], F32R),
            ("wo_nat", [P, KT, GRP2 * P]), ("wo_hi", [P, KT, GRP2 * P], F32R), ("wo_lo", [P, KT, GRP2 * P], F32R),
            ("small2", [P, 4, 8]))
        bank = [ctx.enter_context(nc.psum_tensor(f"bank{i}", [P, 512], F32)) for i in range(8)]
        turn_bank = [bank[0], bank[1]]
        acc = [[bank[2], bank[3]], [bank[4], bank[5]]]
        qk_dram = nc.dram_tensor("qk_scratch", (H2, 2, P, TOK), F32).ap()

        phase = ctx.enter_context(nc.semaphore("phase"))
        begun = ctx.enter_context(nc.semaphore("begun"))
        x_in = sig("x_in")
        cst_in = sig("cst_in")
        tables_in = sig("tables_in")
        cols_in = sig("cols_in")
        adapters_in = sig("adapters_in")
        cleared = sig("cleared")
        loaded = [sig(f"loaded{j}") for j in range(SLOTS)]
        scaled = sig("scaled")
        turned = sig("turned")
        unpacked = sig("unpacked")
        centred = sig("centred")
        dequant = sig("dequant")
        hi = sig("hi")
        lo = sig("lo")
        half0 = sig("half0")
        used = sig("used")
        gate_read = sig("gate_read")
        up_read = sig("up_read")
        h_hi_done = sig("h_hi_done")
        h_lo_done = sig("h_lo_done")
        out_read = sig("out_read")
        step_a = sig("step_a")
        step_b = sig("step_b")
        step_c = sig("step_c")
        step_d = sig("step_d")
        step_e = sig("step_e")
        io = sig("io")
        s_ready = sig("s_ready")
        max_done = sig("max_done")
        exp_done = sig("exp_done")
        pt_ready = sig("pt_ready")
        pt_copied = sig("pt_copied")
        pv_done = sig("pv_done")
        o_normed = sig("o_normed")
        ot_ready = sig("ot_ready")
        ot_hi = sig("ot_hi")
        ot_lo = sig("ot_lo")
        km_made = sig("km_made")
        qs_made = sig("qs_made")
        stored = [sig(f"stored{j}") for j in range(SLOTS)]
        norm_done = sig("norm_done")
        xn_done = [sig("xn0_done"), sig("xn1_done")]
        v_ready = sig("v_ready")
        v_copied = sig("v_copied")
        small = sig("small")
        sq_done = sig("sq_done")
        raw_done = [sig("raw_q_done"), sig("raw_k_done")]
        ssq_done = sig("ssq_done")
        qk_in = [sig(f"qk_in{j}") for j in range(2)]
        v_half = sig("v_half")
        wo_in = [sig(f"wo_in{j}") for j in range(KT)]
        wo_hi_done = sig("wo_hi_done")
        wo_lo_done = sig("wo_lo_done")
        wo_done = sig("wo_done")
        qk_scaled = sig("qk_scaled")
        qk_hi_done = sig("qk_hi_done")
        qk_lo_done = sig("qk_lo_done")
        bias_in = sig("bias_in")
        o_hi_done = sig("o_hi_done")
        o_lo_done = sig("o_lo_done")

        def loop(eng, n, body):
            if n > 2:
                with eng.Fori(0, n) as it:
                    body(it)
            else:
                for it in range(n):
                    body(it)

        STAGES = ["start", "up0", "down0", "in0", "prep0", "att0", "wo0",
                  "up1", "down1", "in1", "prep1", "att1", "wo1",
                  "low_in", "up2", "low_down", "down2", "qk2", "rms2", "att2",
                  "up3", "down3", "in3", "prep3", "att3", "wo3", "end"]

        def barrier(eng, stage):
            eng.drain().then_inc(phase, 1)
            eng.wait_ge(phase, 4 * (STAGES.index(stage) + 1))

        def join(sp, stage):
            sp.wait_ge(phase, 4 * (STAGES.index(stage) + 1))

        def bcast(ap, n):
            return ap.unsqueeze(1).broadcast_to([ap.shape[0], n, ap.shape[1]])

        def tail_bcast(ap, n):
            return ap.unsqueeze(2).broadcast_to([ap.shape[0], ap.shape[1], n])

        def at(half):
            return slice(half * HALF, (half + 1) * HALF)

        def plan_chunks(n, mode, per_slot):
            s = Stage()
            s.n, s.mode = n, mode
            s.lo0, s.hi0, s.used0 = lo.reserve(n), hi.reserve(n), used.reserve(n)
            s.turned0 = turned.reserve(n if mode != "direct" else 0)
            s.scaled0 = scaled.reserve(n if mode == "scaled" else 0)
            m = n if mode == "dequant" else 0
            s.un0, s.cen0, s.deq0 = unpacked.reserve(m), centred.reserve(m), dequant.reserve(m)
            dmas = per_slot if isinstance(per_slot, list) else [per_slot] * n
            s.dmas = dmas
            s.load0 = [loaded[j].reserve(16 * sum(dmas[j::SLOTS])) for j in range(SLOTS)]
            return s

        def loaded_count(s, i, j):
            if isinstance(i, int):
                return s.load0[j] + 16 * sum(s.dmas[j:i + 1:SLOTS])
            return s.load0[j] + 4 * s.dmas[j] * (i - j) + 16 * s.dmas[j]

        def before(i, n):
            return max(i - n + 1, 0) if isinstance(i, int) else i - n + 1

        def sp_slot(sp, s, i):
            if isinstance(i, int) and i < SLOTS or s.mode == "direct":
                sp.wait_ge(lo.sem, s.lo0 + before(i, SLOTS))
            elif s.mode == "dequant":
                sp.wait_ge(centred.sem, s.cen0 + before(i, SLOTS))
            else:
                sp.wait_ge(turned.sem, s.turned0 + before(i, SLOTS))

        def pool_scale(pool, s, i, j, w, factors):
            pool.wait_ge(loaded[j].sem, loaded_count(s, i, j))
            v = nat[:, j, 0:w].rearrange("p (k c) -> p k c", c=P)
            nc.gpsimd.tensor_tensor(v, v, tail_bcast(factors, P), ALU.mult).then_inc(scaled.sem, 1)

        def pe_turn(pe, s, i, j, views):
            if s.mode == "scaled":
                pe.wait_ge(scaled.sem, s.scaled0 + i + 1)
            else:
                pe.wait_ge(loaded[j].sem, loaded_count(s, i, j))
            pe.wait_ge(lo.sem, s.lo0 + before(i, 2))
            for k, v in enumerate(views):
                rows, width = v.shape[0], v.free_size()
                mm = nc.tensor.transpose(turn_bank[j % 2][0:width, k * P:k * P + rows], v, ident[0:rows, 0:rows])
            mm.then_inc(turned.sem, 1)

        def pe_spread(pe, s, i, j, g, hots, first, kts, cols):
            pe.wait_ge(dequant.sem, s.deq0 + before(i, 2))
            for k, (kt, rows) in enumerate(kts):
                for b, table in ((turn_bank[j % 2], zero), (bank[6 + j % 2], scale)):
                    n = cols.stop - cols.start if isinstance(cols, slice) else P
                    mm = nc.tensor.matmul(b[0:rows, k * P:k * P + n], hots[g, first + kt * P:first + kt * P + rows],
                                          table[g, cols], start=True, stop=True)
            mm.then_inc(turned.sem, 1)

        def dve_dequant(dve, s, i, j, parts):
            dve.wait_ge(loaded[j].sem, loaded_count(s, i, j))
            for n, (r, c) in enumerate(parts):
                v = nat[r, j, c].bitcast(I32)
                ins = nc.vector.tensor_scalar(v, v, shift[r, 0:1], 15, ALU.logical_shift_right, ALU.bitwise_and)
            ins.then_inc(unpacked.sem, 1)
            dve.wait_ge(unpacked.sem, s.un0 + i + 1)
            dve.wait_ge(turned.sem, s.turned0 + i + 1)
            dve.wait_ge(lo.sem, s.lo0 + before(i, 2))
            for r, c in parts:
                ins = nc.vector.tensor_tensor(deq[r, j % 2, c], nat[r, j, c].bitcast(I32),
                                              turn_bank[j % 2][r, c], ALU.subtract)
            ins.then_inc(centred.sem, 1)
            dve.wait_ge(centred.sem, s.cen0 + i + 1)
            for r, c in parts:
                ins = nc.vector.tensor_tensor(deq[r, j % 2, c], deq[r, j % 2, c],
                                              bank[6 + j % 2][r, c], ALU.mult)
            ins.then_inc(dequant.sem, 1)

        def chunk_source(s, j):
            if s.mode == "direct":
                return nat[:, j, :]
            if s.mode == "dequant":
                return deq[:, j % 2, :]
            return turn_bank[j % 2]

        def act_hi(act, s, i, j, parts):
            if s.mode == "direct":
                act.wait_ge(loaded[j].sem, loaded_count(s, i, j))
                act.wait_ge(used.sem, s.used0 + before(i, SLOTS))
            elif s.mode == "dequant":
                act.wait_ge(dequant.sem, s.deq0 + i + 1)
            else:
                act.wait_ge(turned.sem, s.turned0 + i + 1)
            src = chunk_source(s, j)
            for r, c in parts:
                ins = nc.scalar.activation(w_hi[r, j, c], src[r, c], ACT.Copy)
            ins.then_inc(hi.sem, 1)

        def dve_lo(dve, s, i, j, parts):
            dve.wait_ge(hi.sem, s.hi0 + i + 1)
            src = chunk_source(s, j)
            for r, c in parts:
                ins = nc.vector.tensor_tensor(w_lo[r, j, c], src[r, c], w_hi[r, j, c].bitcast(F32), ALU.subtract)
            ins.then_inc(lo.sem, 1)

        def pe_chunk(pe, s, i, j, rows, rhs, to, first=True, last=True, more=None, norm=None):
            pe.wait_ge(lo.sem, s.lo0 + i + 1)
            for half in range(NH):
                for k, n in enumerate(rows):
                    if norm is not None:
                        pe.wait_ge(xn_done[half].sem, norm.xn0[half] + k + 1)
                    r_hi, r_lo = rhs(k, half)
                    for x, (w, r) in enumerate(((w_hi, r_hi), (w_hi, r_lo), (w_lo, r_hi))):
                        mm = nc.tensor.matmul(to[half][:, :], w[0:n, j, k * P:(k + 1) * P], r,
                                              start=first and k == 0 and x == 0,
                                              stop=last and more is None and k == len(rows) - 1 and x == 2)
                if more is not None:
                    mm = nc.tensor.matmul(to[half][:, :], *more(half), start=False, stop=True)
                if last and half == 0:
                    mm.then_inc(half0.sem, 1)
            mm.then_inc(used.sem, 1)

        ALL = [(slice(0, P), slice(0, D))]

        def whole(nkt, last_rows=P):
            if last_rows == P:
                return [(slice(0, P), slice(0, nkt * P))]
            return [(slice(0, P), slice(0, (nkt - 1) * P)), (slice(0, last_rows), slice((nkt - 1) * P, nkt * P))]

        def xn(k, half):
            return xn_hi[:, k, at(half)], xn_lo[:, k, at(half)]

        x_rows = t["L0_attn_x"].rearrange("b s d -> (b s) d").rearrange("(n p) d -> p n d", p=P)
        out_rows = out.rearrange("b s d -> (b s) d").rearrange("(n p) d -> p n d", p=P)
        DUP = P // HD

        def sp_start(sp):
            def get(into, dst, src):
                sp.dma_start(dst, src, allow_slow_non_contiguous=True).then_inc(into.sem, 16)
                into.count += 16

            get(cst_in, cst[:, :], t["cst"])
            get(cst_in, shift[:, :], t["shift"])
            sp.wait_ge(cleared.sem, 2)
            for tables in (tables_up, tables_down):
                for g, name, _, _, n_in, width in tables.which:
                    get(tables_in, zero[g, 0:n_in].bitcast(I32), t[f"L0_ffn_{name}_g_idx"].rearrange("(o k) -> o k", o=1)
                        .broadcast_to([g.stop - g.start, n_in]))
                    get(tables_in, packed[g, 0:width // PACK], t[f"L0_ffn_{name}_qzeros"])
                    get(tables_in, scale[g, 0:width], t[f"L0_ffn_{name}_scales"])
            get(x_in, x_nat[:, :, :], x_rows)

        def sp_columns(sp):
            def get(dst, src):
                sp.dma_start(dst, src, allow_slow_non_contiguous=True).then_inc(cols_in.sem, 16)
                cols_in.count += 16

            b = t["L1_attn_b_qkv"]
            for kv in range(KV1):
                rows = slice(kv * HD, (kv + 1) * HD)
                get(bias1[rows, 0:QC], b[kv * QC * HD:(kv + 1) * QC * HD].rearrange("(c d) -> d c", d=HD))
            for n in range(2):
                get(bias1[:, QC + n:QC + n + 1], b[D + n * P:D + (n + 1) * P].rearrange("(d o) -> d o", o=1))
            get(bias1[:, QC + 2:], t["L1_attn_b_o"].rearrange("(c d) -> d c", d=P))
            get(bias3[:, 0:QC], t["L3_attn_wq_b"].rearrange("(c d) -> d c", d=P))
            for n, name in enumerate(("wk", "wv")):
                for r in range(DUP):
                    get(bias3[r * HD:(r + 1) * HD, QC + n:QC + n + 1],
                        t[f"L3_attn_{name}_b"].rearrange("(d o) -> d o", o=1))
            get(bias3[:, QC + 2:], t["L3_attn_wo_b"].rearrange("(c d) -> d c", d=P))
            for n, name in enumerate(("bq", "bk", "bv", "gq", "gk")):
                get(cols2[:, n, :], t[f"L2_attn_{name}"].rearrange("(h d) -> d h", d=P))
            get(bo2[:, :], t["L2_attn_bo"].rearrange("(c d) -> d c", d=P))
            for n, name in enumerate(("w1", "w3")):
                get(wscale[:, n, :, :], t[f"L3_ffn_{name}_scale"].rearrange("(o n) k -> o n k", o=1)
                    .broadcast_to([P, F14, KT]))
            get(wscale2[:, :, :], t["L3_ffn_w2_scale"].rearrange("(o n) k -> o n k", o=1)
                .broadcast_to([P, KT, F14]))

        def pe_start(pe, s):
            pe.wait_ge(cst_in.sem, cst_in.count)
            pe.wait_ge(x_in.sem, x_in.count)
            for half in range(NH):
                for k in range(KT):
                    n = KT * half + k
                    if n >= 2:
                        pe.wait_ge(out_read.sem, s.out0 + n - 1)
                    for j in range(4):
                        mm = nc.tensor.transpose(turn_bank[n % 2][:, j * P:(j + 1) * P],
                                                 x_nat[:, 4 * half + j, k * P:(k + 1) * P], ident)
                    mm.then_inc(step_a.sem, 1)

        def dve_start(dve):
            nc.vector.memset(eps[:, 0:1], LN_EPS)
            nc.vector.memset(eps[:, 1:2], RMS_EPS)
            for x in (hot, zero, scale):
                ins = nc.vector.memset(x[:, :], 0.0)
            ins.then_inc(cleared.sem, 1)
            dve.wait_ge(cst_in.sem, cst_in.count)
            dve.wait_ge(tables_in.sem, tables_in.count)
            dve_tables(dve, tables_up)
            dve_tables(dve, tables_down)

        def act_start(act, s):
            act.wait_ge(cst_in.sem, cst_in.count)
            nc.scalar.activation(ident16[:, :], ident, ACT.Copy)
            nc.scalar.activation(mask16[:, :], cst[:, C_MASK:C_MASK + P], ACT.Copy)
            for half in range(NH):
                for k in range(KT):
                    n = KT * half + k
                    act.wait_ge(step_a.sem, s.a0 + n + 1)
                    nc.scalar.activation(xT[:, k, at(half)], turn_bank[n % 2][:, :], ACT.Copy).then_inc(out_read.sem, 1)

        def plan_start():
            s = Stage()
            s.out0, s.a0 = out_read.reserve(KT * NH), step_a.reserve(KT * NH)
            return s

        def pe_end(pe, s):
            for n in range(TOK // P):
                if n >= 2:
                    pe.wait_ge(out_read.sem, s.out0 + n - 1)
                for k in range(KT):
                    mm = nc.tensor.transpose(turn_bank[n % 2][:, k * P:(k + 1) * P],
                                             xT[:, k, n * P:(n + 1) * P], ident)
                mm.then_inc(step_a.sem, 1)

        def dve_end(dve, s):
            for n in range(TOK // P):
                dve.wait_ge(step_a.sem, s.a0 + n + 1)
                nc.vector.tensor_copy(x_nat[:, n, :], turn_bank[n % 2][:, :]).then_inc(out_read.sem, 1)

        def sp_end(sp, s):
            for n in range(TOK // P):
                sp.wait_ge(out_read.sem, s.out0 + n + 1)
                sp.dma_start(out_rows[:, n, :], x_nat[:, n, :]).then_inc(io.sem, 16)
            sp.wait_ge(io.sem, io.count + 16 * (TOK // P))

        def plan_end():
            s = Stage()
            s.out0, s.a0 = out_read.reserve(TOK // P), step_a.reserve(TOK // P)
            return s

        def plan_norm():
            s = Stage()
            s.a0, s.b0, s.c0, s.d0, s.e0 = (x.reserve(n) for x, n in (
                (step_a, 2 * NH), (step_b, NH * KT), (step_c, NH * (KT + 1)), (step_d, NH * (KT + 1)), (step_e, NH * KT)))
            s.xn0 = [x.reserve(KT) for x in xn_done]
            return s

        TILES = [(half, k) for half in range(NH) for k in range(KT)]

        def pe_norm(pe, s):
            mean = cst[:, C_MEAN:C_MEAN + P]
            for half in range(NH):
                for k in range(KT):
                    mm = nc.tensor.matmul(acc[0][half][:, :], mean, xT[:, k, at(half)], start=k == 0, stop=k == KT - 1)
                mm.then_inc(step_a.sem, 1)
            for n, (half, k) in enumerate(TILES):
                pe.wait_ge(step_c.sem, s.c0 + n + 1)
                mm = nc.tensor.matmul(acc[1][half][:, :], mean, sq[:, k, at(half)], start=k == 0, stop=k == KT - 1)
                if k == KT - 1:
                    mm.then_inc(step_a.sem, 1)

        def dve_norm(dve, s):
            for half, k in TILES:
                dve.wait_ge(step_a.sem, s.a0 + half + 1)
                nc.vector.tensor_tensor(cen[:, k, at(half)], xT[:, k, at(half)], acc[0][half][:, :], ALU.subtract)\
                  .then_inc(step_b.sem, 1)
            for half in range(NH):
                dve.wait_ge(step_c.sem, s.c0 + NH * KT + half + 1)
                nc.vector.reciprocal(inv[:, at(half)], inv[:, at(half)]).then_inc(step_d.sem, 1)
                dve.wait_ge(step_d.sem, s.d0 + (KT + 1) * half + 1)
                for k in range(KT):
                    nc.vector.tensor_tensor(cen[:, k, at(half)], cen[:, k, at(half)], inv[:, at(half)], ALU.mult)\
                      .then_inc(step_d.sem, 1)
                if half == 0:
                    low_norm(dve, s, half)

        def low_norm(eng, s, half):
            for k in range(KT):
                eng.wait_ge(step_e.sem, s.e0 + KT * half + k + 1)
                (nc.vector, nc.gpsimd)[half].tensor_tensor(xn_lo[:, k, at(half)], cen[:, k, at(half)],
                                                           xn_hi[:, k, at(half)].bitcast(F32), ALU.subtract)\
                    .then_inc(xn_done[half].sem, 1)

        def act_norm(act, s):
            for n, (half, k) in enumerate(TILES):
                act.wait_ge(step_b.sem, s.b0 + n + 1)
                nc.scalar.activation(sq[:, k, at(half)], cen[:, k, at(half)], ACT.Square).then_inc(step_c.sem, 1)
            for half in range(NH):
                act.wait_ge(step_a.sem, s.a0 + NH + half + 1)
                nc.scalar.activation(inv[:, at(half)], acc[1][half][:, :], ACT.Sqrt, bias=eps[:, 0:1])\
                  .then_inc(step_c.sem, 1)
            for half, k in TILES:
                act.wait_ge(step_d.sem, s.d0 + (KT + 1) * half + k + 2)
                nc.scalar.activation(xn_hi[:, k, at(half)], cen[:, k, at(half)], ACT.Copy).then_inc(step_e.sem, 1)

        def pool_norm(pool, s):
            low_norm(pool, s, 1)

        def plan_up(width, mode, dmas, gate, up, h, sgf, spread=None, adapters=False, scales=None):
            nf = -(-width // P)
            s = plan_chunks(2 * nf, mode, dmas)
            s.nf, s.width, s.gate, s.up, s.h, s.sg, s.hf = nf, width, gate, up, h, sgf[:, 0], sgf[:, 1]
            s.spread, s.adapters, s.scales = spread, adapters, scales
            s.half00 = half0.reserve(2 * nf)
            s.gate0, s.up0 = gate_read.reserve(2 * nf), up_read.reserve(2 * nf)
            s.hhi0, s.hlo0 = h_hi_done.reserve(2 * nf), h_lo_done.reserve(2 * nf)
            s.small0 = small.reserve(2 * nf if adapters else 0)
            s.rounds, s.tail = nf // 2, nf % 2
            return s

        def up_rounds(eng, s, ahead, work, opening, lead=LEAD):
            def step(i, j, at_h, more):
                if more:
                    ahead(i + lead, (j + lead) % SLOTS, at_h + (j + lead) // 2)
                work(i, j, at_h + j // 2)

            def body(it):
                for j in range(SLOTS):
                    step(4 * it + j, j, 2 * it, True)

            if opening:
                for j in range(lead):
                    ahead(j, j % SLOTS, j // 2)
                return
            rounds = s.rounds - (1 if lead <= LEAD else 2)
            loop(eng, rounds, body)
            for i in range(4 * rounds, s.n):
                step(i, i % SLOTS, i // 4 * 2, i + lead < s.n)

        def up_cols(s, ft):
            if isinstance(ft, int):
                return slice(ft * P, min((ft + 1) * P, s.width))
            return bass.ds(ft * P, P)

        def sp_up(sp, s, opening=False):
            def load(i, j, ft):
                sp_slot(sp, s, i)
                w = (s.gate, s.up)[j % 2]
                if s.mode == "dequant":
                    cols = up_cols(s, ft)
                    n = cols.stop - cols.start if isinstance(cols, slice) else P
                    words = P // PACK
                    v = nat[:, j, :].bitcast(I32).rearrange("p (k c) -> p k c", c=P)
                    for x in range(PACK):
                        sp.dma_start(v[x:P:PACK, :, 0:n], w.rearrange("(k r) c -> r k c", r=words)[:, :, cols])\
                          .then_inc(loaded[j].sem, 16)
                else:
                    rows = up_cols(s, ft)
                    n = rows.stop - rows.start if isinstance(rows, slice) else P
                    sp.dma_start(nat[0:n, j, :], w[rows, :]).then_inc(loaded[j].sem, 16)

            up_rounds(sp, s, load, lambda i, j, ft: None, opening, LEAD_LOAD)

        def pe_up(pe, s, opening=False):
            def ahead(i, j, ft):
                if s.mode == "dequant":
                    pe_spread(pe, s, i, j, slice(0, P), hot, D * (j % 2), [(k, P) for k in range(KT)],
                              up_cols(s, ft))
                else:
                    pe_turn(pe, s, i, j, [nat[:, j, k * P:(k + 1) * P] for k in range(KT)])

            def work(i, j, ft):
                pe.wait_ge((gate_read, up_read)[j % 2].sem, (s.gate0, s.up0)[j % 2] + 2 * ft)
                more = None
                if s.adapters:
                    pe.wait_ge(small.sem, s.small0 + i + 1)
                    r = slice(32 * (j % 2), 32 * (j % 2) + RANK)
                    more = lambda half: (b13s[r, j, :], low[r, at(half)])
                pe_chunk(pe, s, i, j, [P] * KT, xn, acc[j % 2], more=more, norm=s.norm if j == 0 else None)

            up_rounds(pe, s, ahead, work, opening)

        def act_up(act, s, opening=False):
            def work(i, j, ft):
                for half in range(NH):
                    if j % 2 == 0:
                        if half == 0:
                            act.wait_ge(half0.sem, s.half00 + i + 1)
                            act.wait_ge(up_read.sem, s.up0 + 2 * ft)
                        else:
                            act.wait_ge(used.sem, s.used0 + i + 1)
                        nc.scalar.activation(s.sg[:, half, :], acc[0][half][:, :], ACT.Silu).then_inc(gate_read.sem, 1)
                    else:
                        act.wait_ge(up_read.sem, s.up0 + 2 * ft + half + 1)
                        nc.scalar.activation(s.h[0][:, bass.ds(ft, 1), at(half)].rearrange("p o c -> p (o c)"),
                                             s.hf[:, half, :], ACT.Copy).then_inc(h_hi_done.sem, 1)

            up_rounds(act, s, lambda i, j, ft: act_hi(act, s, i, j, ALL), work, opening)

        def dve_up(dve, s, opening=False):
            def ahead(i, j, ft):
                if s.mode == "dequant":
                    dve_dequant(dve, s, i, j, ALL)
                dve_lo(dve, s, i, j, ALL)
                if s.adapters:
                    nc.vector.tensor_scalar(b13s[0:48, j, :], b13[0:48, bass.ds(ft * P, P)], LORA, None, ALU.mult)\
                      .then_inc(small.sem, 1)

            def work(i, j, ft):
                if j % 2 == 0:
                    return
                for half in range(NH):
                    if half == 0:
                        dve.wait_ge(half0.sem, s.half00 + i + 1)
                        dve.wait_ge(h_lo_done.sem, s.hlo0 + 2 * ft)
                    else:
                        dve.wait_ge(used.sem, s.used0 + i + 1)
                    dve.wait_ge(gate_read.sem, s.gate0 + 2 * ft + half + 1)
                    nc.vector.tensor_tensor(s.hf[:, half, :], s.sg[:, half, :], acc[1][half][:, :], ALU.mult)\
                      .then_inc(up_read.sem, 1)

            up_rounds(dve, s, ahead, work, opening)

        def pool_up(pool, s, opening=False):
            def ahead(i, j, ft):
                if s.scales is not None:
                    pool_scale(pool, s, i, j, D, s.scales[:, j % 2, bass.ds(ft, 1), :].rearrange("p o k -> p (o k)"))

            def work(i, j, ft):
                if j % 2 == 0:
                    return
                for half in range(NH):
                    pool.wait_ge(h_hi_done.sem, s.hhi0 + 2 * ft + half + 1)
                    o = [x[:, bass.ds(ft, 1), at(half)].rearrange("p o c -> p (o c)") for x in s.h]
                    nc.gpsimd.tensor_tensor(o[1], s.hf[:, half, :], o[0].bitcast(F32), ALU.subtract)\
                      .then_inc(h_lo_done.sem, 1)

            up_rounds(pool, s, ahead, work, opening, LEAD_SCALE)

        def plan_proj(chunks, mode, n_tiles, rhs, engine):
            s = plan_chunks(len(chunks), mode, [len(c["loads"]) for c in chunks])
            s.chunks, s.n_tiles, s.rhs, s.engine = chunks, n_tiles, rhs, engine
            s.half00 = half0.reserve(n_tiles)
            s.out0 = out_read.reserve(2 * n_tiles)
            return s

        def proj_order(s, ahead, work, opening, lead=LEAD):
            for i in range(min(lead, s.n)) if opening else ():
                ahead(i, i % SLOTS, s.chunks[i])
            for i in range(s.n) if not opening else ():
                if i + lead < s.n:
                    ahead(i + lead, (i + lead) % SLOTS, s.chunks[i + lead])
                work(i, i % SLOTS, s.chunks[i])

        def sp_proj(sp, s, opening=False):
            def load(i, j, c):
                sp_slot(sp, s, i)
                for dst, src in c["loads"]:
                    sp.dma_start(dst(j), src).then_inc(loaded[j].sem, 16)

            proj_order(s, load, lambda i, j, c: None, opening, LEAD_LOAD)

        def pe_proj(pe, s, opening=False):
            def ahead(i, j, c):
                if s.mode == "dequant":
                    pe_spread(pe, s, i, j, ROWS_DOWN, hot_d, 0, c["kts"], c["cols"])
                elif s.mode != "direct":
                    pe_turn(pe, s, i, j, c["views"](j))

            def work(i, j, c):
                if c["first"] and c["tile"] >= 2:
                    pe.wait_ge(out_read.sem, s.out0 + 2 * (c["tile"] - 1))
                pe_chunk(pe, s, i, j, c["rows"], lambda k, half: s.rhs(c["k0"] + k, half, c["rows"][k]),
                         acc[c["tile"] % 2], c["first"], c["last"], c.get("more"), s.norm if i == 0 else None)

            proj_order(s, ahead, work, opening)

        def sums_ready(eng, s, i, tile, half):
            if half == 0:
                eng.wait_ge(half0.sem, s.half00 + tile + 1)
            else:
                eng.wait_ge(used.sem, s.used0 + i + 1)

        def act_proj(act, s, opening=False):
            def work(i, j, c):
                if s.engine != "act" or not c["last"]:
                    return
                for half in range(NH):
                    sums_ready(act, s, i, c["tile"], half)
                    dst, b, factor = c["to"](half)
                    n = dst.shape[0]
                    nc.scalar.activation(dst, acc[c["tile"] % 2][half][0:n, :], ACT.Identity,
                                         bias=0.0 if b is None else b, scale=factor).then_inc(out_read.sem, 1)

            proj_order(s, lambda i, j, c: act_hi(act, s, i, j, c["parts"]), work, opening)

        def dve_proj(dve, s, opening=False):
            def ahead(i, j, c):
                if s.mode == "dequant":
                    dve_dequant(dve, s, i, j, c["parts"])
                dve_lo(dve, s, i, j, c["parts"])

            def work(i, j, c):
                if s.engine != "dve" or not c["last"]:
                    return
                for half in range(NH):
                    sums_ready(dve, s, i, c["tile"], half)
                    x = xT[:, c["tile"], at(half)]
                    a = acc[c["tile"] % 2][half][:, :]
                    if c.get("bias") is None:
                        ins = nc.vector.tensor_tensor(x, a, x, ALU.add)
                    else:
                        ins = nc.vector.scalar_tensor_tensor(x, a, c["bias"], x, ALU.add, ALU.add)
                    ins.then_inc(out_read.sem, 1)

            proj_order(s, ahead, work, opening)

        def pool_proj(pool, s, opening=False):
            if s.mode == "scaled":
                proj_order(s, lambda i, j, c: pool_scale(pool, s, i, j, len(c["rows"]) * P, c["scales"]),
                           lambda i, j, c: None, opening, LEAD_SCALE)

        def nat_views(n, rows=P, last=P):
            return lambda j: [nat[0:rows, j, k * P:k * P + (P if k < n - 1 else last)] for k in range(n)]

        def slot(*index):
            return lambda j: nat[(index[0], j) + tuple(index[1:])]

        def rows_chunk(w, r0, k0=0, **more):
            return dict(loads=[(slot(slice(0, P), slice(0, D)), w[r0:r0 + P, :])], parts=ALL, rows=[P] * KT,
                        views=nat_views(KT), first=True, last=True, k0=k0, **more)

        def split_kts(nf):
            q = -(-nf // 4)
            return [list(range(a, min(a + q, nf))) for a in range(0, nf, q)]

        def h_of(h):
            return lambda k, half, rows: (h[0][0:rows, k, at(half)], h[1][0:rows, k, at(half)])

        def down_chunks(w, width, scales=None, more=None):
            found = []
            nf = -(-width // P)
            for m in range(-(-w.shape[0] // P)):
                for kts in split_kts(nf):
                    a, b = kts[0] * P, min((kts[-1] + 1) * P, width)
                    last = b - kts[-1] * P
                    n = len(kts)
                    r = min(P, w.shape[0] - m * P)
                    c = dict(loads=[(slot(slice(0, r), slice(0, b - a)), w[m * P:m * P + r, a:b])],
                             parts=whole(n, last), rows=[P] * (n - 1) + [last], views=nat_views(n, last=last),
                             first=a == 0, last=b == width, k0=kts[0], tile=m)
                    if scales is not None:
                        c["scales"] = scales[:, m, kts[0]:kts[0] + n]
                    if more is not None and b == width:
                        c["more"] = more(m)
                    found.append(c)
            return found

        def packed_down_chunks(w, width):
            found = []
            nf = -(-width // P)
            words = P // PACK
            for m in range(KT):
                for kts in split_kts(nf):
                    n = len(kts)
                    last = min(P, width - kts[-1] * P)
                    loads = []
                    for x in range(PACK):
                        for k0, n_k, rows in ((0, n if last == P else n - 1, P), (n - 1, 1 if last < P else 0, last)):
                            if n_k:
                                r0 = (kts[0] + k0) * words
                                r1 = r0 + n_k * words if rows == P else r0 + rows // PACK
                                dst = (lambda j, x=x, k0=k0, n_k=n_k, rows=rows:
                                       nat[x:rows:PACK, j, k0 * P:(k0 + n_k) * P].bitcast(I32)
                                       .rearrange("r (k c) -> r k c", c=P))
                                src = w[r0:r1, m * P:(m + 1) * P].rearrange("(k r) c -> r k c", k=n_k)
                                loads.append((dst, src))
                    found.append(dict(loads=loads, parts=whole(n, last), rows=[P] * (n - 1) + [last],
                                      kts=[(k, P if k < kts[-1] else last) for k in kts],
                                      cols=slice(m * P, (m + 1) * P), first=kts[0] == 0,
                                      last=kts[-1] == nf - 1, k0=kts[0], tile=m))
            return found

        def dve_tables(dve, s):

            def chain(ins):
                s.count += 1
                ins.then_inc(step_b.sem, 1)
                dve.wait_ge(step_b.sem, s.count)

            for g, name, hots, first, n_in, width in s.which:
                h, n = hots[g, first:first + n_in], sgf0[g, :, :, :].rearrange("p a b c -> p (a b c)")[:, 0:n_in]
                groups = g.stop - g.start
                chain(nc.vector.tensor_copy(h, zero[g, 0:n_in].bitcast(I32)))
                chain(nc.vector.tensor_scalar(n, h, 0.0, float(groups), ALU.is_lt, ALU.mult))
                chain(nc.vector.tensor_tensor(h, h, n, ALU.add))
                chain(nc.vector.tensor_scalar(h, h, 0.0, groups - 1.0, ALU.max, ALU.min))
                chain(nc.vector.tensor_scalar(n, h, cst[g, C_IDX:C_IDX + 1], float(-g.start), ALU.subtract, ALU.subtract))
                chain(nc.vector.tensor_scalar(h, n, 0.0, None, ALU.is_equal))
                z = zero[g, 0:width]
                for x in range(PACK):
                    zi = z.bitcast(I32).rearrange("p (n x) -> p n x", x=PACK)[:, :, x]
                    chain(nc.vector.tensor_scalar(zi, packed[g, 0:width // PACK], 32 // PACK * x, 15,
                                                  ALU.logical_shift_right, ALU.bitwise_and))
                chain(nc.vector.tensor_scalar(z, z.bitcast(I32), 1.0, None, ALU.add))

        def plan_tables(which):
            s = Stage()
            s.which = which
            s.count = step_b.count
            step_b.count += len(which) * (7 + PACK)
            return s

        def plan_prep(rope, n_k, n_v):
            s = Stage()
            s.rope, s.n_v = rope, n_v
            s.tiles = [(x, c, half) for x, n in ((at_q, QC), (at_k, n_k)) for c in range(n) for half in range(NH)]
            s.tiles = s.tiles if rope else []
            n = len(s.tiles)
            s.a0, s.b0, s.c0, s.d0 = (x.reserve(n) for x in (step_a, step_b, step_c, step_d))
            s.vr0, s.vc0 = v_ready.reserve(2 * n_v), v_copied.reserve(2 * n_v)
            return s

        def pe_prep(pe, s):
            for n, (x, c, half) in enumerate(s.tiles):
                if n >= 2:
                    pe.wait_ge(step_b.sem, s.b0 + n - 1)
                r = s.rope[2]
                nc.tensor.matmul(turn_bank[n % 2][:, :], cst[:, r:r + P], x[:, c, at(half)], start=True, stop=True)\
                  .then_inc(step_a.sem, 1)
            for n in range(2 * s.n_v):
                if n >= 2:
                    pe.wait_ge(v_copied.sem, s.vc0 + n - 1)
                for j in range(4):
                    tt = 4 * (n % 2) + j
                    mm = nc.tensor.transpose(bank[2 + n % 2][:, j * P:(j + 1) * P],
                                             at_v[:, n // 2, tt * P:(tt + 1) * P], ident)
                mm.then_inc(v_ready.sem, 1)

        def seqs(ap):
            return ap.rearrange("p (b s) -> p b s", s=SEQ)

        def dve_prep(dve, s):
            for n, (x, c, half) in enumerate(s.tiles):
                rot = at_km[:, n % 2, 0:2, :]
                dve.wait_ge(step_a.sem, s.a0 + n + 1)
                if n >= 2:
                    dve.wait_ge(step_d.sem, s.d0 + n - 1)
                nc.vector.tensor_tensor(rot, seqs(turn_bank[n % 2][:, :]),
                                        bcast(cst[:, s.rope[1]:s.rope[1] + SEQ], 2), ALU.mult).then_inc(step_b.sem, 1)
                dve.wait_ge(step_b.sem, s.b0 + n + 1)
                dve.wait_ge(step_c.sem, s.c0 + n + 1)
                nc.vector.tensor_tensor(seqs(x[:, c, at(half)]), seqs(x[:, c, at(half)]), rot, ALU.add)\
                  .then_inc(step_d.sem, 1)
            for n in range(2 * s.n_v):
                dve.wait_ge(v_ready.sem, s.vr0 + n + 1)
                tt = 4 * (n % 2)
                nc.vector.tensor_copy(at_val[:, tt:tt + 4, n // 2, :, 0:HD],
                                      bank[2 + n % 2][:, :].rearrange("p (t h d) -> p t h d", t=4, h=HPC))\
                  .then_inc(v_copied.sem, 1)

        def pool_prep(pool, s):
            nc.gpsimd.memset(at_val[:, :, 0:s.n_v, :, HD:VW].rearrange("p t c h o -> p t (c h o)"), 1.0)
            for n, (x, c, half) in enumerate(s.tiles):
                pool.wait_ge(step_a.sem, s.a0 + n + 1)
                v = seqs(x[:, c, at(half)])
                nc.gpsimd.tensor_tensor(v, v, bcast(cst[:, s.rope[0]:s.rope[0] + SEQ], 2), ALU.mult)\
                  .then_inc(step_c.sem, 1)

        STEPS = 6
        ALL_STEPS = STEPS * QC

        def plan_att(n_k, n_v):
            s = Stage()
            n = BATCH * ALL_STEPS
            s.n_k, s.n_v = n_k, n_v
            s.sr, s.mx, s.ex, s.pr, s.pc, s.pv = (x.reserve(n) for x in (
                s_ready, max_done, exp_done, pt_ready, pt_copied, pv_done))
            s.on, s.tr, s.th, s.tl, s.sm = (x.reserve(BATCH * QC) for x in (o_normed, ot_ready, ot_hi, ot_lo, small))
            s.km, s.qs = km_made.reserve(BATCH * n_k), qs_made.reserve(BATCH)
            return s

        def step_heads(part):
            return (0, 4 * part, 4) if part < 2 else (1, 2 * (part - 2), 2)

        def pe_att(pe, s):
            def body(b):
                def scores(n):
                    c, part = divmod(n, STEPS)
                    qt, h, nh = step_heads(part)
                    if n == 0:
                        pe.wait_ge(qs_made.sem, s.qs + b + 1)
                    if part == 0 and c < s.n_k:
                        pe.wait_ge(km_made.sem, s.km + s.n_k * b + c + 1)
                    if n >= 3:
                        pe.wait_ge(exp_done.sem, s.ex + ALL_STEPS * b + n - 2)
                    o = bank[n % 3][:, :].rearrange("p (h k) -> p h k", h=nh)
                    keys = (qt + 1) * P
                    nc.tensor.matmul(o, at_qs[:, c, qt * P:(qt + 1) * P],
                                     at_km[:, c % 2 if s.n_k > 1 else 0, h:h + nh, 0:keys], start=True, stop=False)
                    nc.tensor.matmul(o[:, :, qt * P:keys], ident16[:, :], bcast(mask16[:, :], nh), start=False, stop=True)\
                      .then_inc(s_ready.sem, 1)

                def turns(n):
                    pe.wait_ge(exp_done.sem, s.ex + ALL_STEPS * b + n + 1)
                    if n >= 2:
                        pe.wait_ge(pt_copied.sem, s.pc + ALL_STEPS * b + n - 1)
                    for j in range(4):
                        mm = nc.tensor.transpose(bank[3 + n % 2][:, j * P:(j + 1) * P],
                                                 at_p[:, n % 3, j * P:(j + 1) * P], ident)
                    mm.then_inc(pt_ready.sem, 1)

                def values(n):
                    c, part = divmod(n, STEPS)
                    qt, h, nh = step_heads(part)
                    pe.wait_ge(pt_copied.sem, s.pc + ALL_STEPS * b + n + 1)
                    if part == 0 and c >= 2:
                        pe.wait_ge(o_normed.sem, s.on + QC * b + c - 1)
                    o = bank[5 + c % 2][:, 0:2 * HPC * VW].rearrange("p (q h d) -> p q h d", q=2, h=HPC)
                    for x in range(nh):
                        for kb in range(qt + 1):
                            j = x * (qt + 1) + kb
                            v = at_val[:, bass.ds(2 * b + kb, 1), c if s.n_v > 1 else 0, h + x, :]
                            mm = nc.tensor.matmul(o[:, qt, h + x, :], at_pt[:, n % 2, j * P:(j + 1) * P],
                                                  v.rearrange("p o d -> p (o d)"), start=kb == 0, stop=kb == qt)
                    mm.then_inc(pv_done.sem, 1)

                def turn_out(c):
                    pe.wait_ge(o_normed.sem, s.on + QC * b + c + 1)
                    pe.wait_ge(ot_lo.sem, s.tl + QC * b + c)
                    for qt in range(2):
                        mm = nc.tensor.transpose(bank[7][:, qt * P:(qt + 1) * P], at_on[:, c % 2, qt, :], ident)
                    mm.then_inc(ot_ready.sem, 1)

                scores(0)
                scores(1)
                for n in range(ALL_STEPS):
                    if n + 2 < ALL_STEPS:
                        scores(n + 2)
                    turns(n)
                    if n >= 1:
                        values(n - 1)
                    if n >= 8 and n % STEPS == 2:
                        turn_out(n // STEPS - 1)
                values(ALL_STEPS - 1)
                turn_out(QC - 1)

            loop(pe, BATCH, body)

        def dve_att(dve, s):
            def body(b):
                def top(n):
                    qt, h, nh = step_heads(n % STEPS)
                    dve.wait_ge(s_ready.sem, s.sr + ALL_STEPS * b + n + 1)
                    nc.vector.tensor_reduce(at_small[:, 4 * (n % 3):4 * (n % 3) + nh],
                                            bank[n % 3][:, :].rearrange("p (h k) -> p h k", h=nh), AX.X, ALU.max,
                                            negate=True).then_inc(max_done.sem, 1)

                def copy(n):
                    dve.wait_ge(pt_ready.sem, s.pr + ALL_STEPS * b + n + 1)
                    if n >= 2:
                        dve.wait_ge(pv_done.sem, s.pv + ALL_STEPS * b + n - 1)
                    nc.vector.tensor_copy(at_pt[:, n % 2, :], bank[3 + n % 2][:, :]).then_inc(pt_copied.sem, 1)

                def norm(c):
                    dve.wait_ge(pv_done.sem, s.pv + ALL_STEPS * b + STEPS * (c + 1))
                    o = bank[5 + c % 2][:, 0:2 * HPC * VW].rearrange("p (q h d) -> p q h d", q=2, h=HPC)
                    r = at_small[:, 16 + 16 * (c % 2):32 + 16 * (c % 2)].rearrange("p (q h o) -> p q h o", q=2, o=1)
                    nc.vector.reciprocal(r, o[:, :, :, HD:VW]).then_inc(small.sem, 1)
                    dve.wait_ge(small.sem, s.sm + QC * b + c + 1)
                    if c >= 2:
                        dve.wait_ge(ot_ready.sem, s.tr + QC * b + c - 1)
                    nc.vector.tensor_tensor(at_on[:, c % 2, :, :].rearrange("p q (h d) -> p q h d", d=HD),
                                            o[:, :, :, 0:HD], r.broadcast_to([P, 2, HPC, HD]), ALU.mult)\
                      .then_inc(o_normed.sem, 1)

                def low_part(c):
                    dve.wait_ge(ot_hi.sem, s.th + QC * b + c + 1)
                    nc.vector.tensor_tensor(at_lo[:, c, bass.ds(b * SEQ, SEQ)], bank[7][:, 0:SEQ],
                                            at_hi[:, c, bass.ds(b * SEQ, SEQ)].bitcast(F32), ALU.subtract)\
                      .then_inc(ot_lo.sem, 1)

                top(0)
                top(1)
                for n in range(ALL_STEPS):
                    if n + 2 < ALL_STEPS:
                        top(n + 2)
                    copy(n)
                    if n >= STEPS and n % STEPS == 0:
                        norm(n // STEPS - 1)
                    if n >= 9 and n % STEPS == 3:
                        low_part(n // STEPS - 1)
                norm(QC - 1)
                low_part(QC - 1)

            loop(dve, BATCH, body)

        def act_att(act, s):
            def body(b):
                def high_part(c):
                    act.wait_ge(ot_ready.sem, s.tr + QC * b + c + 1)
                    nc.scalar.activation(at_hi[:, c, bass.ds(b * SEQ, SEQ)], bank[7][:, 0:SEQ], ACT.Copy)\
                      .then_inc(ot_hi.sem, 1)

                for n in range(ALL_STEPS):
                    qt, h, nh = step_heads(n % STEPS)
                    act.wait_ge(max_done.sem, s.mx + ALL_STEPS * b + n + 1)
                    if n >= 3:
                        act.wait_ge(pt_ready.sem, s.pr + ALL_STEPS * b + n - 2)
                    w = 512 // nh
                    for x in range(nh):
                        ins = nc.scalar.activation(at_p[:, n % 3, x * w:(x + 1) * w], bank[n % 3][:, x * w:(x + 1) * w],
                                                   ACT.Exp, bias=at_small[:, 4 * (n % 3) + x:4 * (n % 3) + x + 1])
                    ins.then_inc(exp_done.sem, 1)
                    if n >= 9 and n % STEPS == 3:
                        high_part(n // STEPS - 1)
                high_part(QC - 1)

            loop(act, BATCH, body)

        def pool_att(pool, s):
            def body(b):
                pool.wait_ge(s_ready.sem, s.sr + ALL_STEPS * b)
                nc.gpsimd.tensor_copy(at_qs[:, :, :], at_q[:, :, bass.ds(b * SEQ, SEQ)]).then_inc(qs_made.sem, 1)
                for c in range(s.n_k):
                    if c >= 2:
                        pool.wait_ge(s_ready.sem, s.sr + ALL_STEPS * b + STEPS * (c - 1))
                    nc.gpsimd.tensor_tensor(at_km[:, c % 2, :, :], bcast(at_k[:, c, bass.ds(b * SEQ, SEQ)], HPC),
                                            tail_bcast(cst[:, C_HEAD:C_HEAD + HPC], SEQ), ALU.mult)\
                      .then_inc(km_made.sem, 1)

            loop(pool, BATCH, body)

        def plan_qk2():
            s = plan_chunks(2 * H2, "direct", 1)
            n = 4 * H2
            s.half00, s.sq0, s.ssq0 = half0.reserve(2 * H2), sq_done.reserve(n), ssq_done.reserve(n + 1) + 1
            s.small0 = small.reserve(2 * H2)
            s.raw0 = [x.reserve(2 * H2) for x in raw_done]
            s.st0 = [x.reserve(16 * H2 // 2) for x in stored]
            s.rounds, s.tail = H2 // 2, 0
            return s

        def sp_qk2(sp, s, opening=False):
            def load(i, j, h):
                sp_slot(sp, s, i)
                w = t["L2_attn_W" + "qk"[j % 2]].rearrange("(k p) n -> p k n", p=P)
                sp.dma_start(nat[:, j, :].rearrange("p (k c) -> p k c", c=P), w[:, :, bass.ds(h * P, P)])\
                  .then_inc(loaded[j].sem, 16)

            def store(i, j, h):
                sp.wait_ge(raw_done[j % 2].sem, s.raw0[j % 2] + 2 * h + 2)
                sp.dma_start(qk_dram[bass.ds(h, 1), j % 2, :, :].rearrange("o p c -> (o p) c"), raw2[:, j, :])\
                  .then_inc(stored[j].sem, 16)

            up_rounds(sp, s, load, store, opening, LEAD_LOAD)
            for j in range(SLOTS) if not opening else ():
                sp.wait_ge(stored[j].sem, stored[j].count)

        def pe_qk2(pe, s, opening=False):
            def work(i, j, h):
                pe.wait_ge(raw_done[j % 2].sem, s.raw0[j % 2] + 2 * h)
                pe_chunk(pe, s, i, j, [P] * KT, xn, acc[j % 2])

            up_rounds(pe, s, lambda i, j, h: None, work, opening)

        def act_qk2(act, s, opening=False):
            def work(i, j, h):
                for half in range(NH):
                    if half == 0:
                        act.wait_ge(half0.sem, s.half00 + i + 1)
                        act.wait_ge(small.sem, s.small0 + i + 1)
                        act.wait_ge(ssq_done.sem, s.ssq0 + 2 * (i - j))
                    else:
                        act.wait_ge(used.sem, s.used0 + i + 1)
                    nc.scalar.activation(sq2[:, j, at(half)], acc[j % 2][half][:, :], ACT.Square,
                                         bias=b2s[:, j:j + 1]).then_inc(sq_done.sem, 1)

            up_rounds(act, s, lambda i, j, h: act_hi(act, s, i, j, ALL), work, opening)

        def dve_qk2(dve, s, opening=False):
            def ahead(i, j, h):
                nc.vector.tensor_scalar(b2s[:, j:j + 1], cols2[:, j % 2, bass.ds(h, 1)], 0.0, None, ALU.add)\
                  .then_inc(small.sem, 1)
                dve_lo(dve, s, i, j, ALL)

            def work(i, j, h):
                for half in range(NH):
                    dve.wait_ge(sq_done.sem, s.sq0 + 2 * i + half + 1)
                    if half == 0:
                        dve.wait_ge(stored[j].sem, s.st0[j] + 4 * (i - j))
                    nc.vector.tensor_scalar(raw2[:, j, at(half)], acc[j % 2][half][:, :],
                                            cols2[:, j % 2, bass.ds(h, 1)], cols2[:, 3 + j % 2, bass.ds(h, 1)],
                                            ALU.add, ALU.mult).then_inc(raw_done[j % 2].sem, 1)

            up_rounds(dve, s, ahead, work, opening)

        def pool_qk2(pool, s, opening=False):
            def work(i, j, h):
                for half in range(NH):
                    pool.wait_ge(sq_done.sem, s.sq0 + 2 * i + half + 1)
                    pool.wait_ge(ssq_done.sem, s.ssq0 + 2 * i + half)
                    v = ssq[:, j % 2, at(half)]
                    nc.gpsimd.tensor_tensor(v, v, sq2[:, j, at(half)], ALU.add).then_inc(ssq_done.sem, 1)

            if not opening:
                nc.gpsimd.memset(ssq[:, :, :], 0.0).then_inc(ssq_done.sem, 1)
            up_rounds(pool, s, lambda i, j, h: None, work, opening)

        def plan_rms():
            s = Stage()
            s.a0, s.b0, s.c0 = step_a.reserve(4), step_b.reserve(4), step_c.reserve(4)
            return s

        def pe_rms(pe, s):
            for n in range(2):
                for half in range(NH):
                    nc.tensor.matmul(acc[n][half][:, :], cst[:, C_MEAN2:C_MEAN2 + P], ssq[:, n, at(half)],
                                     start=True, stop=True).then_inc(step_a.sem, 1)

        def act_rms(act, s):
            for n in range(2):
                for half in range(NH):
                    act.wait_ge(step_a.sem, s.a0 + 2 * n + half + 1)
                    nc.scalar.activation(rms[:, n, at(half)], acc[n][half][:, :], ACT.Sqrt, bias=eps[:, 1:2])\
                      .then_inc(step_b.sem, 1)

        def dve_rms(dve, s):
            for m in range(KT):
                nc.vector.tensor_scalar(xT[:, m, :], xT[:, m, :], bo2[:, m:m + 1], None, ALU.add)
            for n in range(2):
                for half in range(NH):
                    dve.wait_ge(step_b.sem, s.b0 + 2 * n + half + 1)
                    v = rms[:, n, at(half)]
                    nc.vector.reciprocal(v, v).then_inc(step_c.sem, 1)
            dve.wait_ge(step_c.sem, s.c0 + 2)
            nc.vector.tensor_scalar(rms[:, 0, :], rms[:, 0, :], float(1.0 / np.sqrt(HD2)), None, ALU.mult)

        GSTEPS = GRP2 * BATCH
        HSTEPS = GSTEPS // NH
        GROUPS2 = H2 // GRP2
        WO_SPLIT = (5, 9, 11, 13)

        def plan_att2():
            s = plan_chunks(GROUPS2 * KT, "direct", 1)
            used.count -= GROUPS2 * KT
            n = GROUPS2 * GSTEPS
            s.n = n
            s.sr, s.mx, s.ex, s.nd, s.pr, s.pc, s.pv, s.sm, s.oh, s.ol = (x.reserve(n) for x in (
                s_ready, max_done, exp_done, norm_done, pt_ready, pt_copied, pv_done, small, o_hi_done, o_lo_done))
            s.bv = bias_in.reserve(GROUPS2)
            s.q = n // 2
            s.qi = [x.reserve(16 * s.q // 2) for x in qk_in]
            s.qs, s.qh, s.ql = (x.reserve(s.q) for x in (qk_scaled, qk_hi_done, qk_lo_done))
            s.v = GROUPS2 * NH * (HALF // P)
            s.vh, s.vr, s.vc = (x.reserve(s.v) for x in (v_half, v_ready, v_copied))
            s.o = GROUPS2 * NH * KT
            s.wd, s.out0 = wo_done.reserve(s.o), out_read.reserve(s.o)
            s.wi = [x.reserve(16 * GROUPS2) for x in wo_in]
            s.wh, s.wl = (x.reserve(GROUPS2 * KT) for x in (wo_hi_done, wo_lo_done))
            return s

        def real(i, n):
            return not isinstance(i, int) or 0 <= i < n

        def groups(eng, body):
            body(-1)
            body(0)
            with eng.Fori(0, GROUPS2 - 2) as it:
                body(it + 1)
            body(GROUPS2 - 1)
            body(GROUPS2)

        def place(n):
            n %= GSTEPS
            return n // HSTEPS, n % HSTEPS // 2, n % 2

        def wo_place(i):
            return i % (NH * KT) // KT, i % KT

        def sp_att2(sp, s):
            def load_wv(g):
                for k in range(KT):
                    sp.wait_ge(lo.sem, s.lo0 + KT * g - KT + k + 1 if not isinstance(g, int) or g > 0 else s.lo0)
                    sp.dma_start(nat[:, k, :], t["L2_attn_Wv"][k * P:(k + 1) * P, bass.ds(g * GRP2 * HD2, GRP2 * HD2)])\
                      .then_inc(loaded[k].sem, 16)

            def load_wo(g, m):
                if not isinstance(g, int) or g > 0:
                    sp.wait_ge(wo_lo_done.sem, s.wl + KT * (g - 1) + m + 1)
                sp.dma_start(wo_nat[:, m, :].rearrange("p (k c) -> p k c", c=P),
                             t["L2_attn_Wo"].rearrange("(h p) n -> p h n", p=P)
                             [:, bass.ds(GRP2 * g, GRP2), m * P:(m + 1) * P]).then_inc(wo_in[m].sem, 16)

            def load_qk(g, e):
                q = 8 * g + e
                if not isinstance(q, int) or q >= 2:
                    sp.wait_ge(qk_lo_done.sem, s.ql + q - 1)
                half, x, _ = place(2 * e)
                h = GRP2 * (g + e // 8) + x
                sp.dma_start(qk_raw[:, e % 2, :, :], qk_dram[bass.ds(h, 1), :, :, at(half)]
                             .rearrange("o n p c -> (o p) n c")).then_inc(qk_in[e % 2].sem, 16)

            def body(g):
                if real(g + 1, GROUPS2):
                    load_wv(g + 1)
                for e in range(8):
                    if real(8 * g + e + 2, s.q):
                        load_qk(g, e + 2)
                    if e == 0 and real(g, GROUPS2):
                        load_wo(g, 3)
                    if e == 6 and real(g + 1, GROUPS2):
                        load_wo(g + 1, 0)
                if real(g + 1, GROUPS2):
                    load_wo(g + 1, 1)
                    load_wo(g + 1, 2)

            groups(sp, body)

        def pe_att2(pe, s):
            def scores(g, n):
                i = GSTEPS * g + n
                _, x, b = place(n)
                if b == 0:
                    pe.wait_ge(qk_lo_done.sem, s.ql + 8 * g + n // 2 + 1)
                if real(i - 2, s.n):
                    pe.wait_ge(exp_done.sem, s.ex + i - 1)
                for qt in range(2):
                    q = slice(b * SEQ + qt * P, b * SEQ + (qt + 1) * P)
                    for y, (a, c) in enumerate(((qk_hi, qk_hi), (qk_hi, qk_lo), (qk_lo, qk_hi))):
                        mm = nc.tensor.matmul(bank[n % 2][:, qt * SEQ:(qt + 1) * SEQ], a[:, x % 2, 0, q],
                                              c[:, x % 2, 1, b * SEQ:(b + 1) * SEQ], start=y == 0, stop=y == 2)
                mm.then_inc(s_ready.sem, 1)

            def values(g, n):
                i = 8 * g + 4 + n // 2
                part = n % 2
                tt = i % 8 if isinstance(i, int) else (4 + n // 2) % 8
                if n in (8, 9):
                    pe.wait_ge(lo.sem, s.lo0 + KT * (g + 1) + 2 * part + 2)
                if part == 0 and real(i - 1, s.v):
                    pe.wait_ge(v_copied.sem, s.vc + i)
                for k in (2 * part, 2 * part + 1):
                    for y, (a, w) in enumerate(((xn_hi, w_hi), (xn_lo, w_hi), (xn_hi, w_lo))):
                        mm = nc.tensor.matmul(bank[3][:, :], a[:, k, tt * P:(tt + 1) * P], w[:, k, :],
                                              start=k == 0 and y == 0, stop=k == KT - 1 and y == 2)
                mm.then_inc((v_half, v_ready)[part].sem, 1)

            def turns(g, n):
                i = GSTEPS * g + n
                pe.wait_ge(norm_done.sem, s.nd + i + 1)
                if real(i - 1, s.n):
                    pe.wait_ge(pt_copied.sem, s.pc + i)
                for kb in range(2):
                    for qt in range(2):
                        mm = nc.tensor.transpose(bank[2][:, kb * SEQ + qt * P:kb * SEQ + (qt + 1) * P],
                                                 p2[:, n % 4, qt, kb * P:(kb + 1) * P], ident)
                mm.then_inc(pt_ready.sem, 1)

            def project(g, n):
                i = 8 * g - 5 + n // 2
                part = n % 2
                half, m = wo_place(3 + n // 2)
                if part == 0:
                    if real(i - 2, s.o):
                        pe.wait_ge(out_read.sem, s.out0 + i - 1)
                    if half == 0:
                        pe.wait_ge(wo_lo_done.sem, s.wl + KT * (g if n >= 10 else g - 1) + m + 1)
                if m == 0:
                    pe.wait_ge(o_lo_done.sem, s.ol + 2 * i + 4 * part + 4)
                for k in (2 * part, 2 * part + 1):
                    for y, (w, o) in enumerate(((wo_hi, o2_hi), (wo_hi, o2_lo), (wo_lo, o2_hi))):
                        mm = nc.tensor.matmul(bank[6 + m % 2][:, :], w[:, m, k * P:(k + 1) * P], o[:, half, k, :],
                                              start=k == 0 and y == 0, stop=k == GRP2 - 1 and y == 2)
                if part == 1:
                    mm.then_inc(wo_done.sem, 1)

            def outputs(g, n):
                i = GSTEPS * g + n
                half, x, b = place(n)
                pe.wait_ge(pt_copied.sem, s.pc + i + 1)
                if n % HSTEPS == 0:
                    pe.wait_ge(v_copied.sem, s.vc + 8 * g + 4 * half + 4)
                if real(i - 2, s.n):
                    pe.wait_ge(o_lo_done.sem, s.ol + i - 1)
                for kb in range(2):
                    mm = nc.tensor.matmul(bank[4 + n % 2][:, 0:SEQ], val2[:, half, 2 * b + kb, x * HD2:(x + 1) * HD2],
                                          pt2[:, n % 2, kb, :], start=kb == 0, stop=kb == 1)
                mm.then_inc(pv_done.sem, 1)

            def body(g):
                for n in range(GSTEPS):
                    i = GSTEPS * g + n
                    if real(i + 2, s.n):
                        scores(g + (n + 2) // GSTEPS, (n + 2) % GSTEPS)
                    if real(8 * g + 4 + n // 2, s.v):
                        values(g, n)
                    if real(i, s.n):
                        turns(g, n)
                    if real(8 * g - 5 + n // 2, s.o):
                        project(g, n)
                    if real(i - 1, s.n):
                        outputs(g + (n - 1) // GSTEPS, (n - 1) % GSTEPS)

            groups(pe, body)

        def act_att2(act, s):
            def high_part(g, n):
                i = GSTEPS * g + n
                half, x, b = place(n)
                act.wait_ge(pv_done.sem, s.pv + i + 1)
                if n == 0:
                    act.wait_ge(bias_in.sem, s.bv + g + 1)
                if n % HSTEPS == 0 and real(2 * g + half - 2, 2 * GROUPS2):
                    act.wait_ge(wo_done.sem, s.wd + 8 * g + 4 * half - 4)
                nc.scalar.activation(o2_hi[:, half, x, b * SEQ:(b + 1) * SEQ], bank[4 + n % 2][:, 0:SEQ], ACT.Identity,
                                     bias=bv2[:, x:x + 1]).then_inc(o_hi_done.sem, 1)

            def split_qk(g, e):
                q = 8 * g + e
                act.wait_ge(qk_scaled.sem, s.qs + q + 1)
                if real(q - 2, s.q):
                    act.wait_ge(s_ready.sem, s.sr + 2 * q - 2)
                nc.scalar.activation(qk_hi[:, e % 2, :, :], qk_raw[:, e % 2, :, :], ACT.Copy).then_inc(qk_hi_done.sem, 1)

            def exps(g, n):
                i = GSTEPS * g + n
                act.wait_ge(max_done.sem, s.mx + i + 1)
                if real(i - 4, s.n):
                    act.wait_ge(pt_ready.sem, s.pr + i - 3)
                for qt in range(2):
                    ins = nc.scalar.activation(p2[:, n % 4, qt, :], bank[n % 2][:, qt * SEQ:(qt + 1) * SEQ], ACT.Exp,
                                               bias=small2[:, n % 4, qt:qt + 1], accum_out=small2[:, n % 4, 2 + qt:3 + qt])
                ins.then_inc(exp_done.sem, 1)

            def copy_values(g, n):
                i = 8 * g + 4 + n // 2
                tt = (4 + n // 2) % 8
                act.wait_ge(v_ready.sem, s.vr + i + 1)
                if tt % 4 == 0 and real(i - 8, s.v):
                    act.wait_ge(pv_done.sem, s.pv + 2 * i - 8)
                nc.scalar.activation(val2[:, tt // 4, tt % 4, :], bank[3][:, :], ACT.Copy).then_inc(v_copied.sem, 1)

            def split_wv(g, ks, done):
                for k in ks:
                    act.wait_ge(loaded[k].sem, s.load0[k] + 16 * g + 16)
                    if real(g - 1, GROUPS2):
                        act.wait_ge(*done)
                    else:
                        act.wait_ge(used.sem, s.used0)
                    nc.scalar.activation(w_hi[:, k, :], nat[:, k, :], ACT.Copy).then_inc(hi.sem, 1)

            def split_wo(g, m):
                act.wait_ge(wo_in[m].sem, s.wi[m] + 16 * g + 16)
                if real(g - 1, GROUPS2):
                    act.wait_ge(wo_done.sem, s.wd + 8 * g - 4 + m + 1)
                nc.scalar.activation(wo_hi[:, m, :], wo_nat[:, m, :], ACT.Copy).then_inc(wo_hi_done.sem, 1)

            def body(g):
                for n in range(GSTEPS):
                    i = GSTEPS * g + n
                    if real(i - 2, s.n):
                        high_part(g + (n - 2) // GSTEPS, (n - 2) % GSTEPS)
                    if n % 2 == 0 and real(8 * g + n // 2 + 2, s.q):
                        split_qk(g + (n // 2 + 2) // 8, (n // 2 + 2) % 8)
                    if n == 8 and real(g + 1, GROUPS2):
                        split_wv(g + 1, (2, 3), (v_ready.sem, s.vr + 8 * g + 8))
                    if real(i + 2, s.n):
                        exps(g + (n + 2) // GSTEPS, (n + 2) % GSTEPS)
                    if n % 2 == 1 and real(8 * g + 4 + n // 2, s.v):
                        copy_values(g, n)
                    if n == 7 and real(g + 1, GROUPS2):
                        split_wv(g + 1, (0, 1), (v_half.sem, s.vh + 8 * g + 8))
                    if n in WO_SPLIT and real(g, GROUPS2):
                        split_wo(g, WO_SPLIT.index(n))

            groups(act, body)

        def dve_att2(dve, s):
            def norm(g, n):
                i = GSTEPS * g + n
                dve.wait_ge(exp_done.sem, s.ex + i + 1)
                nc.vector.reciprocal(small2[:, n % 4, 4:6], small2[:, n % 4, 2:4]).then_inc(small.sem, 1)
                dve.wait_ge(small.sem, s.sm + i + 1)
                nc.vector.tensor_tensor(p2[:, n % 4, :, :], p2[:, n % 4, :, :], tail_bcast(small2[:, n % 4, 4:6], SEQ),
                                        ALU.mult).then_inc(norm_done.sem, 1)

            def top(g, n):
                dve.wait_ge(s_ready.sem, s.sr + GSTEPS * g + n + 1)
                nc.vector.tensor_reduce(small2[:, n % 4, 0:2], bank[n % 2][:, :].rearrange("p (q k) -> p q k", q=2),
                                        AX.X, ALU.max, negate=True).then_inc(max_done.sem, 1)

            def low_part(g, n):
                half, x, b = place(n)
                dve.wait_ge(o_hi_done.sem, s.oh + GSTEPS * g + n + 1)
                v = slice(b * SEQ, (b + 1) * SEQ)
                nc.vector.scalar_tensor_tensor(o2_lo[:, half, x, v], bank[4 + n % 2][:, 0:SEQ], bv2[:, x:x + 1],
                                               o2_hi[:, half, x, v].bitcast(F32), ALU.add, ALU.subtract)\
                  .then_inc(o_lo_done.sem, 1)

            def copy(g, n):
                i = GSTEPS * g + n
                dve.wait_ge(pt_ready.sem, s.pr + i + 1)
                if real(i - 2, s.n):
                    dve.wait_ge(pv_done.sem, s.pv + i - 1)
                nc.vector.tensor_copy(pt2[:, n % 2, :, :], bank[2][:, :].rearrange("p (k q) -> p k q", k=2))\
                  .then_inc(pt_copied.sem, 1)

            def add(g, n):
                half, m = wo_place(2 + n // 2)
                dve.wait_ge(wo_done.sem, s.wd + 8 * g - 6 + n // 2 + 1)
                nc.vector.tensor_tensor(xT[:, m, at(half)], bank[6 + m % 2][:, :], xT[:, m, at(half)], ALU.add)\
                  .then_inc(out_read.sem, 1)

            def split(hi_sem, count, hi_part, lo_part, src, lo_sem):
                dve.wait_ge(hi_sem, count)
                nc.vector.tensor_tensor(lo_part, src, hi_part.bitcast(F32), ALU.subtract).then_inc(lo_sem, 1)

            def split_wv(g, ks):
                for k in ks:
                    split(hi.sem, s.hi0 + KT * g + k + 1, w_hi[:, k, :], w_lo[:, k, :], nat[:, k, :], lo.sem)

            def body(g):
                for n in range(GSTEPS):
                    i = GSTEPS * g + n
                    if n == 2 and real(g, GROUPS2):
                        if real(g - 1, GROUPS2):
                            dve.wait_ge(o_lo_done.sem, s.ol + GSTEPS * g)
                        nc.vector.tensor_scalar(bv2[:, :], cols2[:, 2, bass.ds(GRP2 * g, GRP2)], 0.0, None, ALU.add)\
                          .then_inc(bias_in.sem, 1)
                        dve.wait_ge(bias_in.sem, s.bv + g + 1)
                    if real(i + 1, s.n):
                        norm(g + (n + 1) // GSTEPS, (n + 1) % GSTEPS)
                    if n == 8 and real(g + 1, GROUPS2):
                        split_wv(g + 1, (2, 3))
                    if real(i + 2, s.n):
                        top(g + (n + 2) // GSTEPS, (n + 2) % GSTEPS)
                    if real(i - 2, s.n):
                        low_part(g + (n - 2) // GSTEPS, (n - 2) % GSTEPS)
                    if real(i, s.n):
                        copy(g, n)
                    if n % 2 == 0 and real(8 * g - 6 + n // 2, s.o):
                        add(g, n)
                    if n == 7 and real(g + 1, GROUPS2):
                        split_wv(g + 1, (0, 1))
                    if n in WO_SPLIT and real(g, GROUPS2):
                        m = WO_SPLIT.index(n)
                        split(wo_hi_done.sem, s.wh + KT * g + m + 1, wo_hi[:, m, :], wo_lo[:, m, :], wo_nat[:, m, :],
                              wo_lo_done.sem)

            groups(dve, body)

        def pool_att2(pool, s):
            def scale_qk(g, e):
                q = 8 * g + e
                pool.wait_ge(qk_in[e % 2].sem, s.qi[e % 2] + 64 * g + 16 * (e // 2 + 1))
                half, _, _ = place(2 * e)
                v = qk_raw[:, e % 2, :, :]
                nc.gpsimd.tensor_tensor(v, v, rms[:, :, at(half)], ALU.mult).then_inc(qk_scaled.sem, 1)

            def split_qk(g, e):
                pool.wait_ge(qk_hi_done.sem, s.qh + 8 * g + e + 1)
                nc.gpsimd.tensor_tensor(qk_lo[:, e % 2, :, :], qk_raw[:, e % 2, :, :], qk_hi[:, e % 2, :, :].bitcast(F32),
                                        ALU.subtract).then_inc(qk_lo_done.sem, 1)

            def body(g):
                for e in range(8):
                    if real(8 * g + e + 1, s.q):
                        scale_qk(g + (e + 1) // 8, (e + 1) % 8)
                    if real(8 * g + e, s.q):
                        split_qk(g, e)

            groups(pool, body)

        def sp_adapters(sp):
            sp.wait_ge(cleared.sem, 3)
            for dst, name in ((b13[0:RANK, 0:F0], "B1"), (b13[32:32 + RANK, 0:F0], "B3"), (b2[:, :], "B2")):
                sp.dma_start(dst, t[f"L2_ffn_lora_{name}"].rearrange("o r -> r o"), allow_slow_non_contiguous=True)\
                  .then_inc(adapters_in.sem, 16)
                adapters_in.count += 16

        def pool_adapters(pool):
            nc.gpsimd.memset(b13[:, :], 0.0).then_inc(cleared.sem, 1)

        def rhs_xn(k, half, rows):
            return xn_hi[:, k, at(half)], xn_lo[:, k, at(half)]

        def rhs_out(k, half, rows):
            return at_hi[:, k, at(half)], at_lo[:, k, at(half)]

        def dest(x, c, b=None, factor=1.0):
            return lambda half: (x[:, c, at(half)], b, factor)

        def qkv0():
            found = []
            for x, name in ((at_q, "wq"), (at_k, "wk"), (at_v, "wv")):
                for c in range(QC):
                    found.append(rows_chunk(t[f"L0_attn_{name}"], c * P, tile=len(found), to=dest(x, c)))
            return found

        def qkv1():
            w = t["L1_attn_w_qkv"]
            found = []
            for c in range(QC):
                q = rows_chunk(w, 0, tile=c, to=dest(at_q, c, bias1[:, c:c + 1]))
                q["loads"] = [(slot(slice(kv * HD, (kv + 1) * HD), slice(0, D)),
                               w[(kv * QC + c) * HD:(kv * QC + c + 1) * HD, :]) for kv in range(KV1)]
                found.append(q)
            for n, x in enumerate((at_k, at_v)):
                found.append(rows_chunk(w, D + n * P, tile=QC + n, to=dest(x, 0, bias1[:, QC + n:QC + n + 1])))
            return found

        def qkv3():
            found = [rows_chunk(t["L3_attn_wq_w"], c * P, tile=c, to=dest(at_q, c, bias3[:, c:c + 1])) for c in range(QC)]
            for n, (x, name) in enumerate(((at_k, "wk"), (at_v, "wv"))):
                c = rows_chunk(t["L3_attn_wq_w"], 0, tile=QC + n, to=dest(x, 0, bias3[:, QC + n:QC + n + 1]))
                c["loads"] = [(slot(slice(r * HD, (r + 1) * HD), slice(0, D)), t[f"L3_attn_{name}_w"]) for r in range(DUP)]
                found.append(c)
            return found

        def wo(w, b=None, by_key_head=False):
            found = []
            for m in range(KT):
                c = rows_chunk(w, m * P, tile=m)
                if b is not None:
                    c["bias"] = b[:, QC + 2 + m:QC + 3 + m]
                if by_key_head:
                    src = w[m * P:(m + 1) * P, :].rearrange("p (v c d) -> p c v d", c=QC, d=HD)
                    c["loads"] = [(lambda j, n=n: nat[:, j, n * P:(n + 1) * P].rearrange("p (v d) -> p v d", d=HD),
                                   src[:, n, :, :]) for n in range(QC)]
                found.append(c)
            return found

        def adapter_chunks():
            c = rows_chunk(t["L2_ffn_w1"], 0, tile=0)
            c["loads"] = [(slot(slice(r, r + RANK), slice(0, D)), t[f"L2_ffn_lora_{n}"]) for r, n in ((0, "A1"), (32, "A3"))]
            c["to"] = lambda half: (low[0:48, at(half)], None, 1.0)
            return [c]

        def adapters_down():
            found = down_chunks(t["L2_ffn_lora_A2"], F0)
            for c in found:
                c["to"] = lambda half: (low[0:RANK, at(half)], None, LORA)
            return found

        start = plan_start()
        tables_up = plan_tables([(slice(0, GROUPS_UP), "gate", hot, 0, D, F0),
                                 (slice(32, 32 + GROUPS_UP), "up", hot, D, D, F0)])
        tables_down = plan_tables([(ROWS_DOWN, "down", hot_d, 0, F0, D)])
        norms = []
        norms.append(plan_norm())
        up0 = plan_up(F0, "dequant", PACK, t["L0_ffn_gate_qweight"], t["L0_ffn_up_qweight"], (h0_hi, h0_lo), sgf0)
        down0 = plan_proj(packed_down_chunks(t["L0_ffn_down_qweight"], F0), "dequant", KT, h_of((h0_hi, h0_lo)), "dve")
        in0 = plan_proj(qkv0(), "turn", 3 * QC, rhs_xn, "act")
        prep0 = plan_prep((C_COS0, C_SIN0, C_ROT0), QC, QC)
        att0 = plan_att(QC, QC)
        wo0 = plan_proj(wo(t["L0_attn_wo"]), "turn", KT, rhs_out, "dve")

        norms.append(plan_norm())
        up1 = plan_up(F0, "turn", 1, t["L1_ffn_W_gate"], t["L1_ffn_W_up"], (h1_hi, h1_lo), sgf1)
        down1 = plan_proj(down_chunks(t["L1_ffn_W_down"], F0), "turn", KT, h_of((h1_hi, h1_lo)), "dve")
        in1 = plan_proj(qkv1(), "turn", QC + 2, rhs_xn, "act")
        prep1 = plan_prep((C_COS1, C_SIN1, C_ROT1), 1, 1)
        att1 = plan_att(1, 1)
        wo1 = plan_proj(wo(t["L1_attn_w_o"], bias1, True), "turn", KT, rhs_out, "dve")

        norms.append(plan_norm())
        low_in = plan_proj(adapter_chunks(), "turn", 1, rhs_xn, "act")
        up2 = plan_up(F0, "turn", 1, t["L2_ffn_w1"], t["L2_ffn_w3"], (h2_hi, h2_lo), sgf2, adapters=True)
        low_down = plan_proj(adapters_down(), "turn", 1, h_of((h2_hi, h2_lo)), "act")
        down2 = plan_proj(down_chunks(t["L2_ffn_w2"], F0, more=lambda m: lambda half: (
            b2[:, m * P:(m + 1) * P], low[0:RANK, at(half)])), "turn", KT, h_of((h2_hi, h2_lo)), "dve")
        qk2 = plan_qk2()
        rms2 = plan_rms()
        att2 = plan_att2()

        norms.append(plan_norm())
        up3 = plan_up(F3, "scaled", 1, t["L3_ffn_w1"], t["L3_ffn_w3"], (h3_hi, h3_lo), sgf3, scales=wscale)
        down3 = plan_proj(down_chunks(t["L3_ffn_w2"], F3, scales=wscale2), "scaled", KT, h_of((h3_hi, h3_lo)), "dve")
        in3 = plan_proj(qkv3(), "turn", QC + 2, rhs_xn, "act")
        prep3 = plan_prep(None, 1, 1)
        att3 = plan_att(1, 1)
        wo3 = plan_proj(wo(t["L3_attn_wo_w"], bias3), "turn", KT, rhs_out, "dve")
        end = plan_end()

        for n, first in enumerate((up0, up1, low_in, up3)):
            first.norm = norms[n]

        block = ctx.enter_context(nc.Block())

        @block.sync
        def _(sp):
            sp.wait_ge(begun, 1)
            sp_start(sp)
            sp_up(sp, up0, True)
            sp_columns(sp)
            sp_up(sp, up0)
            sp_proj(sp, down0, True)
            sp_proj(sp, down0)
            sp_proj(sp, in0, True)
            sp_proj(sp, in0)
            sp_proj(sp, wo0, True)
            sp_proj(sp, wo0)
            sp_up(sp, up1, True)
            sp_up(sp, up1)
            sp_adapters(sp)
            sp_proj(sp, down1, True)
            sp_proj(sp, down1)
            sp_proj(sp, in1, True)
            sp_proj(sp, in1)
            sp_proj(sp, wo1, True)
            sp_proj(sp, wo1)
            sp_proj(sp, low_in, True)
            sp_proj(sp, low_in)
            sp_up(sp, up2, True)
            sp_up(sp, up2)
            sp_proj(sp, low_down, True)
            sp_proj(sp, low_down)
            sp_proj(sp, down2, True)
            sp_proj(sp, down2)
            sp_qk2(sp, qk2, True)
            sp_qk2(sp, qk2)
            join(sp, "rms2")
            sp_att2(sp, att2)
            sp_up(sp, up3, True)
            sp_up(sp, up3)
            sp_proj(sp, down3, True)
            sp_proj(sp, down3)
            sp_proj(sp, in3, True)
            sp_proj(sp, in3)
            sp_proj(sp, wo3, True)
            sp_proj(sp, wo3)
            sp_end(sp, end)

        @block.tensor
        def _(pe):
            pe.wait_ge(begun, 1)
            pe_start(pe, start)
            barrier(pe, "start")
            pe_norm(pe, norms[0])
            pe_up(pe, up0, True)
            pe_up(pe, up0)
            pe_proj(pe, down0, True)
            barrier(pe, "up0")
            pe_proj(pe, down0)
            pe_proj(pe, in0, True)
            barrier(pe, "down0")
            pe_proj(pe, in0)
            barrier(pe, "in0")
            pe_prep(pe, prep0)
            barrier(pe, "prep0")
            pe_att(pe, att0)
            pe_proj(pe, wo0, True)
            barrier(pe, "att0")
            pe_proj(pe, wo0)
            pe_up(pe, up1, True)
            barrier(pe, "wo0")
            pe_norm(pe, norms[1])
            pe_up(pe, up1)
            pe_proj(pe, down1, True)
            barrier(pe, "up1")
            pe_proj(pe, down1)
            pe_proj(pe, in1, True)
            barrier(pe, "down1")
            pe_proj(pe, in1)
            barrier(pe, "in1")
            pe_prep(pe, prep1)
            barrier(pe, "prep1")
            pe_att(pe, att1)
            pe_proj(pe, wo1, True)
            barrier(pe, "att1")
            pe_proj(pe, wo1)
            pe_proj(pe, low_in, True)
            barrier(pe, "wo1")
            pe_norm(pe, norms[2])
            pe_proj(pe, low_in)
            pe_up(pe, up2, True)
            barrier(pe, "low_in")
            pe_up(pe, up2)
            pe_proj(pe, low_down, True)
            barrier(pe, "up2")
            pe_proj(pe, low_down)
            pe_proj(pe, down2, True)
            barrier(pe, "low_down")
            pe_proj(pe, down2)
            pe_qk2(pe, qk2, True)
            barrier(pe, "down2")
            pe_qk2(pe, qk2)
            barrier(pe, "qk2")
            pe_rms(pe, rms2)
            barrier(pe, "rms2")
            pe_att2(pe, att2)
            pe_up(pe, up3, True)
            barrier(pe, "att2")
            pe_norm(pe, norms[3])
            pe_up(pe, up3)
            pe_proj(pe, down3, True)
            barrier(pe, "up3")
            pe_proj(pe, down3)
            pe_proj(pe, in3, True)
            barrier(pe, "down3")
            pe_proj(pe, in3)
            barrier(pe, "in3")
            pe_prep(pe, prep3)
            barrier(pe, "prep3")
            pe_att(pe, att3)
            pe_proj(pe, wo3, True)
            barrier(pe, "att3")
            pe_proj(pe, wo3)
            barrier(pe, "wo3")
            pe_end(pe, end)
            barrier(pe, "end")

        @block.scalar
        def _(act):
            act.wait_ge(begun, 1)
            act_start(act, start)
            barrier(act, "start")
            act_norm(act, norms[0])
            act_up(act, up0, True)
            act_up(act, up0)
            act_proj(act, down0, True)
            barrier(act, "up0")
            act_proj(act, down0)
            act_proj(act, in0, True)
            barrier(act, "down0")
            act_proj(act, in0)
            barrier(act, "in0")
            barrier(act, "prep0")
            act_att(act, att0)
            act_proj(act, wo0, True)
            barrier(act, "att0")
            act_proj(act, wo0)
            act.wait_ge(cols_in.sem, cols_in.count)
            act_up(act, up1, True)
            barrier(act, "wo0")
            act_norm(act, norms[1])
            act_up(act, up1)
            act_proj(act, down1, True)
            barrier(act, "up1")
            act_proj(act, down1)
            act_proj(act, in1, True)
            barrier(act, "down1")
            act_proj(act, in1)
            barrier(act, "in1")
            barrier(act, "prep1")
            act_att(act, att1)
            act_proj(act, wo1, True)
            barrier(act, "att1")
            act_proj(act, wo1)
            act_proj(act, low_in, True)
            barrier(act, "wo1")
            act_norm(act, norms[2])
            act_proj(act, low_in)
            act_up(act, up2, True)
            barrier(act, "low_in")
            act_up(act, up2)
            act_proj(act, low_down, True)
            barrier(act, "up2")
            act_proj(act, low_down)
            act_proj(act, down2, True)
            barrier(act, "low_down")
            act_proj(act, down2)
            act_qk2(act, qk2, True)
            barrier(act, "down2")
            act_qk2(act, qk2)
            barrier(act, "qk2")
            act_rms(act, rms2)
            barrier(act, "rms2")
            act_att2(act, att2)
            act_up(act, up3, True)
            barrier(act, "att2")
            act_norm(act, norms[3])
            act_up(act, up3)
            act_proj(act, down3, True)
            barrier(act, "up3")
            act_proj(act, down3)
            act_proj(act, in3, True)
            barrier(act, "down3")
            act_proj(act, in3)
            barrier(act, "in3")
            barrier(act, "prep3")
            act_att(act, att3)
            act_proj(act, wo3, True)
            barrier(act, "att3")
            act_proj(act, wo3)
            barrier(act, "wo3")
            barrier(act, "end")

        @block.vector
        def _(dve):
            dve.wait_ge(begun, 1)
            dve_start(dve)
            barrier(dve, "start")
            dve_norm(dve, norms[0])
            dve_up(dve, up0, True)
            dve_up(dve, up0)
            dve_proj(dve, down0, True)
            barrier(dve, "up0")
            dve_proj(dve, down0)
            dve_proj(dve, in0, True)
            barrier(dve, "down0")
            dve_proj(dve, in0)
            barrier(dve, "in0")
            dve_prep(dve, prep0)
            barrier(dve, "prep0")
            dve_att(dve, att0)
            dve_proj(dve, wo0, True)
            barrier(dve, "att0")
            dve_proj(dve, wo0)
            dve_up(dve, up1, True)
            barrier(dve, "wo0")
            dve_norm(dve, norms[1])
            dve_up(dve, up1)
            dve_proj(dve, down1, True)
            barrier(dve, "up1")
            dve_proj(dve, down1)
            dve_proj(dve, in1, True)
            barrier(dve, "down1")
            dve_proj(dve, in1)
            barrier(dve, "in1")
            dve_prep(dve, prep1)
            barrier(dve, "prep1")
            dve_att(dve, att1)
            dve_proj(dve, wo1, True)
            barrier(dve, "att1")
            dve_proj(dve, wo1)
            dve_proj(dve, low_in, True)
            barrier(dve, "wo1")
            dve_norm(dve, norms[2])
            dve_proj(dve, low_in)
            dve.wait_ge(adapters_in.sem, adapters_in.count)
            dve_up(dve, up2, True)
            barrier(dve, "low_in")
            dve_up(dve, up2)
            dve_proj(dve, low_down, True)
            barrier(dve, "up2")
            dve_proj(dve, low_down)
            dve_proj(dve, down2, True)
            barrier(dve, "low_down")
            dve_proj(dve, down2)
            dve_qk2(dve, qk2, True)
            barrier(dve, "down2")
            dve_qk2(dve, qk2)
            barrier(dve, "qk2")
            dve_rms(dve, rms2)
            barrier(dve, "rms2")
            dve_att2(dve, att2)
            dve_up(dve, up3, True)
            barrier(dve, "att2")
            dve_norm(dve, norms[3])
            dve_up(dve, up3)
            dve_proj(dve, down3, True)
            barrier(dve, "up3")
            dve_proj(dve, down3)
            dve_proj(dve, in3, True)
            barrier(dve, "down3")
            dve_proj(dve, in3)
            barrier(dve, "in3")
            dve_prep(dve, prep3)
            barrier(dve, "prep3")
            dve_att(dve, att3)
            dve_proj(dve, wo3, True)
            barrier(dve, "att3")
            dve_proj(dve, wo3)
            barrier(dve, "wo3")
            dve_end(dve, end)
            barrier(dve, "end")

        @block.gpsimd
        def _(pool):
            for x in signals:
                pool.sem_inc(x.sem, 1)
            pool.sem_inc(begun, 1)
            barrier(pool, "start")
            pool_norm(pool, norms[0])
            pool_up(pool, up0, True)
            pool_up(pool, up0)
            barrier(pool, "up0")
            pool_proj(pool, down0)
            barrier(pool, "down0")
            pool_proj(pool, in0)
            barrier(pool, "in0")
            pool_prep(pool, prep0)
            barrier(pool, "prep0")
            pool_att(pool, att0)
            barrier(pool, "att0")
            pool_proj(pool, wo0)
            barrier(pool, "wo0")
            pool_norm(pool, norms[1])
            pool_adapters(pool)
            pool_up(pool, up1)
            barrier(pool, "up1")
            pool_proj(pool, down1)
            barrier(pool, "down1")
            pool_proj(pool, in1)
            barrier(pool, "in1")
            pool_prep(pool, prep1)
            barrier(pool, "prep1")
            pool_att(pool, att1)
            barrier(pool, "att1")
            pool_proj(pool, wo1)
            barrier(pool, "wo1")
            pool_norm(pool, norms[2])
            pool_proj(pool, low_in)
            barrier(pool, "low_in")
            pool_up(pool, up2)
            barrier(pool, "up2")
            pool_proj(pool, low_down)
            barrier(pool, "low_down")
            pool_proj(pool, down2)
            barrier(pool, "down2")
            pool_qk2(pool, qk2)
            barrier(pool, "qk2")
            barrier(pool, "rms2")
            pool_att2(pool, att2)
            pool_up(pool, up3, True)
            barrier(pool, "att2")
            pool_norm(pool, norms[3])
            pool_up(pool, up3)
            pool_proj(pool, down3, True)
            barrier(pool, "up3")
            pool_proj(pool, down3)
            barrier(pool, "down3")
            pool_proj(pool, in3)
            barrier(pool, "in3")
            pool_prep(pool, prep3)
            barrier(pool, "prep3")
            pool_att(pool, att3)
            barrier(pool, "att3")
            pool_proj(pool, wo3)
            barrier(pool, "wo3")
            barrier(pool, "end")


def kernel(**inputs):
    import concourse.bacc as bacc
    from concourse.bass_utils import run_bass_kernel_spmd

    nc = bacc.Bacc("TRN2", target_bir_lowering=False, num_devices=1)
    arrays, t = {}, {}
    cst, shift = constants()
    for name, a in (*inputs.items(), ("cst", cst), ("shift", shift)):
        arrays[f"in_{name}"] = a = np.ascontiguousarray(a)
        t[name] = nc.dram_tensor(f"in_{name}", a.shape, mybir.dt.from_np(a.dtype), kind="ExternalInput").ap()
    out = nc.dram_tensor("out", (BATCH, SEQ, D), F32, kind="ExternalOutput").ap()
    build(nc, t, out)
    return run_bass_kernel_spmd(nc, [arrays], core_ids=[0]).results[0]["out"]
```

```python
from contextlib import ExitStack

import numpy as np

import concourse.bass as bass
from concourse import mybir

P = 128
BATCH, SEQ, D = 4, 256, 512
TOK = BATCH * SEQ
HALF = 512
NH = TOK // HALF
KT = D // P
SLOTS = 4

HEADS, HD = 32, 16
HPC = P // HD
QC = HEADS // HPC
VW = HD + 1
KV1 = 8
PACK = 8
F0 = 1376
F3 = 1792
GROUPS_UP, GROUPS_DOWN = 4, 10
H2, HD2 = 32, 128
INNER2 = H2 * HD2
GRP2 = 4
LORA = 2.0
RANK = 16
LEAD = 3
LEAD_SCALE = 5
LEAD_LOAD = 6
LN_EPS, RMS_EPS = 1e-5, 1e-6
MASKED = -1e30

F32 = mybir.dt.float32
F32R = mybir.dt.float32r
BF16 = mybir.dt.bfloat16
I32 = mybir.dt.int32
ALU = mybir.AluOpType
ACT = mybir.ActivationFunctionType
AX = mybir.AxisListType

C_ID, C_MEAN, C_MEAN2, C_ROT0, C_ROT1 = 0, 128, 256, 384, 512
C_MASK = 640
C_COS0, C_SIN0, C_COS1, C_SIN1 = 776, 1032, 1288, 1544
C_IDX = 1800
C_PAIR = 1802
C_WIDTH = 1804


def constants():
    c = np.zeros((P, C_WIDTH), np.float32)
    c[:, C_ID:C_ID + P] = np.eye(P)
    c[:, C_MEAN:C_MEAN + P] = 1.0 / D
    c[:, C_MEAN2:C_MEAN2 + P] = 1.0 / INNER2
    for p in range(P):
        h, d = p - p % HD, p % HD
        if d < HD // 2:
            c[h + d + HD // 2, C_ROT0 + p] = -1.0
        else:
            c[h + d - HD // 2, C_ROT0 + p] = 1.0
        if d % 2 == 0:
            c[p + 1, C_ROT1 + p] = -1.0
        else:
            c[p - 1, C_ROT1 + p] = 1.0
    c[:, C_MASK:C_MASK + P] = np.where(np.arange(P)[:, None] >= np.arange(P)[None], 0.0, MASKED)
    c[np.arange(P), C_PAIR + np.arange(P) // HD % 2] = 1.0 / np.sqrt(np.float32(HD))
    freq = (1.0 / 10000.0 ** (np.arange(0, HD, 2, dtype=np.float32) / HD)).astype(np.float32)
    ang = np.outer(np.arange(SEQ, dtype=np.float32), freq).astype(np.float32)
    half = ang[:, np.arange(P) % (HD // 2)].T
    pair = ang[:, (np.arange(P) % HD) // 2].T
    c[:, C_COS0:C_COS0 + SEQ], c[:, C_SIN0:C_SIN0 + SEQ] = np.cos(half), np.sin(half)
    c[:, C_COS1:C_COS1 + SEQ], c[:, C_SIN1:C_SIN1 + SEQ] = np.cos(pair), np.sin(pair)
    c[:, C_IDX] = np.arange(P)
    shift = np.zeros((P, 1), np.int32)
    shift[:, 0] = (np.arange(P) % PACK) * (32 // PACK)
    return c, shift


class Signal:

    def __init__(self, sem):
        self.sem = sem
        self.count = 1

    def reserve(self, n):
        base = self.count
        self.count += n
        return base




class Stage:

    norm = None
    heads = None


def build(nc, t, out):
    ctx = ExitStack()
    with ctx:
        def sb(name, shape, dt=F32):
            return ctx.enter_context(nc.sbuf_tensor(name, shape, dt))

        signals = []

        def sig(name):
            signals.append(Signal(ctx.enter_context(nc.semaphore(name))))
            return signals[-1]

        cst = sb("cst", [P, C_WIDTH])
        shift = sb("shift", [P, 1], I32)
        ident = cst[:, C_ID:C_ID + P]
        ident16 = sb("ident16", [P, P], BF16)
        mask16 = sb("mask16", [P, P], BF16)
        eps = sb("eps", [P, 2])
        bias1 = sb("bias1", [P, QC + 2 + KT])
        bias3 = sb("bias3", [P, QC + 2 + KT])
        cols2 = sb("cols2", [P, 5, H2])
        bo2 = sb("bo2", [P, KT])
        b2s = sb("b2s", [P, SLOTS])
        wscale = sb("wscale", [P, 2, F3 // P, KT])
        wscale2 = sb("wscale2", [P, KT, F3 // P])
        xT = sb("xT", [P, KT, TOK])
        xn_hi = sb("xn_hi", [P, KT, TOK], F32R)
        xn_lo = sb("xn_lo", [P, KT, TOK], F32R)
        nat = sb("nat", [P, SLOTS, D])
        w_hi = sb("w_hi", [P, SLOTS, D], F32R)
        w_lo = sb("w_lo", [P, SLOTS, D], F32R)
        arena_at = nc.sbuf_base

        def arena(*tensors):
            with ExitStack() as own:
                made = [own.enter_context(nc.sbuf_tensor(n, s, *(dt or [F32]))) for n, s, *dt in tensors]
            assert nc.sbuf_base == arena_at
            return made

        F11, F14 = -(-F0 // P), F3 // P
        x_nat, = arena(("x_nat", [P, TOK // P, D]))
        cen, sq, inv = arena(("cen", [P, KT, TOK]), ("sq", [P, KT, TOK]), ("inv", [P, TOK]))
        ROWS_DOWN = slice(64, 64 + GROUPS_DOWN)
        h0_hi, h0_lo, sgf0, hot, hot_d, packed, zero, scale, deq, zero_d, scale_d = arena(
            ("h0_hi", [P, F11, TOK], F32R), ("h0_lo", [P, F11, TOK], F32R), ("sgf0", [P, 2, NH, HALF]),
            ("hot", [P, F0]), ("hot_d", [P, F0]), ("packed", [P, F0 // PACK], I32),
            ("zero", [P, F0]), ("scale", [P, F0]), ("deq", [P, 2, D]),
            ("zero_d", [P, D]), ("scale_d", [P, D]))
        _, _, tmp_down = arena(("h0", [P, F11, TOK]), ("h0_first", [P, F11 - 2, TOK]), ("tmp_down", [P, 2 * TOK]))
        h1_hi, h1_lo, sgf1 = arena(
            ("h1_hi", [P, F11, TOK], F32R), ("h1_lo", [P, F11, TOK], F32R), ("sgf1", [P, 2, NH, HALF]))
        h2_hi, h2_lo, sgf2, a13, a2, b2, _, b13 = arena(
            ("h2_hi", [P, F11, TOK], F32R), ("h2_lo", [P, F11, TOK], F32R), ("sgf2", [P, 2, NH, HALF]),
            ("a13", [RANK, 2, D]), ("a2", [RANK, F0]), ("b2", [RANK, D]), ("pad2", [P, 1696]), ("b13", [RANK, 2, F11 * P]))
        h3_hi, h3_lo, sgf3 = arena(
            ("h3_hi", [P, F14, TOK], F32R), ("h3_lo", [P, F14, TOK], F32R), ("sgf3", [P, 2, NH, HALF]))
        ST = 2 * HD
        STACK = P // ST
        PAIRS = HPC // 2
        WIDE = 64

        def rows_width(n_v):
            return TOK // P * n_v * HPC * VW + WIDE - VW

        at_k, km0_hi, km0_lo, at_rows, at_p, at_pt, at_on, at_small, q0_hi, q0_lo, qs0, ks0, qs1, ks1 = arena(
            ("at_k", [P, QC, TOK]), ("km0_hi", [P, 2, 2, HALF], F32R), ("km0_lo", [P, 2, 2, HALF], F32R),
            ("at_rows", [P, rows_width(QC)]), ("at_p", [P, 3, 512]), ("at_pt", [P, 2, 512]), ("at_on", [P, 2, 2, P]),
            ("at_small", [P, 64]), ("q0_hi", [P, HALF], F32R), ("q0_lo", [P, HALF], F32R),
            ("qs0", [P, PAIRS, HALF], F32R), ("ks0", [P, PAIRS, 2, HALF], F32R),
            ("qs1", [P, PAIRS, HALF], F32R), ("ks1", [P, PAIRS, 2, HALF], F32R))
        _, _, km0, _, _, _, _, _, _, _, at_q, at_v = arena(
            ("at_k2", [P, QC, TOK]), ("km0_hi2", [P, 2, 2, HALF]), ("km0", [P, 2, 2, HALF]),
            ("at_rows2", [P, rows_width(QC)]), ("at_p2", [P, 3, 512]), ("at_pt2", [P, 2, 512]), ("at_on2", [P, 2, 2, P]),
            ("at_small2", [P, 64]), ("q0", [P, 2, HALF]), ("slot0", [P, 3, PAIRS, HALF]), ("at_q", [P, QC, TOK]), ("at_v", [P, QC, TOK]))
        unit_qs, unit_ks = (qs0, qs1), (ks0, ks1)
        st_hi, st_q, st_qs, st_ks, st_rows, st_p, st_pt, st_on, st_small = arena(
            ("st_hi", [P, QC, TOK], F32R), ("st_q", [P, QC, TOK]), ("st_qs", [P, 2, QC, PAIRS, SEQ], F32R),
            ("st_ks", [P, PAIRS, 2, TOK], F32R), ("st_rows", [P, rows_width(1)]),
            ("st_p", [P, 3, 512]), ("st_pt", [P, 2, 512]), ("st_on", [P, 2, 2, P]), ("st_small", [P, 64]))
        _, st_lo, _, st_k, km_hi, km_lo, _, _, _, _, st_v = arena(
            ("st_hi2", [P, QC, TOK], F32R), ("st_lo", [P, QC, TOK], F32R), ("st_slot0", [P, QC, PAIRS, SEQ]),
            ("st_k", [P, 1, TOK]), ("km_hi", [P, 2, HALF], F32R), ("km_lo", [P, 2, HALF], F32R), ("st_pad", [P, TOK]),
            ("st_ks2", [P, PAIRS, 2, TOK], F32R), ("st_rows2", [P, rows_width(1)]),
            ("st_p2", [P, 3, 512]), ("st_v", [P, 1, TOK]))
        km = (km_hi, km_lo), (xn_hi[:, 0, :].rearrange("p (i t) -> p i t", i=2), xn_lo[:, 0, :].rearrange("p (i t) -> p i t", i=2))
        heads0, heads1 = Stage(), Stage()
        for x, n_k, made in ((heads0, QC, (at_q, at_k, at_v, at_rows, at_p, at_pt, at_on, at_small, xn_hi, xn_lo)),
                             (heads1, 1, (st_q, st_k, st_v, st_rows, st_p, st_pt, st_on, st_small, st_hi, st_lo))):
            x.n_k = n_k
            x.q, x.k, x.v, x.rows, x.p, x.pt, x.on, x.small, x.hi, x.lo = made
            x.val = x.rows[:, 0:TOK // P * n_k * HPC * VW].rearrange("p (t c h d) -> p t c h d", c=n_k, h=HPC, d=VW)
        heads0.split_k = [(km0_hi[:, u, i, :], km0_lo[:, u, i, :], at_k[:, u, 0:HALF], i, u)
                          for u in range(2) for i in range(2)]
        heads1.split_k = [(km[half][0][:, i, :], km[half][1][:, i, :], st_k[:, 0, half * HALF:(half + 1) * HALF], i, half)
                          for half in range(NH) for i in range(2)]
        rms, ssq, raw2, sq2, rms_rows = arena(
            ("rms", [P, 2, TOK]), ("ssq", [P, 2, TOK]), ("raw2", [P, SLOTS, TOK]), ("sq2", [P, SLOTS, TOK]),
            ("rms_rows", [P, 2, TOK // P]))
        (rms_, qk_raw, qk_hi, qk_lo, val2, p2, pt2, bv2, o2_hi, o2_lo, wo_nat, wo_hi, wo_lo, small2) = arena(
            ("rms_", [P, 2, TOK]), ("qk_raw", [P, 2, 2, HALF]),
            ("qk_hi", [P, 2, 2, HALF], F32R), ("qk_lo", [P, 2, 2, HALF], F32R),
            ("val2", [P, NH, HALF // P, GRP2 * HD2]), ("p2", [P, 4, 2, SEQ]), ("pt2", [P, 2, 2, SEQ]),
            ("bv2", [P, GRP2]), ("o2_hi", [P, NH, GRP2, HALF], F32R), ("o2_lo", [P, NH, GRP2, HALF], F32R),
            ("wo_nat", [P, KT, GRP2 * P]), ("wo_hi", [P, KT, GRP2 * P], F32R), ("wo_lo", [P, KT, GRP2 * P], F32R),
            ("small2", [P, 4, 8]))
        bank = [ctx.enter_context(nc.psum_tensor(f"bank{i}", [P, 512], F32)) for i in range(8)]
        turn_bank = [bank[0], bank[1]]
        acc = [[bank[2], bank[3]], [bank[4], bank[5]]]
        qk_dram = nc.dram_tensor("qk_scratch", (H2, 2, P, TOK), F32).ap()

        phase = ctx.enter_context(nc.semaphore("phase"))
        begun = ctx.enter_context(nc.semaphore("begun"))
        x_in = sig("x_in")
        cst_in = sig("cst_in")
        tables_in = sig("tables_in")
        cols_in = sig("cols_in")
        adapters_in = [sig("adapters13_in"), sig("adapters2_in")]
        adapters_scaled = sig("adapters_scaled")
        cleared = sig("cleared")
        loaded = [sig(f"loaded{j}") for j in range(SLOTS)]
        scaled = sig("scaled")
        turned = sig("turned")
        unpacked = sig("unpacked")
        centred = sig("centred")
        dequant = sig("dequant")
        hi = sig("hi")
        lo = sig("lo")
        half0 = sig("half0")
        used = sig("used")
        gate_read = sig("gate_read")
        up_read = sig("up_read")
        h_hi_done = sig("h_hi_done")
        h_lo_done = sig("h_lo_done")
        out_read = sig("out_read")
        step_a = sig("step_a")
        step_b = sig("step_b")
        step_c = sig("step_c")
        step_d = sig("step_d")
        step_e = sig("step_e")
        io = sig("io")
        s_ready = sig("s_ready")
        max_done = sig("max_done")
        exp_done = sig("exp_done")
        pt_ready = sig("pt_ready")
        pt_copied = sig("pt_copied")
        pv_done = sig("pv_done")
        o_normed = sig("o_normed")
        ot_ready = sig("ot_ready")
        ot_hi = sig("ot_hi")
        ot_lo = sig("ot_lo")
        stored = [sig(f"stored{j}") for j in range(SLOTS)]
        split_hi = sig("split_hi")
        k_split = sig("k_split")
        unit_split = sig("unit_split")
        q_split = [sig("q_split_dve"), sig("q_split_pool")]
        stack_in = [[sig(f"stack{slot}_{pair}_in") for pair in range(HPC // 2)] for slot in range(2)]
        norm_done = sig("norm_done")
        xn_done = [sig("xn0_done"), sig("xn1_done")]
        v_ready = sig("v_ready")
        v_copied = sig("v_copied")
        small = sig("small")
        sq_done = sig("sq_done")
        raw_done = [sig("raw_q_done"), sig("raw_k_done")]
        ssq_done = sig("ssq_done")
        qk_in = [sig(f"qk_in{j}") for j in range(2)]
        v_half = sig("v_half")
        wo_in = [sig(f"wo_in{j}") for j in range(KT)]
        wo_hi_done = sig("wo_hi_done")
        wo_lo_done = sig("wo_lo_done")
        wo_done = sig("wo_done")
        qk_scaled = sig("qk_scaled")
        qk_hi_done = sig("qk_hi_done")
        qk_lo_done = sig("qk_lo_done")
        bias_in = sig("bias_in")
        o_hi_done = sig("o_hi_done")
        o_lo_done = sig("o_lo_done")

        def loop(eng, n, body):
            if n > 2:
                with eng.Fori(0, n) as it:
                    body(it)
            else:
                for it in range(n):
                    body(it)

        STAGES = ["start", "up0", "down0", "in0", "prep0", "att0", "wo0",
                  "up1", "down1", "in1", "prep1", "att1", "wo1",
                  "up2", "down2", "qk2", "rms2", "att2",
                  "up3", "down3", "in3", "prep3", "att3", "wo3", "end"]

        def barrier(eng, stage):
            eng.drain().then_inc(phase, 1)
            eng.wait_ge(phase, 4 * (STAGES.index(stage) + 1))

        def join(sp, stage):
            sp.wait_ge(phase, 4 * (STAGES.index(stage) + 1))

        def bcast(ap, n):
            return ap.unsqueeze(1).broadcast_to([ap.shape[0], n, ap.shape[1]])

        def tail_bcast(ap, n):
            return ap.unsqueeze(2).broadcast_to([ap.shape[0], ap.shape[1], n])

        def at(half):
            return slice(half * HALF, (half + 1) * HALF)

        def plan_chunks(n, mode, per_slot):
            s = Stage()
            s.n, s.mode = n, mode
            s.lo0, s.hi0, s.used0 = lo.reserve(n), hi.reserve(n), used.reserve(n)
            s.turned0 = turned.reserve(n if mode != "direct" else 0)
            s.scaled0 = scaled.reserve(n if mode == "scaled" else 0)
            m = n if mode == "dequant" else 0
            s.un0, s.cen0, s.deq0 = unpacked.reserve(m), centred.reserve(m), dequant.reserve(m)
            dmas = per_slot if isinstance(per_slot, list) else [per_slot] * n
            s.dmas = dmas
            s.load0 = [loaded[j].reserve(16 * sum(dmas[j::SLOTS])) for j in range(SLOTS)]
            return s

        def loaded_count(s, i, j):
            if isinstance(i, int):
                return s.load0[j] + 16 * sum(s.dmas[j:i + 1:SLOTS])
            return s.load0[j] + 4 * s.dmas[j] * (i - j) + 16 * s.dmas[j]

        def before(i, n):
            return max(i - n + 1, 0) if isinstance(i, int) else i - n + 1

        def sp_slot(sp, s, i):
            if isinstance(i, int) and i < SLOTS or s.mode == "direct":
                sp.wait_ge(lo.sem, s.lo0 + before(i, SLOTS))
            elif s.mode == "dequant":
                sp.wait_ge(centred.sem, s.cen0 + before(i, SLOTS))
            else:
                sp.wait_ge(turned.sem, s.turned0 + before(i, SLOTS))

        def pool_scale(pool, s, i, j, w, factors):
            pool.wait_ge(loaded[j].sem, loaded_count(s, i, j))
            v = nat[:, j, 0:w].rearrange("p (k c) -> p k c", c=P)
            nc.gpsimd.tensor_tensor(v, v, tail_bcast(factors, P), ALU.mult).then_inc(scaled.sem, 1)

        def pe_turn(pe, s, i, j, views, adapter=None):
            if s.mode == "scaled":
                pe.wait_ge(scaled.sem, s.scaled0 + i + 1)
            else:
                pe.wait_ge(loaded[j].sem, loaded_count(s, i, j))
            pe.wait_ge(lo.sem, s.lo0 + before(i, 2))
            for k, v in enumerate(views):
                rows, width = v.shape[0], v.free_size()
                to = turn_bank[j % 2][0:width, k * P:k * P + rows]
                mm = nc.tensor.transpose(to, v, ident[0:rows, 0:rows])
                if adapter is not None:
                    a, b = adapter
                    mm = nc.tensor.matmul(to, a[k], b, start=False, stop=True, skip_group_check=True)
            mm.then_inc(turned.sem, 1)

        def pe_spread(pe, s, i, j, g, hots, tables, first, kts, cols):
            pe.wait_ge(dequant.sem, s.deq0 + before(i, 2))
            for k, (kt, rows) in enumerate(kts):
                for b, table in zip((turn_bank[j % 2], bank[6 + j % 2]), tables):
                    n = cols.stop - cols.start if isinstance(cols, slice) else P
                    mm = nc.tensor.matmul(b[0:rows, k * P:k * P + n], hots[g, first + kt * P:first + kt * P + rows],
                                          table[g, cols], start=True, stop=True)
            mm.then_inc(turned.sem, 1)

        def dve_dequant(dve, s, i, j, parts):
            dve.wait_ge(loaded[j].sem, loaded_count(s, i, j))
            for n, (r, c) in enumerate(parts):
                v = nat[r, j, c].bitcast(I32)
                ins = nc.vector.tensor_scalar(v, v, shift[r, 0:1], 15, ALU.logical_shift_right, ALU.bitwise_and)
            ins.then_inc(unpacked.sem, 1)
            dve.wait_ge(unpacked.sem, s.un0 + i + 1)
            dve.wait_ge(turned.sem, s.turned0 + i + 1)
            dve.wait_ge(lo.sem, s.lo0 + before(i, 2))
            for r, c in parts:
                ins = nc.vector.tensor_tensor(deq[r, j % 2, c], nat[r, j, c].bitcast(I32),
                                              turn_bank[j % 2][r, c], ALU.subtract)
            ins.then_inc(centred.sem, 1)
            dve.wait_ge(centred.sem, s.cen0 + i + 1)
            for r, c in parts:
                ins = nc.vector.tensor_tensor(deq[r, j % 2, c], deq[r, j % 2, c],
                                              bank[6 + j % 2][r, c], ALU.mult)
            ins.then_inc(dequant.sem, 1)

        def chunk_source(s, j):
            if s.mode == "direct":
                return nat[:, j, :]
            if s.mode == "dequant":
                return deq[:, j % 2, :]
            return turn_bank[j % 2]

        def act_hi(act, s, i, j, parts):
            if s.mode == "direct":
                act.wait_ge(loaded[j].sem, loaded_count(s, i, j))
                act.wait_ge(used.sem, s.used0 + before(i, SLOTS))
            elif s.mode == "dequant":
                act.wait_ge(dequant.sem, s.deq0 + i + 1)
            else:
                act.wait_ge(turned.sem, s.turned0 + i + 1)
            src = chunk_source(s, j)
            for r, c in parts:
                ins = nc.scalar.activation(w_hi[r, j, c], src[r, c], ACT.Copy)
            ins.then_inc(hi.sem, 1)

        def dve_lo(dve, s, i, j, parts):
            dve.wait_ge(hi.sem, s.hi0 + i + 1)
            src = chunk_source(s, j)
            for r, c in parts:
                ins = nc.vector.tensor_tensor(w_lo[r, j, c], src[r, c], w_hi[r, j, c].bitcast(F32), ALU.subtract)
            ins.then_inc(lo.sem, 1)

        def pe_chunk(pe, s, i, j, rows, rhs, to, first=True, last=True, norm=None):
            pe.wait_ge(lo.sem, s.lo0 + i + 1)
            for half in range(NH):
                for k, n in enumerate(rows):
                    if norm is not None:
                        pe.wait_ge(xn_done[half].sem, norm.xn0[half] + k + 1)
                    r_hi, r_lo = rhs(k, half)
                    for x, (w, r) in enumerate(((w_hi, r_hi), (w_hi, r_lo), (w_lo, r_hi))):
                        mm = nc.tensor.matmul(to[half][:, :], w[0:n, j, k * P:(k + 1) * P], r,
                                              start=first and k == 0 and x == 0,
                                              stop=last and k == len(rows) - 1 and x == 2)
                if last and half == 0:
                    mm.then_inc(half0.sem, 1)
            mm.then_inc(used.sem, 1)

        ALL = [(slice(0, P), slice(0, D))]

        def whole(nkt, last_rows=P):
            if last_rows == P:
                return [(slice(0, P), slice(0, nkt * P))]
            return [(slice(0, P), slice(0, (nkt - 1) * P)), (slice(0, last_rows), slice((nkt - 1) * P, nkt * P))]

        def xn(k, half):
            return xn_hi[:, k, at(half)], xn_lo[:, k, at(half)]

        x_rows = t["L0_attn_x"].rearrange("b s d -> (b s) d").rearrange("(n p) d -> p n d", p=P)
        out_rows = out.rearrange("b s d -> (b s) d").rearrange("(n p) d -> p n d", p=P)
        DUP = P // HD

        def sp_start(sp):
            def get(into, dst, src):
                sp.dma_start(dst, src, allow_slow_non_contiguous=True).then_inc(into.sem, 16)
                into.count += 16

            get(cst_in, cst[:, :], t["cst"])
            get(cst_in, shift[:, :], t["shift"])
            get(x_in, x_nat[:, :, :], x_rows)
            sp.wait_ge(cleared.sem, 2)
            for tables in (tables_gate, tables_up, tables_down):
                g = tables.rows
                get(tables_in, tables.hots[g, tables.first:tables.first + tables.n_in].bitcast(I32), t[f"L0_ffn_{tables.name}_g_idx"]
                    .rearrange("(o k) -> o k", o=1).broadcast_to([g.stop - g.start, tables.n_in]))
                get(tables_in, packed[g, 0:tables.width // PACK], t[f"L0_ffn_{tables.name}_qzeros"])
                get(tables_in, tables.scales[g, 0:tables.width], t[f"L0_ffn_{tables.name}_scales"])

        def sp_columns(sp):
            def get(dst, src):
                sp.dma_start(dst, src, allow_slow_non_contiguous=True).then_inc(cols_in.sem, 16)
                cols_in.count += 16

            b = t["L1_attn_b_qkv"]
            for kv in range(KV1):
                rows = slice(kv * HD, (kv + 1) * HD)
                get(bias1[rows, 0:QC], b[kv * QC * HD:(kv + 1) * QC * HD].rearrange("(c d) -> d c", d=HD))
            for n in range(2):
                get(bias1[:, QC + n:QC + n + 1], b[D + n * P:D + (n + 1) * P].rearrange("(d o) -> d o", o=1))
            get(bias1[:, QC + 2:], t["L1_attn_b_o"].rearrange("(c d) -> d c", d=P))
            get(bias3[:, 0:QC], t["L3_attn_wq_b"].rearrange("(c d) -> d c", d=P))
            for n, name in enumerate(("wk", "wv")):
                for r in range(DUP):
                    get(bias3[r * HD:(r + 1) * HD, QC + n:QC + n + 1],
                        t[f"L3_attn_{name}_b"].rearrange("(d o) -> d o", o=1))
            get(bias3[:, QC + 2:], t["L3_attn_wo_b"].rearrange("(c d) -> d c", d=P))
            for n, name in enumerate(("bq", "bk", "bv", "gq", "gk")):
                get(cols2[:, n, :], t[f"L2_attn_{name}"].rearrange("(h d) -> d h", d=P))
            get(bo2[:, :], t["L2_attn_bo"].rearrange("(c d) -> d c", d=P))
            for n, name in enumerate(("w1", "w3")):
                get(wscale[:, n, :, :], t[f"L3_ffn_{name}_scale"].rearrange("(o n) k -> o n k", o=1)
                    .broadcast_to([P, F14, KT]))
            get(wscale2[:, :, :], t["L3_ffn_w2_scale"].rearrange("(o n) k -> o n k", o=1)
                .broadcast_to([P, KT, F14]))

        def pe_start(pe, s):
            pe.wait_ge(cst_in.sem, cst_in.count)
            pe.wait_ge(x_in.sem, x_in.count)
            for half in range(NH):
                for k in range(KT):
                    n = KT * half + k
                    if n >= 2:
                        pe.wait_ge(out_read.sem, s.out0 + n - 1)
                    for j in range(4):
                        mm = nc.tensor.transpose(turn_bank[n % 2][:, j * P:(j + 1) * P],
                                                 x_nat[:, 4 * half + j, k * P:(k + 1) * P], ident)
                    mm.then_inc(step_a.sem, 1)

        def dve_start(dve):
            nc.vector.memset(eps[:, 0:1], LN_EPS)
            nc.vector.memset(eps[:, 1:2], RMS_EPS)
            for x in (hot, zero, scale):
                ins = nc.vector.memset(x[:, :], 0.0)
            ins.then_inc(cleared.sem, 1)
            dve.wait_ge(cst_in.sem, cst_in.count)
            dve.wait_ge(tables_in.sem, tables_in.count)
            dve_tables(dve, tables_gate)

        def act_start(act, s):
            act.wait_ge(cst_in.sem, cst_in.count)
            nc.scalar.activation(ident16[:, :], ident, ACT.Copy)
            nc.scalar.activation(mask16[:, :], cst[:, C_MASK:C_MASK + P], ACT.Copy)
            for half in range(NH):
                for k in range(KT):
                    n = KT * half + k
                    act.wait_ge(step_a.sem, s.a0 + n + 1)
                    nc.scalar.activation(xT[:, k, at(half)], turn_bank[n % 2][:, :], ACT.Copy).then_inc(out_read.sem, 1)

        def plan_start():
            s = Stage()
            s.out0, s.a0 = out_read.reserve(KT * NH), step_a.reserve(KT * NH)
            return s

        def pe_end(pe, s):
            for n in range(TOK // P):
                if n >= 2:
                    pe.wait_ge(out_read.sem, s.out0 + n - 1)
                for k in range(KT):
                    mm = nc.tensor.transpose(turn_bank[n % 2][:, k * P:(k + 1) * P],
                                             xT[:, k, n * P:(n + 1) * P], ident)
                mm.then_inc(step_a.sem, 1)

        def dve_end(dve, s):
            for n in range(TOK // P):
                dve.wait_ge(step_a.sem, s.a0 + n + 1)
                nc.vector.tensor_copy(x_nat[:, n, :], turn_bank[n % 2][:, :]).then_inc(out_read.sem, 1)

        def sp_end(sp, s):
            for n in range(TOK // P):
                sp.wait_ge(out_read.sem, s.out0 + n + 1)
                sp.dma_start(out_rows[:, n, :], x_nat[:, n, :]).then_inc(io.sem, 16)
            sp.wait_ge(io.sem, io.count + 16 * (TOK // P))

        def plan_end():
            s = Stage()
            s.out0, s.a0 = out_read.reserve(TOK // P), step_a.reserve(TOK // P)
            return s

        def plan_norm():
            s = Stage()
            s.a0, s.b0, s.c0, s.d0, s.e0 = (x.reserve(n) for x, n in (
                (step_a, 2 * NH), (step_b, NH * KT), (step_c, NH * (KT + 1)), (step_d, NH * (KT + 1)), (step_e, NH * KT)))
            s.xn0 = [x.reserve(KT) for x in xn_done]
            return s

        TILES = [(half, k) for half in range(NH) for k in range(KT)]

        def pe_norm(pe, s):
            mean = cst[:, C_MEAN:C_MEAN + P]
            for half in range(NH):
                for k in range(KT):
                    mm = nc.tensor.matmul(acc[0][half][:, :], mean, xT[:, k, at(half)], start=k == 0, stop=k == KT - 1)
                mm.then_inc(step_a.sem, 1)
            for n, (half, k) in enumerate(TILES):
                pe.wait_ge(step_c.sem, s.c0 + n + 1)
                mm = nc.tensor.matmul(acc[1][half][:, :], mean, sq[:, k, at(half)], start=k == 0, stop=k == KT - 1)
                if k == KT - 1:
                    mm.then_inc(step_a.sem, 1)

        def dve_norm(dve, s, before=None, opening=None):
            for half, k in TILES:
                dve.wait_ge(step_a.sem, s.a0 + half + 1)
                nc.vector.tensor_tensor(cen[:, k, at(half)], xT[:, k, at(half)], acc[0][half][:, :], ALU.subtract)\
                  .then_inc(step_b.sem, 1)
            if before:
                before()
            for half in range(NH):
                dve.wait_ge(step_c.sem, s.c0 + NH * KT + half + 1)
                nc.vector.reciprocal(inv[:, at(half)], inv[:, at(half)]).then_inc(step_d.sem, 1)
                dve.wait_ge(step_d.sem, s.d0 + (KT + 1) * half + 1)
                for k in range(KT):
                    nc.vector.tensor_tensor(cen[:, k, at(half)], cen[:, k, at(half)], inv[:, at(half)], ALU.mult)\
                      .then_inc(step_d.sem, 1)
                if half == 0:
                    if opening:
                        opening()
                    low_norm(dve, s, half)

        def low_norm(eng, s, half):
            for k in range(KT):
                eng.wait_ge(step_e.sem, s.e0 + KT * half + k + 1)
                (nc.vector, nc.gpsimd)[half].tensor_tensor(xn_lo[:, k, at(half)], cen[:, k, at(half)],
                                                           xn_hi[:, k, at(half)].bitcast(F32), ALU.subtract)\
                    .then_inc(xn_done[half].sem, 1)

        def act_norm(act, s, opening=None):
            for n, (half, k) in enumerate(TILES):
                act.wait_ge(step_b.sem, s.b0 + n + 1)
                nc.scalar.activation(sq[:, k, at(half)], cen[:, k, at(half)], ACT.Square).then_inc(step_c.sem, 1)
            for half in range(NH):
                act.wait_ge(step_a.sem, s.a0 + NH + half + 1)
                nc.scalar.activation(inv[:, at(half)], acc[1][half][:, :], ACT.Sqrt, bias=eps[:, 0:1])\
                  .then_inc(step_c.sem, 1)
            if opening:
                opening()
            for half, k in TILES:
                act.wait_ge(step_d.sem, s.d0 + (KT + 1) * half + k + 2)
                nc.scalar.activation(xn_hi[:, k, at(half)], cen[:, k, at(half)], ACT.Copy).then_inc(step_e.sem, 1)

        def pool_norm(pool, s):
            low_norm(pool, s, 1)

        def plan_up(width, mode, dmas, gate, up, h, sgf, spread=None, adapters=False, scales=None):
            nf = -(-width // P)
            s = plan_chunks(2 * nf, mode, dmas)
            s.nf, s.width, s.gate, s.up, s.h, s.sg, s.hf = nf, width, gate, up, h, sgf[:, 0], sgf[:, 1]
            s.spread, s.adapters, s.scales = spread, adapters, scales
            s.half00 = half0.reserve(2 * nf)
            s.gate0, s.up0 = gate_read.reserve(2 * nf), up_read.reserve(2 * nf)
            s.hhi0, s.hlo0 = h_hi_done.reserve(2 * nf), h_lo_done.reserve(2 * nf)
            s.rounds, s.tail = nf // 2, nf % 2
            return s

        def up_rounds(eng, s, ahead, work, opening, lead=LEAD):
            def step(i, j, at_h, more):
                if more:
                    ahead(i + lead, (j + lead) % SLOTS, at_h + (j + lead) // 2)
                work(i, j, at_h + j // 2)

            def body(it):
                for j in range(SLOTS):
                    step(4 * it + j, j, 2 * it, True)

            if opening:
                for j in range(lead):
                    ahead(j, j % SLOTS, j // 2)
                return
            rounds = s.rounds - (1 if lead <= LEAD else 2)
            loop(eng, rounds, body)
            for i in range(4 * rounds, s.n):
                step(i, i % SLOTS, i // 4 * 2, i + lead < s.n)

        def up_cols(s, ft):
            if isinstance(ft, int):
                return slice(ft * P, min((ft + 1) * P, s.width))
            return bass.ds(ft * P, P)

        def sp_up(sp, s, opening=False):
            def load(i, j, ft):
                sp_slot(sp, s, i)
                w = (s.gate, s.up)[j % 2]
                if s.mode == "dequant":
                    cols = up_cols(s, ft)
                    n = cols.stop - cols.start if isinstance(cols, slice) else P
                    words = P // PACK
                    v = nat[:, j, :].bitcast(I32).rearrange("p (k c) -> p k c", c=P)
                    for x in range(PACK):
                        sp.dma_start(v[x:P:PACK, :, 0:n], w.rearrange("(k r) c -> r k c", r=words)[:, :, cols])\
                          .then_inc(loaded[j].sem, 16)
                else:
                    rows = up_cols(s, ft)
                    n = rows.stop - rows.start if isinstance(rows, slice) else P
                    sp.dma_start(nat[0:n, j, :], w[rows, :]).then_inc(loaded[j].sem, 16)

            up_rounds(sp, s, load, lambda i, j, ft: None, opening, LEAD_LOAD)

        def pe_up(pe, s, opening=False):
            def ahead(i, j, ft):
                if s.mode == "dequant":
                    pe_spread(pe, s, i, j, slice(0, P), hot, (zero, scale), D * (j % 2), [(k, P) for k in range(KT)],
                              up_cols(s, ft))
                else:
                    adapter = None
                    if s.adapters:
                        pe.wait_ge(adapters_scaled.sem, 2)
                        adapter = ([a13[:, j % 2, k * P:(k + 1) * P] for k in range(KT)], b13[:, j % 2, bass.ds(ft * P, P)])
                    pe_turn(pe, s, i, j, [nat[:, j, k * P:(k + 1) * P] for k in range(KT)], adapter)

            def work(i, j, ft):
                pe.wait_ge((gate_read, up_read)[j % 2].sem, (s.gate0, s.up0)[j % 2] + 2 * ft)
                pe_chunk(pe, s, i, j, [P] * KT, xn, acc[j % 2], norm=s.norm if j == 0 else None)

            up_rounds(pe, s, ahead, work, opening)

        def act_up(act, s, opening=False):
            def work(i, j, ft):
                for half in range(NH):
                    if j % 2 == 0:
                        if half == 0:
                            act.wait_ge(half0.sem, s.half00 + i + 1)
                            act.wait_ge(up_read.sem, s.up0 + 2 * ft)
                        else:
                            act.wait_ge(used.sem, s.used0 + i + 1)
                        nc.scalar.activation(s.sg[:, half, :], acc[0][half][:, :], ACT.Silu).then_inc(gate_read.sem, 1)
                    else:
                        act.wait_ge(up_read.sem, s.up0 + 2 * ft + half + 1)
                        nc.scalar.activation(s.h[0][:, bass.ds(ft, 1), at(half)].rearrange("p o c -> p (o c)"),
                                             s.hf[:, half, :], ACT.Copy).then_inc(h_hi_done.sem, 1)

            up_rounds(act, s, lambda i, j, ft: act_hi(act, s, i, j, ALL), work, opening)

        def dve_up(dve, s, opening=False):
            def ahead(i, j, ft):
                if s.mode == "dequant":
                    dve_dequant(dve, s, i, j, ALL)
                dve_lo(dve, s, i, j, ALL)

            def work(i, j, ft):
                if j % 2 == 0:
                    return
                for half in range(NH):
                    if half == 0:
                        dve.wait_ge(half0.sem, s.half00 + i + 1)
                        dve.wait_ge(h_lo_done.sem, s.hlo0 + 2 * ft)
                    else:
                        dve.wait_ge(used.sem, s.used0 + i + 1)
                    dve.wait_ge(gate_read.sem, s.gate0 + 2 * ft + half + 1)
                    nc.vector.tensor_tensor(s.hf[:, half, :], s.sg[:, half, :], acc[1][half][:, :], ALU.mult)\
                      .then_inc(up_read.sem, 1)

            up_rounds(dve, s, ahead, work, opening)

        def pool_up(pool, s, opening=False):
            def ahead(i, j, ft):
                if s.scales is not None:
                    pool_scale(pool, s, i, j, D, s.scales[:, j % 2, bass.ds(ft, 1), :].rearrange("p o k -> p (o k)"))

            def work(i, j, ft):
                if j % 2 == 0:
                    return
                for half in range(NH):
                    pool.wait_ge(h_hi_done.sem, s.hhi0 + 2 * ft + half + 1)
                    o = [x[:, bass.ds(ft, 1), at(half)].rearrange("p o c -> p (o c)") for x in s.h]
                    nc.gpsimd.tensor_tensor(o[1], s.hf[:, half, :], o[0].bitcast(F32), ALU.subtract)\
                      .then_inc(h_lo_done.sem, 1)

            up_rounds(pool, s, ahead, work, opening, LEAD_SCALE)

        def plan_proj(chunks, mode, n_tiles, rhs, engine):
            s = plan_chunks(len(chunks), mode, [len(c["loads"]) for c in chunks])
            s.chunks, s.n_tiles, s.rhs, s.engine = chunks, n_tiles, rhs, engine
            s.half00 = half0.reserve(n_tiles)
            s.out0 = out_read.reserve(2 * n_tiles)
            return s

        def proj_order(s, ahead, work, opening, lead=LEAD):
            for i in range(min(lead, s.n)) if opening else ():
                ahead(i, i % SLOTS, s.chunks[i])
            for i in range(s.n) if not opening else ():
                if i + lead < s.n:
                    ahead(i + lead, (i + lead) % SLOTS, s.chunks[i + lead])
                work(i, i % SLOTS, s.chunks[i])

        def sp_proj(sp, s, opening=False):
            def load(i, j, c):
                sp_slot(sp, s, i)
                for dst, src in c["loads"]:
                    sp.dma_start(dst(j), src).then_inc(loaded[j].sem, 16)

            proj_order(s, load, lambda i, j, c: None, opening, LEAD_LOAD)

        def pe_proj(pe, s, opening=False):
            def ahead(i, j, c):
                if s.mode == "dequant":
                    pe_spread(pe, s, i, j, ROWS_DOWN, hot_d, (zero_d, scale_d), 0, c["kts"], c["cols"])
                elif s.mode != "direct":
                    if "adapter" in c:
                        pe.wait_ge(adapters_scaled.sem, 3)
                    pe_turn(pe, s, i, j, c["views"](j), c.get("adapter"))

            def work(i, j, c):
                if c["first"] and c["tile"] >= 2:
                    pe.wait_ge(out_read.sem, s.out0 + 2 * (c["tile"] - 1))
                pe_chunk(pe, s, i, j, c["rows"], lambda k, half: s.rhs(c["k0"] + k, half, c["rows"][k]),
                         acc[c["tile"] % 2], c["first"], c["last"], s.norm if i == 0 else None)
                if s.heads and i >= 1:
                    pe_heads(pe, s, i - 1)

            proj_order(s, ahead, work, opening)
            if s.heads and not opening:
                pe_heads(pe, s, s.n - 1)

        def sums_ready(eng, s, i, tile, half):
            if half == 0:
                eng.wait_ge(half0.sem, s.half00 + tile + 1)
            else:
                eng.wait_ge(used.sem, s.used0 + i + 1)

        def act_proj(act, s, opening=False):
            def work(i, j, c):
                if s.engine != "act" or not c["last"]:
                    return
                for half in range(NH):
                    sums_ready(act, s, i, c["tile"], half)
                    dst, b, factor = c["to"](half)
                    n = dst.shape[0]
                    nc.scalar.activation(dst, acc[c["tile"] % 2][half][0:n, :], ACT.Identity,
                                         bias=0.0 if b is None else b, scale=factor).then_inc(out_read.sem, 1)

                if s.heads and i >= 2:
                    act_heads(act, s, i - 2)

            proj_order(s, lambda i, j, c: act_hi(act, s, i, j, c["parts"]), work, opening)
            if s.heads and not opening:
                for i in (s.n - 2, s.n - 1):
                    act_heads(act, s, i)

        def dve_proj(dve, s, opening=False):
            def ahead(i, j, c):
                if s.mode == "dequant":
                    dve_dequant(dve, s, i, j, c["parts"])
                dve_lo(dve, s, i, j, c["parts"])

            def work(i, j, c):
                if s.heads and i >= 1:
                    dve_heads(dve, s, i - 1)
                if s.heads and i >= 2:
                    dve_split(dve, s.heads.split, s.heads.split.early[i - 2])
                if s.engine != "dve" or not c["last"]:
                    return
                for half in range(NH):
                    sums_ready(dve, s, i, c["tile"], half)
                    x = xT[:, c["tile"], at(half)]
                    a = acc[c["tile"] % 2][half][:, :]
                    if c.get("bias") is None:
                        ins = nc.vector.tensor_tensor(x, a, x, ALU.add)
                    else:
                        ins = nc.vector.scalar_tensor_tensor(x, a, c["bias"], x, ALU.add, ALU.add)
                    ins.then_inc(out_read.sem, 1)

            proj_order(s, ahead, work, opening)
            if s.heads and not opening:
                dve_heads(dve, s, s.n - 1)
                for i in (s.n - 2, s.n - 1):
                    dve_split(dve, s.heads.split, s.heads.split.early[i])

        def pool_proj(pool, s, opening=False):
            if s.mode == "scaled":
                proj_order(s, lambda i, j, c: pool_scale(pool, s, i, j, len(c["rows"]) * P, c["scales"]),
                           lambda i, j, c: None, opening, LEAD_SCALE)
            if s.heads and not opening:
                pool_heads(pool, s)

        def nat_views(n, rows=P, last=P):
            return lambda j: [nat[0:rows, j, k * P:k * P + (P if k < n - 1 else last)] for k in range(n)]

        def slot(*index):
            return lambda j: nat[(index[0], j) + tuple(index[1:])]

        def rows_chunk(w, r0, k0=0, **more):
            return dict(loads=[(slot(slice(0, P), slice(0, D)), w[r0:r0 + P, :])], parts=ALL, rows=[P] * KT,
                        views=nat_views(KT), first=True, last=True, k0=k0, **more)

        def split_kts(nf):
            q = -(-nf // 4)
            return [list(range(a, min(a + q, nf))) for a in range(0, nf, q)]

        def h_of(h):
            return lambda k, half, rows: (h[0][0:rows, k, at(half)], h[1][0:rows, k, at(half)])

        def down_chunks(w, width, scales=None, adapter=None):
            found = []
            nf = -(-width // P)
            for m in range(-(-w.shape[0] // P)):
                for kts in split_kts(nf):
                    a, b = kts[0] * P, min((kts[-1] + 1) * P, width)
                    last = b - kts[-1] * P
                    n = len(kts)
                    r = min(P, w.shape[0] - m * P)
                    c = dict(loads=[(slot(slice(0, r), slice(0, b - a)), w[m * P:m * P + r, a:b])],
                             parts=whole(n, last), rows=[P] * (n - 1) + [last], views=nat_views(n, last=last),
                             first=a == 0, last=b == width, k0=kts[0], tile=m)
                    if scales is not None:
                        c["scales"] = scales[:, m, kts[0]:kts[0] + n]
                    if adapter is not None:
                        c["adapter"] = ([adapter[0][:, k * P:min((k + 1) * P, width)] for k in kts],
                                        adapter[1][:, m * P:(m + 1) * P])
                    found.append(c)
            return found

        def packed_down_chunks(w, width):
            found = []
            nf = -(-width // P)
            words = P // PACK
            for m in range(KT):
                for kts in split_kts(nf):
                    n = len(kts)
                    last = min(P, width - kts[-1] * P)
                    loads = []
                    for x in range(PACK):
                        for k0, n_k, rows in ((0, n if last == P else n - 1, P), (n - 1, 1 if last < P else 0, last)):
                            if n_k:
                                r0 = (kts[0] + k0) * words
                                r1 = r0 + n_k * words if rows == P else r0 + rows // PACK
                                dst = (lambda j, x=x, k0=k0, n_k=n_k, rows=rows:
                                       nat[x:rows:PACK, j, k0 * P:(k0 + n_k) * P].bitcast(I32)
                                       .rearrange("r (k c) -> r k c", c=P))
                                src = w[r0:r1, m * P:(m + 1) * P].rearrange("(k r) c -> r k c", k=n_k)
                                loads.append((dst, src))
                    found.append(dict(loads=loads, parts=whole(n, last), rows=[P] * (n - 1) + [last],
                                      kts=[(k, P if k < kts[-1] else last) for k in kts],
                                      cols=slice(m * P, (m + 1) * P), first=kts[0] == 0,
                                      last=kts[-1] == nf - 1, k0=kts[0], tile=m))
            return found

        def dve_tables(dve, s):

            def chain(ins):
                s.count += 1
                ins.then_inc(step_b.sem, 1)
                dve.wait_ge(step_b.sem, s.count)

            g, n_in, width = s.rows, s.n_in, s.width
            h, n = s.hots[g, s.first:s.first + n_in], s.tmp[g, 0:n_in]
            groups = g.stop - g.start
            chain(nc.vector.tensor_copy(h, h.bitcast(I32)))
            chain(nc.vector.tensor_scalar(n, h, 0.0, float(groups), ALU.is_lt, ALU.mult))
            chain(nc.vector.tensor_tensor(h, h, n, ALU.add))
            chain(nc.vector.tensor_scalar(h, h, 0.0, groups - 1.0, ALU.max, ALU.min))
            chain(nc.vector.tensor_scalar(n, h, cst[g, C_IDX:C_IDX + 1], float(-g.start), ALU.subtract, ALU.subtract))
            chain(nc.vector.tensor_scalar(h, n, 0.0, None, ALU.is_equal))
            z = s.zeros[g, 0:width]
            for x in range(PACK):
                zi = z.bitcast(I32).rearrange("p (n x) -> p n x", x=PACK)[:, :, x]
                chain(nc.vector.tensor_scalar(zi, packed[g, 0:width // PACK], 32 // PACK * x, 15,
                                              ALU.logical_shift_right, ALU.bitwise_and))
            chain(nc.vector.tensor_scalar(z, z.bitcast(I32), 1.0, None, ALU.add))

        def plan_tables(rows, name, hots, first, n_in, width, tmp, zeros=zero, scales=scale):
            s = Stage()
            s.rows, s.name, s.hots, s.first, s.n_in, s.width, s.tmp = rows, name, hots, first, n_in, width, tmp
            s.zeros, s.scales = zeros, scales
            s.count = step_b.reserve(7 + PACK)
            s.done = step_b.count
            return s

        def plan_heads(proj, m, rope):
            s = Stage()
            s.m, s.rope = m, rope
            s.chunks = [(m.k, c) for c in range(m.n_k)] + [(m.q, c) for c in range(QC)] + [(m.v, c) for c in range(m.n_k)]
            s.turned = (m.n_k + QC) * NH if rope else 0
            s.a0, s.b0, s.c0, s.d0 = (x.reserve(s.turned) for x in (step_a, step_b, step_c, step_d))
            s.vr0, s.vc0 = v_ready.reserve(NH * m.n_k), v_copied.reserve(NH * m.n_k)
            proj.heads = s
            return s

        def pe_heads(pe, proj, i):
            s = proj.heads
            x, c = s.chunks[i]
            for half in range(NH):
                if x is s.m.v:
                    n = NH * c + half
                    pe.wait_ge(out_read.sem, proj.out0 + NH * i + half + 1)
                    if n >= 2:
                        pe.wait_ge(v_copied.sem, s.vc0 + n - 1)
                    elif s.rope:
                        pe.wait_ge(step_b.sem, s.b0 + s.turned)
                    for j in range(4):
                        tt = 4 * half + j
                        mm = nc.tensor.transpose(bank[6 + n % 2][:, j * P:(j + 1) * P], x[:, c, tt * P:(tt + 1) * P], ident)
                    mm.then_inc(v_ready.sem, 1)
                elif s.rope:
                    n = NH * i + half
                    pe.wait_ge(out_read.sem, proj.out0 + n + 1)
                    if n >= 2:
                        pe.wait_ge(step_b.sem, s.b0 + n - 1)
                    r = s.rope[2]
                    nc.tensor.matmul(bank[6 + n % 2][:, :], cst[:, r:r + P], x[:, c, at(half)], start=True, stop=True)\
                      .then_inc(step_a.sem, 1)

        def act_heads(act, proj, i):
            s = proj.heads
            if s.split.early[i]:
                if s.rope:
                    act.wait_ge(step_d.sem, s.d0 + NH * (i + 1))
                else:
                    act.wait_ge(out_read.sem, proj.out0 + NH * (i + 1))
                act_split(act, s.split, s.split.early[i])

        def seqs(ap):
            return ap.rearrange("p (b s) -> p b s", s=SEQ)

        def dve_heads(dve, proj, i):
            s = proj.heads
            x, c = s.chunks[i]
            for half in range(NH):
                if x is s.m.v:
                    n = NH * c + half
                    dve.wait_ge(v_ready.sem, s.vr0 + n + 1)
                    tt = 4 * half
                    nc.vector.tensor_copy(s.m.val[:, tt:tt + 4, c, :, 0:HD],
                                          bank[6 + n % 2][:, :].rearrange("p (t h d) -> p t h d", t=4, h=HPC))\
                      .then_inc(v_copied.sem, 1)
                elif s.rope:
                    n = NH * i + half
                    rot = seqs(s.m.p[:, n % 2, :])
                    dve.wait_ge(step_a.sem, s.a0 + n + 1)
                    if n >= 2:
                        dve.wait_ge(step_d.sem, s.d0 + n - 1)
                    nc.vector.tensor_tensor(rot, seqs(bank[6 + n % 2][:, :]),
                                            bcast(cst[:, s.rope[1]:s.rope[1] + SEQ], 2), ALU.mult).then_inc(step_b.sem, 1)
                    dve.wait_ge(step_b.sem, s.b0 + n + 1)
                    dve.wait_ge(step_c.sem, s.c0 + n + 1)
                    nc.vector.tensor_tensor(seqs(x[:, c, at(half)]), seqs(x[:, c, at(half)]), rot, ALU.add)\
                      .then_inc(step_d.sem, 1)

        def pool_heads(pool, proj):
            s = proj.heads
            ones = s.m.rows[:, 0:TOK // P * s.m.n_k * HPC * VW].rearrange("p (r d) -> p r d", d=VW)
            nc.gpsimd.memset(s.m.rows[:, TOK // P * s.m.n_k * HPC * VW:], 0.0)
            nc.gpsimd.memset(ones[:, :, HD:VW], 1.0)
            for i, (x, c) in enumerate(s.chunks):
                for n in range(NH * i, min(NH * (i + 1), s.turned)):
                    pool.wait_ge(step_a.sem, s.a0 + n + 1)
                    v = seqs(x[:, c, at(n % NH)])
                    nc.gpsimd.tensor_tensor(v, v, bcast(cst[:, s.rope[0]:s.rope[0] + SEQ], 2), ALU.mult)\
                      .then_inc(step_c.sem, 1)
                if i >= 1:
                    pool_split(pool, s.split, s.split.early[i - 1])

        STEPS = 6
        ALL_STEPS = STEPS * QC

        CHUNKS = 2 * QC
        LOOP_STEPS = STEPS * CHUNKS
        UNITS = NH * QC

        def chunk_and_seq(s, c):
            return (c // 2, c % 2) if s.m is heads0 else (c % QC, c // QC)

        def plan_att(m, split):
            s = Stage()
            n = BATCH * ALL_STEPS
            s.m, s.split = m, split
            s.sr, s.mx, s.ex, s.pr, s.pc, s.pv = (x.reserve(n) for x in (
                s_ready, max_done, exp_done, pt_ready, pt_copied, pv_done))
            s.on, s.tr, s.th, s.tl, s.sm = (x.reserve(BATCH * QC) for x in (o_normed, ot_ready, ot_hi, ot_lo, small))
            if m is heads0:
                s.loads = (2 * STACK, 2 * STACK)
                s.per = 2 * 2 * STACK
                s.u0 = unit_split.reserve(3 * (UNITS - 2))
            else:
                s.loads = (2 * STACK, 2 * STACK)
                s.per = STACK
            total = [UNITS // 2 * n if m is heads0 else n + s.per for n in s.loads]
            s.si = [[x.reserve(16 * n) for x in stack_in[slot]] for slot, n in enumerate(total)]
            return s

        def sp_stack(sp, s, slot, stacks, parts, pair):
            rows = slice(pair * ST, (pair + 1) * ST)
            for x in range(STACK):
                sp.dma_start(stacks[x * ST:(x + 1) * ST].bitcast(F32), parts[x][rows].bitcast(F32))\
                  .then_inc(stack_in[slot][pair].sem, 16)

        def sp_q_split(sp, s, tiles):
            f = s.split
            sp.wait_ge(split_hi.sem, f.hi0 + max(f.order.index(n) for n in tiles) + 1)
            for x in range(2):
                mine = [n for n in f.order if n in range(x, len(SPLIT_Q), 2)]
                if any(n in mine for n in tiles):
                    sp.wait_ge(q_split[x].sem, f.q0[x] + max(mine.index(n) for n in tiles if n in mine) + 1)

        def sp_k_split(sp, s, tile):
            f = s.split
            sp.wait_ge(split_hi.sem, f.hi0 + f.order.index(("k", 2 * tile + 1)) + 1)
            sp.wait_ge(k_split.sem, f.k0 + 2 * (tile + 1))

        def sp_units(sp, s):
            f = s.split
            for u in range(UNITS):
                slot = u % 2
                if u < 2:
                    sp_k_split(sp, s, u)
                else:
                    sp.wait_ge(unit_split.sem, s.u0 + 3 * (u - 1))
                if u == 1:
                    sp.wait_ge(v_ready.sem, f.heads_in.vr0 + 2 * QC)
                sp_q_split(sp, s, range(len(SPLIT_Q)) if u == 1 else [u])
                if u >= 2:
                    sp.wait_ge(s_ready.sem, s.sr + 2 * STEPS * (u - 1))
                kh, kl = km0_hi[:, slot], km0_lo[:, slot]
                _, qh, ql = q_parts(f, u)
                for pair in range(PAIRS):
                    sp_stack(sp, s, slot, unit_ks[slot][:, pair], (kh, kh, kl, kl), pair)
                    sp_stack(sp, s, slot, unit_qs[slot][:, pair], (qh, ql, qh, ql), pair)

        def pool_units(pool, s):
            for u in range(2, UNITS):
                half, c = divmod(u, QC)
                slot = u % 2
                for pair in range(PAIRS):
                    pool.wait_ge(stack_in[slot][pair].sem, s.si[slot][pair] + 16 * 2 * STACK * (u // 2))
                n = s.u0 + 3 * (u - 2)
                nc.gpsimd.tensor_tensor(km0[:, slot], bcast(at_k[:, c, at(half)], 2),
                                        tail_bcast(cst[:, C_PAIR:C_PAIR + 2], HALF), ALU.mult).then_inc(unit_split.sem, 1)
                pool.wait_ge(unit_split.sem, n + 1)
                nc.gpsimd.tensor_copy(km0_hi[:, slot], km0[:, slot]).then_inc(unit_split.sem, 1)
                pool.wait_ge(unit_split.sem, n + 2)
                nc.gpsimd.tensor_tensor(km0_lo[:, slot], km0[:, slot], km0_hi[:, slot].bitcast(F32), ALU.subtract)\
                  .then_inc(unit_split.sem, 1)

        def sp_att(sp, s):
            def keys(half, pair):
                high, low = km[half]
                sp_stack(sp, s, half, st_ks[:, pair, :, at(half)], (high, high, low, low), pair)

            for b in range(BATCH):
                if b == 0:
                    sp_k_split(sp, s, 0)
                    for pair in range(PAIRS):
                        keys(0, pair)
                if b == 1:
                    sp_k_split(sp, s, 1)
                    for pair in range(PAIRS):
                        sp.wait_ge(stack_in[0][pair].sem, s.si[0][pair] + s.loads[0] * 16)
                    for pair in range(PAIRS):
                        keys(1, pair)
                if b >= 2:
                    sp.wait_ge(s_ready.sem, s.sr + ALL_STEPS * (b - 1))
                sp_q_split(sp, s, [n for n in range(len(SPLIT_Q)) if SPLIT_Q[n][1] == b * SEQ // HALF])
                qh, ql = (x[:, :, b * SEQ:(b + 1) * SEQ] for x in (s.m.hi, s.m.lo))
                for pair in range(PAIRS):
                    sp_stack(sp, s, b % 2, st_qs[:, b % 2, :, pair], (qh, ql, qh, ql), pair)

        SPLIT_Q = [(c, half) for half in range(NH) for c in range(QC)]

        def plan_split(heads):
            s = Stage()
            s.heads_in, s.m = heads, heads.m
            s.hi0 = split_hi.reserve(len(s.m.split_k) + len(SPLIT_Q))
            s.k0 = k_split.reserve(len(s.m.split_k))
            s.q0 = [x.reserve(len(SPLIT_Q) // 2) for x in q_split]
            q = list(range(len(SPLIT_Q)))
            if s.m is heads0:
                s.early = [[("k", 0), ("k", 1)], [("k", 2), ("k", 3)]] + [[]] * (QC - 2) + [[0]] + [[]] * (2 * QC - 1)
                s.late = q[1:]
            else:
                s.early = [[("k", 0), ("k", 1)]] + [[c, QC + c] for c in range(QC)] + [[]]
                s.late = [("k", 2), ("k", 3)]
            s.order = [x for chunk in s.early for x in chunk] + s.late
            heads.split = s
            return s

        def q_parts(s, n):
            c, half = SPLIT_Q[n]
            hi, lo = s.m.hi[:, c, at(half)], s.m.lo[:, c, at(half)]
            if s.m is heads0 and n == 0:
                hi, lo = q0_hi[:, :], q0_lo[:, :]
            return s.m.q[:, c, at(half)], hi, lo

        def act_split(act, s, parts):
            for x in parts:
                if x in range(len(SPLIT_Q)):
                    q, hi, lo = q_parts(s, x)
                    ins = nc.scalar.activation(hi, q, ACT.Copy)
                else:
                    high, low, k, i, tile = s.m.split_k[x[1]]
                    ins = nc.scalar.activation(high, k, ACT.Copy, scale=cst[:, C_PAIR + i:C_PAIR + i + 1])
                ins.then_inc(split_hi.sem, 1)

        def low_split(eng, e, s, n):
            q, hi, lo = q_parts(s, n)
            eng.wait_ge(split_hi.sem, s.hi0 + s.order.index(n) + 1)
            e.tensor_tensor(lo, q, hi.bitcast(F32), ALU.subtract).then_inc(q_split[n % 2].sem, 1)

        def dve_split(dve, s, parts):
            for x in parts:
                if x in range(len(SPLIT_Q)):
                    if x % 2 == 0:
                        low_split(dve, nc.vector, s, x)
                else:
                    high, low, k, i, tile = s.m.split_k[x[1]]
                    dve.wait_ge(split_hi.sem, s.hi0 + s.order.index(x) + 1)
                    nc.vector.scalar_tensor_tensor(low, k, cst[:, C_PAIR + i:C_PAIR + i + 1], high.bitcast(F32),
                                                   ALU.mult, ALU.subtract).then_inc(k_split.sem, 1)

        def pool_split(pool, s, parts):
            for x in parts:
                if x in range(1, len(SPLIT_Q), 2):
                    low_split(pool, nc.gpsimd, s, x)

        def step_heads(part):
            return (0, 4 * part, 4) if part < 2 else (1, 2 * (part - 2), 2)

        def att_loop(eng, s, body):
            with eng.Fori(0, BATCH // 2) as it:
                body(it)

        def seq_tokens(s, it, c):
            return bass.ds((2 * it + chunk_and_seq(s, c)[1]) * SEQ, SEQ)

        def pe_att(pe, s):
            def body(it):
                def scores(n):
                    c, part = divmod(n, STEPS)
                    qt, h, nh = step_heads(part)
                    if n >= 3:
                        pe.wait_ge(exp_done.sem, s.ex + LOOP_STEPS * it + n - 2)
                    o = bank[n % 3][:, :].rearrange("p (h k) -> p h k", h=nh)
                    keys = (qt + 1) * P
                    chunk, seq = chunk_and_seq(s, c)
                    first = seq == 0 if s.m is heads0 else chunk == 0
                    slot = chunk % 2 if s.m is heads0 else seq
                    unit = chunk // 2 if s.m is heads0 else 0
                    products = []
                    for pair in range(h // 2, (h + nh) // 2):
                        if first and part < 2:
                            pe.wait_ge(stack_in[slot][pair].sem,
                                       s.si[slot][pair] + 16 * s.loads[slot] * (unit + 1) + 16 * s.per * it)
                        if s.m is heads0:
                            queries = unit_qs[slot][:, pair, seq * SEQ + qt * P:seq * SEQ + (qt + 1) * P]
                            at_keys = unit_ks[slot][:, pair, :, seq * SEQ:seq * SEQ + keys]
                        else:
                            queries = st_qs[:, slot, chunk, pair, qt * P:(qt + 1) * P]
                            at_keys = st_ks[:, pair, :, bass.ds((2 * it + seq) * SEQ, keys)]
                        products.append((o[:, 2 * pair - h:2 * pair - h + 2, :], queries, at_keys))
                    for to, queries, at_keys in products:
                        nc.tensor.matmul(to, queries, at_keys, start=True, stop=False)
                        mm = nc.tensor.matmul(to[:, :, qt * P:keys], ident16[:, :], bcast(mask16[:, :], to.shape[1]),
                                              start=False, stop=True)
                    mm.then_inc(s_ready.sem, 1)

                def turns(n):
                    pe.wait_ge(exp_done.sem, s.ex + LOOP_STEPS * it + n + 1)
                    if n >= 2:
                        pe.wait_ge(pt_copied.sem, s.pc + LOOP_STEPS * it + n - 1)
                    for j in range(4):
                        mm = nc.tensor.transpose(bank[3 + n % 2][:, j * P:(j + 1) * P],
                                                 s.m.p[:, n % 3, j * P:(j + 1) * P], ident)
                    mm.then_inc(pt_ready.sem, 1)

                def values(n):
                    c, part = divmod(n, STEPS)
                    qt, h, nh = step_heads(part)
                    pe.wait_ge(pt_copied.sem, s.pc + LOOP_STEPS * it + n + 1)
                    if part == 0 and c >= 2:
                        pe.wait_ge(o_normed.sem, s.on + CHUNKS * it + c - 1)
                    chunk, seq = chunk_and_seq(s, c)
                    row = HPC * VW
                    for x in range(nh):
                        col = (qt * HPC + h + x) * VW
                        for kb in range(qt + 1):
                            j = x * (qt + 1) + kb
                            tile = 2 * (2 * it + seq) + kb
                            v_at = tile * (s.m.n_k * row) + (chunk % s.m.n_k * row + (h + x) * VW)
                            mm = nc.tensor.matmul(bank[5 + c % 2][:, col:col + WIDE], s.m.pt[:, n % 2, j * P:(j + 1) * P],
                                                  s.m.rows[:, bass.ds(v_at, WIDE)], start=kb == 0, stop=kb == qt)
                    mm.then_inc(pv_done.sem, 1)

                def turn_out(c):
                    pe.wait_ge(o_normed.sem, s.on + CHUNKS * it + c + 1)
                    pe.wait_ge(ot_lo.sem, s.tl + CHUNKS * it + c)
                    for qt in range(2):
                        mm = nc.tensor.transpose(bank[7][:, qt * P:(qt + 1) * P], s.m.on[:, c % 2, qt, :], ident)
                    mm.then_inc(ot_ready.sem, 1)

                scores(0)
                scores(1)
                for n in range(LOOP_STEPS):
                    if n + 2 < LOOP_STEPS:
                        scores(n + 2)
                    turns(n)
                    if n >= 1:
                        values(n - 1)
                    if n >= 8 and n % STEPS == 2:
                        turn_out(n // STEPS - 1)
                values(LOOP_STEPS - 1)
                turn_out(CHUNKS - 1)

            att_loop(pe, s, body)

        def dve_att(dve, s):
            def body(it):
                def top(n):
                    qt, h, nh = step_heads(n % STEPS)
                    dve.wait_ge(s_ready.sem, s.sr + LOOP_STEPS * it + n + 1)
                    nc.vector.tensor_reduce(s.m.small[:, 4 * (n % 3):4 * (n % 3) + nh],
                                            bank[n % 3][:, :].rearrange("p (h k) -> p h k", h=nh), AX.X, ALU.max,
                                            negate=True).then_inc(max_done.sem, 1)

                def copy(n):
                    dve.wait_ge(pt_ready.sem, s.pr + LOOP_STEPS * it + n + 1)
                    if n >= 2:
                        dve.wait_ge(pv_done.sem, s.pv + LOOP_STEPS * it + n - 1)
                    nc.vector.tensor_copy(s.m.pt[:, n % 2, :], bank[3 + n % 2][:, :]).then_inc(pt_copied.sem, 1)

                def norm(c):
                    dve.wait_ge(pv_done.sem, s.pv + LOOP_STEPS * it + STEPS * (c + 1))
                    o = bank[5 + c % 2][:, 0:2 * HPC * VW].rearrange("p (q h d) -> p q h d", q=2, h=HPC)
                    r = s.m.small[:, 16 + 16 * (c % 2):32 + 16 * (c % 2)].rearrange("p (q h o) -> p q h o", q=2, o=1)
                    nc.vector.reciprocal(r, o[:, :, :, HD:VW]).then_inc(small.sem, 1)
                    dve.wait_ge(small.sem, s.sm + CHUNKS * it + c + 1)
                    if c >= 2:
                        dve.wait_ge(ot_ready.sem, s.tr + CHUNKS * it + c - 1)
                    nc.vector.tensor_tensor(s.m.on[:, c % 2, :, :].rearrange("p q (h d) -> p q h d", d=HD),
                                            o[:, :, :, 0:HD], r.broadcast_to([P, 2, HPC, HD]), ALU.mult)\
                      .then_inc(o_normed.sem, 1)

                def low_part(c):
                    dve.wait_ge(ot_hi.sem, s.th + CHUNKS * it + c + 1)
                    nc.vector.tensor_tensor(s.m.lo[:, chunk_and_seq(s, c)[0], seq_tokens(s, it, c)], bank[7][:, 0:SEQ],
                                            s.m.hi[:, chunk_and_seq(s, c)[0], seq_tokens(s, it, c)].bitcast(F32), ALU.subtract)\
                      .then_inc(ot_lo.sem, 1)

                top(0)
                top(1)
                for n in range(LOOP_STEPS):
                    if n + 2 < LOOP_STEPS:
                        top(n + 2)
                    copy(n)
                    if n >= STEPS and n % STEPS == 0:
                        norm(n // STEPS - 1)
                    if n >= 9 and n % STEPS == 3:
                        low_part(n // STEPS - 1)
                norm(CHUNKS - 1)
                low_part(CHUNKS - 1)

            att_loop(dve, s, body)

        def act_att(act, s):
            def body(it):
                def high_part(c):
                    act.wait_ge(ot_ready.sem, s.tr + CHUNKS * it + c + 1)
                    nc.scalar.activation(s.m.hi[:, chunk_and_seq(s, c)[0], seq_tokens(s, it, c)], bank[7][:, 0:SEQ], ACT.Copy)\
                      .then_inc(ot_hi.sem, 1)

                for n in range(LOOP_STEPS):
                    qt, h, nh = step_heads(n % STEPS)
                    act.wait_ge(max_done.sem, s.mx + LOOP_STEPS * it + n + 1)
                    if n >= 3:
                        act.wait_ge(pt_ready.sem, s.pr + LOOP_STEPS * it + n - 2)
                    w = 512 // nh
                    for x in range(nh):
                        ins = nc.scalar.activation(s.m.p[:, n % 3, x * w:(x + 1) * w], bank[n % 3][:, x * w:(x + 1) * w],
                                                   ACT.Exp, bias=s.m.small[:, 4 * (n % 3) + x:4 * (n % 3) + x + 1])
                    ins.then_inc(exp_done.sem, 1)
                    if n >= 9 and n % STEPS == 3:
                        high_part(n // STEPS - 1)
                high_part(CHUNKS - 1)

            att_loop(act, s, body)

        def plan_qk2():
            s = plan_chunks(2 * H2, "direct", 1)
            n = 4 * H2
            s.half00, s.sq0, s.ssq0 = half0.reserve(2 * H2), sq_done.reserve(n), ssq_done.reserve(n + 1) + 1
            s.small0 = small.reserve(2 * H2)
            s.raw0 = [x.reserve(2 * H2) for x in raw_done]
            s.st0 = [x.reserve(16 * H2 // 2) for x in stored]
            s.rounds, s.tail = H2 // 2, 0
            return s

        def sp_qk2(sp, s, opening=False):
            def load(i, j, h):
                sp_slot(sp, s, i)
                w = t["L2_attn_W" + "qk"[j % 2]].rearrange("(k p) n -> p k n", p=P)
                sp.dma_start(nat[:, j, :].rearrange("p (k c) -> p k c", c=P), w[:, :, bass.ds(h * P, P)])\
                  .then_inc(loaded[j].sem, 16)

            def store(i, j, h):
                sp.wait_ge(raw_done[j % 2].sem, s.raw0[j % 2] + 2 * h + 2)
                sp.dma_start(qk_dram[bass.ds(h, 1), j % 2, :, :].rearrange("o p c -> (o p) c"), raw2[:, j, :])\
                  .then_inc(stored[j].sem, 16)

            up_rounds(sp, s, load, store, opening, LEAD_LOAD)
            for j in range(SLOTS) if not opening else ():
                sp.wait_ge(stored[j].sem, stored[j].count)

        def pe_qk2(pe, s, opening=False):
            def work(i, j, h):
                pe.wait_ge(raw_done[j % 2].sem, s.raw0[j % 2] + 2 * h)
                pe_chunk(pe, s, i, j, [P] * KT, xn, acc[j % 2])

            up_rounds(pe, s, lambda i, j, h: None, work, opening)

        def act_qk2(act, s, opening=False):
            def work(i, j, h):
                for half in range(NH):
                    if half == 0:
                        act.wait_ge(half0.sem, s.half00 + i + 1)
                        act.wait_ge(small.sem, s.small0 + i + 1)
                        act.wait_ge(ssq_done.sem, s.ssq0 + 2 * (i - j))
                    else:
                        act.wait_ge(used.sem, s.used0 + i + 1)
                    nc.scalar.activation(sq2[:, j, at(half)], acc[j % 2][half][:, :], ACT.Square,
                                         bias=b2s[:, j:j + 1]).then_inc(sq_done.sem, 1)

            up_rounds(act, s, lambda i, j, h: act_hi(act, s, i, j, ALL), work, opening)

        def dve_qk2(dve, s, opening=False):
            def ahead(i, j, h):
                nc.vector.tensor_scalar(b2s[:, j:j + 1], cols2[:, j % 2, bass.ds(h, 1)], 0.0, None, ALU.add)\
                  .then_inc(small.sem, 1)
                dve_lo(dve, s, i, j, ALL)

            def work(i, j, h):
                for half in range(NH):
                    dve.wait_ge(sq_done.sem, s.sq0 + 2 * i + half + 1)
                    if half == 0:
                        dve.wait_ge(stored[j].sem, s.st0[j] + 4 * (i - j))
                    nc.vector.tensor_scalar(raw2[:, j, at(half)], acc[j % 2][half][:, :],
                                            cols2[:, j % 2, bass.ds(h, 1)], cols2[:, 3 + j % 2, bass.ds(h, 1)],
                                            ALU.add, ALU.mult).then_inc(raw_done[j % 2].sem, 1)

            up_rounds(dve, s, ahead, work, opening)

        def pool_qk2(pool, s, opening=False):
            def work(i, j, h):
                for half in range(NH):
                    pool.wait_ge(sq_done.sem, s.sq0 + 2 * i + half + 1)
                    pool.wait_ge(ssq_done.sem, s.ssq0 + 2 * i + half)
                    v = ssq[:, j % 2, at(half)]
                    nc.gpsimd.tensor_tensor(v, v, sq2[:, j, at(half)], ALU.add).then_inc(ssq_done.sem, 1)

            if not opening:
                nc.gpsimd.memset(ssq[:, :, :], 0.0).then_inc(ssq_done.sem, 1)
            up_rounds(pool, s, lambda i, j, h: None, work, opening)

        PARTS = [(n, half) for n in range(2) for half in range(NH)]
        TT = HALF // P

        def plan_rms():
            s = Stage()
            s.a0, s.b0, s.c0 = step_a.reserve(2 * len(PARTS)), step_b.reserve(len(PARTS)), step_c.reserve(3)
            s.spread = [bank[0], bank[1], bank[6], bank[7]]
            return s

        def pe_rms(pe, s):
            for n, half in PARTS:
                for tt in range(TT):
                    x = half * HALF + tt * P
                    mm = nc.tensor.matmul(acc[n][half][:, tt:tt + 1], ssq[:, n, x:x + P], cst[:, C_MEAN2:C_MEAN2 + 1],
                                          start=True, stop=True)
                mm.then_inc(step_a.sem, 1)
            for x, (n, half) in enumerate(PARTS):
                if half == 0:
                    pe.wait_ge(step_c.sem, s.c0 + 2 + n)
                for tt in range(TT):
                    v = rms_rows[:, n, TT * half + tt:TT * half + tt + 1].broadcast_to([P, P])
                    mm = nc.tensor.matmul(s.spread[x][:, tt * P:(tt + 1) * P], v, ident, start=True, stop=True)
                mm.then_inc(step_a.sem, 1)

        def act_rms(act, s):
            for x, (n, half) in enumerate(PARTS):
                act.wait_ge(step_a.sem, s.a0 + x + 1)
                nc.scalar.activation(rms_rows[:, n, TT * half:TT * (half + 1)], acc[n][half][:, 0:TT], ACT.Sqrt,
                                     bias=eps[:, 1:2]).then_inc(step_b.sem, 1)

        def act_rms_spread(act, s):
            for x, (n, half) in enumerate(PARTS):
                if n == 1:
                    act.wait_ge(step_a.sem, s.a0 + len(PARTS) + x + 1)
                    nc.scalar.activation(rms[:, n, at(half)], s.spread[x][:, :], ACT.Copy)

        def dve_rms(dve, s):
            for m in range(KT):
                nc.vector.tensor_scalar(xT[:, m, :], xT[:, m, :], bo2[:, m:m + 1], None, ALU.add)
            q, k = rms_rows[:, 0, :], rms_rows[:, 1, :]
            dve.wait_ge(step_b.sem, s.b0 + 2)
            nc.vector.reciprocal(q, q).then_inc(step_c.sem, 1)
            dve.wait_ge(step_c.sem, s.c0 + 1)
            nc.vector.tensor_scalar(q, q, float(1.0 / np.sqrt(HD2)), None, ALU.mult).then_inc(step_c.sem, 1)
            dve.wait_ge(step_b.sem, s.b0 + 4)
            nc.vector.reciprocal(k, k).then_inc(step_c.sem, 1)

        def dve_rms_spread(dve, s):
            for x, (n, half) in enumerate(PARTS):
                if n == 0:
                    dve.wait_ge(step_a.sem, s.a0 + len(PARTS) + x + 1)
                    nc.vector.tensor_copy(rms[:, n, at(half)], s.spread[x][:, :])

        GSTEPS = GRP2 * BATCH
        HSTEPS = GSTEPS // NH
        GROUPS2 = H2 // GRP2
        WO_SPLIT = (5, 9, 11, 13)

        def plan_att2():
            s = plan_chunks(GROUPS2 * KT, "direct", 1)
            used.count -= GROUPS2 * KT
            n = GROUPS2 * GSTEPS
            s.n = n
            s.sr, s.mx, s.ex, s.nd, s.pr, s.pc, s.pv, s.sm, s.oh, s.ol = (x.reserve(n) for x in (
                s_ready, max_done, exp_done, norm_done, pt_ready, pt_copied, pv_done, small, o_hi_done, o_lo_done))
            s.bv = bias_in.reserve(GROUPS2)
            s.q = n // 2
            s.qi = [x.reserve(16 * s.q // 2) for x in qk_in]
            s.qs, s.qh, s.ql = (x.reserve(s.q) for x in (qk_scaled, qk_hi_done, qk_lo_done))
            s.v = GROUPS2 * NH * (HALF // P)
            s.vh, s.vr, s.vc = (x.reserve(s.v) for x in (v_half, v_ready, v_copied))
            s.o = GROUPS2 * NH * KT
            s.wd, s.out0 = wo_done.reserve(s.o), out_read.reserve(s.o)
            s.wi = [x.reserve(16 * GROUPS2) for x in wo_in]
            s.wh, s.wl = (x.reserve(GROUPS2 * KT) for x in (wo_hi_done, wo_lo_done))
            return s

        def real(i, n):
            return not isinstance(i, int) or 0 <= i < n

        def groups(eng, body):
            body(-1)
            body(0)
            with eng.Fori(0, GROUPS2 - 2) as it:
                body(it + 1)
            body(GROUPS2 - 1)
            body(GROUPS2)

        def place(n):
            n %= GSTEPS
            return n // HSTEPS, n % HSTEPS // 2, n % 2

        def wo_place(i):
            return i % (NH * KT) // KT, i % KT

        def sp_att2(sp, s):
            def load_wv(g):
                for k in range(KT):
                    sp.wait_ge(lo.sem, s.lo0 + KT * g - KT + k + 1 if not isinstance(g, int) or g > 0 else s.lo0)
                    sp.dma_start(nat[:, k, :], t["L2_attn_Wv"][k * P:(k + 1) * P, bass.ds(g * GRP2 * HD2, GRP2 * HD2)])\
                      .then_inc(loaded[k].sem, 16)

            def load_wo(g, m):
                if not isinstance(g, int) or g > 0:
                    sp.wait_ge(wo_lo_done.sem, s.wl + KT * (g - 1) + m + 1)
                sp.dma_start(wo_nat[:, m, :].rearrange("p (k c) -> p k c", c=P),
                             t["L2_attn_Wo"].rearrange("(h p) n -> p h n", p=P)
                             [:, bass.ds(GRP2 * g, GRP2), m * P:(m + 1) * P]).then_inc(wo_in[m].sem, 16)

            def load_qk(g, e):
                q = 8 * g + e
                if not isinstance(q, int) or q >= 2:
                    sp.wait_ge(qk_lo_done.sem, s.ql + q - 1)
                half, x, _ = place(2 * e)
                h = GRP2 * (g + e // 8) + x
                if isinstance(q, int) and q == 0:
                    sp.wait_ge(step_a.sem, rms2.a0 + len(PARTS))
                sp.dma_start(qk_raw[:, e % 2, :, :], qk_dram[bass.ds(h, 1), :, :, at(half)]
                             .rearrange("o n p c -> (o p) n c")).then_inc(qk_in[e % 2].sem, 16)

            def body(g):
                if real(g + 1, GROUPS2):
                    load_wv(g + 1)
                for e in range(8):
                    if real(8 * g + e + 2, s.q):
                        load_qk(g, e + 2)
                    if e == 0 and real(g, GROUPS2):
                        load_wo(g, 3)
                    if e == 6 and real(g + 1, GROUPS2):
                        load_wo(g + 1, 0)
                if real(g + 1, GROUPS2):
                    load_wo(g + 1, 1)
                    load_wo(g + 1, 2)

            groups(sp, body)

        def pe_att2(pe, s):
            def scores(g, n):
                i = GSTEPS * g + n
                _, x, b = place(n)
                if b == 0:
                    pe.wait_ge(qk_lo_done.sem, s.ql + 8 * g + n // 2 + 1)
                if real(i - 2, s.n):
                    pe.wait_ge(exp_done.sem, s.ex + i - 1)
                for qt in range(2):
                    q = slice(b * SEQ + qt * P, b * SEQ + (qt + 1) * P)
                    for y, (a, c) in enumerate(((qk_hi, qk_hi), (qk_hi, qk_lo), (qk_lo, qk_hi))):
                        mm = nc.tensor.matmul(bank[n % 2][:, qt * SEQ:(qt + 1) * SEQ], a[:, x % 2, 0, q],
                                              c[:, x % 2, 1, b * SEQ:(b + 1) * SEQ], start=y == 0, stop=y == 2)
                mm.then_inc(s_ready.sem, 1)

            def values(g, n):
                i = 8 * g + 4 + n // 2
                part = n % 2
                tt = i % 8 if isinstance(i, int) else (4 + n // 2) % 8
                if n in (8, 9):
                    pe.wait_ge(lo.sem, s.lo0 + KT * (g + 1) + 2 * part + 2)
                if part == 0 and real(i - 1, s.v):
                    pe.wait_ge(v_copied.sem, s.vc + i)
                for k in (2 * part, 2 * part + 1):
                    for y, (a, w) in enumerate(((xn_hi, w_hi), (xn_lo, w_hi), (xn_hi, w_lo))):
                        mm = nc.tensor.matmul(bank[3][:, :], a[:, k, tt * P:(tt + 1) * P], w[:, k, :],
                                              start=k == 0 and y == 0, stop=k == KT - 1 and y == 2)
                mm.then_inc((v_half, v_ready)[part].sem, 1)

            def turns(g, n):
                i = GSTEPS * g + n
                pe.wait_ge(norm_done.sem, s.nd + i + 1)
                if real(i - 1, s.n):
                    pe.wait_ge(pt_copied.sem, s.pc + i)
                for kb in range(2):
                    for qt in range(2):
                        mm = nc.tensor.transpose(bank[2][:, kb * SEQ + qt * P:kb * SEQ + (qt + 1) * P],
                                                 p2[:, n % 4, qt, kb * P:(kb + 1) * P], ident)
                mm.then_inc(pt_ready.sem, 1)

            def project(g, n):
                i = 8 * g - 5 + n // 2
                part = n % 2
                half, m = wo_place(3 + n // 2)
                if part == 0:
                    if real(i - 2, s.o):
                        pe.wait_ge(out_read.sem, s.out0 + i - 1)
                    if half == 0:
                        pe.wait_ge(wo_lo_done.sem, s.wl + KT * (g if n >= 10 else g - 1) + m + 1)
                if m == 0:
                    pe.wait_ge(o_lo_done.sem, s.ol + 2 * i + 4 * part + 4)
                for k in (2 * part, 2 * part + 1):
                    for y, (w, o) in enumerate(((wo_hi, o2_hi), (wo_hi, o2_lo), (wo_lo, o2_hi))):
                        mm = nc.tensor.matmul(bank[6 + m % 2][:, :], w[:, m, k * P:(k + 1) * P], o[:, half, k, :],
                                              start=k == 0 and y == 0, stop=k == GRP2 - 1 and y == 2)
                if part == 1:
                    mm.then_inc(wo_done.sem, 1)

            def outputs(g, n):
                i = GSTEPS * g + n
                half, x, b = place(n)
                pe.wait_ge(pt_copied.sem, s.pc + i + 1)
                if n % HSTEPS == 0:
                    pe.wait_ge(v_copied.sem, s.vc + 8 * g + 4 * half + 4)
                if real(i - 2, s.n):
                    pe.wait_ge(o_lo_done.sem, s.ol + i - 1)
                for kb in range(2):
                    mm = nc.tensor.matmul(bank[4 + n % 2][:, 0:SEQ], val2[:, half, 2 * b + kb, x * HD2:(x + 1) * HD2],
                                          pt2[:, n % 2, kb, :], start=kb == 0, stop=kb == 1)
                mm.then_inc(pv_done.sem, 1)

            def body(g):
                for n in range(GSTEPS):
                    i = GSTEPS * g + n
                    if real(i + 2, s.n):
                        scores(g + (n + 2) // GSTEPS, (n + 2) % GSTEPS)
                    if real(8 * g + 4 + n // 2, s.v):
                        values(g, n)
                    if real(i, s.n):
                        turns(g, n)
                    if real(8 * g - 5 + n // 2, s.o):
                        project(g, n)
                    if real(i - 1, s.n):
                        outputs(g + (n - 1) // GSTEPS, (n - 1) % GSTEPS)

            groups(pe, body)

        def act_att2(act, s, opening=False):
            def high_part(g, n):
                i = GSTEPS * g + n
                half, x, b = place(n)
                act.wait_ge(pv_done.sem, s.pv + i + 1)
                if n == 0:
                    act.wait_ge(bias_in.sem, s.bv + g + 1)
                if n % HSTEPS == 0 and real(2 * g + half - 2, 2 * GROUPS2):
                    act.wait_ge(wo_done.sem, s.wd + 8 * g + 4 * half - 4)
                nc.scalar.activation(o2_hi[:, half, x, b * SEQ:(b + 1) * SEQ], bank[4 + n % 2][:, 0:SEQ], ACT.Identity,
                                     bias=bv2[:, x:x + 1]).then_inc(o_hi_done.sem, 1)

            def split_qk(g, e):
                q = 8 * g + e
                act.wait_ge(qk_scaled.sem, s.qs + q + 1)
                if real(q - 2, s.q):
                    act.wait_ge(s_ready.sem, s.sr + 2 * q - 2)
                nc.scalar.activation(qk_hi[:, e % 2, :, :], qk_raw[:, e % 2, :, :], ACT.Copy).then_inc(qk_hi_done.sem, 1)

            def exps(g, n):
                i = GSTEPS * g + n
                act.wait_ge(max_done.sem, s.mx + i + 1)
                if real(i - 4, s.n):
                    act.wait_ge(pt_ready.sem, s.pr + i - 3)
                for qt in range(2):
                    ins = nc.scalar.activation(p2[:, n % 4, qt, :], bank[n % 2][:, qt * SEQ:(qt + 1) * SEQ], ACT.Exp,
                                               bias=small2[:, n % 4, qt:qt + 1], accum_out=small2[:, n % 4, 2 + qt:3 + qt])
                ins.then_inc(exp_done.sem, 1)

            def copy_values(g, n):
                i = 8 * g + 4 + n // 2
                tt = (4 + n // 2) % 8
                act.wait_ge(v_ready.sem, s.vr + i + 1)
                if tt % 4 == 0 and real(i - 8, s.v):
                    act.wait_ge(pv_done.sem, s.pv + 2 * i - 8)
                nc.scalar.activation(val2[:, tt // 4, tt % 4, :], bank[3][:, :], ACT.Copy).then_inc(v_copied.sem, 1)

            def split_wv(g, ks, done):
                for k in ks:
                    act.wait_ge(loaded[k].sem, s.load0[k] + 16 * g + 16)
                    if real(g - 1, GROUPS2):
                        act.wait_ge(*done)
                    else:
                        act.wait_ge(used.sem, s.used0)
                    nc.scalar.activation(w_hi[:, k, :], nat[:, k, :], ACT.Copy).then_inc(hi.sem, 1)

            def split_wo(g, m):
                act.wait_ge(wo_in[m].sem, s.wi[m] + 16 * g + 16)
                if real(g - 1, GROUPS2):
                    act.wait_ge(wo_done.sem, s.wd + 8 * g - 4 + m + 1)
                nc.scalar.activation(wo_hi[:, m, :], wo_nat[:, m, :], ACT.Copy).then_inc(wo_hi_done.sem, 1)

            def body(g):
                for n in range(GSTEPS):
                    i = GSTEPS * g + n
                    if real(i - 2, s.n):
                        high_part(g + (n - 2) // GSTEPS, (n - 2) % GSTEPS)
                    if n % 2 == 0 and real(8 * g + n // 2 + 2, s.q):
                        split_qk(g + (n // 2 + 2) // 8, (n // 2 + 2) % 8)
                    if n == 8 and real(g, GROUPS2 - 1):
                        split_wv(g + 1, (2, 3), (v_ready.sem, s.vr + 8 * g + 8))
                    if real(i + 2, s.n):
                        exps(g + (n + 2) // GSTEPS, (n + 2) % GSTEPS)
                    if n % 2 == 1 and real(8 * g + 4 + n // 2, s.v):
                        copy_values(g, n)
                    if n == 7 and real(g, GROUPS2 - 1):
                        split_wv(g + 1, (0, 1), (v_half.sem, s.vh + 8 * g + 8))
                    if n in WO_SPLIT and real(g, GROUPS2):
                        split_wo(g, WO_SPLIT.index(n))

            if opening:
                split_wv(0, range(KT), None)
                return
            groups(act, body)

        def dve_att2(dve, s, opening=False):
            def norm(g, n):
                i = GSTEPS * g + n
                dve.wait_ge(exp_done.sem, s.ex + i + 1)
                nc.vector.reciprocal(small2[:, n % 4, 4:6], small2[:, n % 4, 2:4]).then_inc(small.sem, 1)
                dve.wait_ge(small.sem, s.sm + i + 1)
                nc.vector.tensor_tensor(p2[:, n % 4, :, :], p2[:, n % 4, :, :], tail_bcast(small2[:, n % 4, 4:6], SEQ),
                                        ALU.mult).then_inc(norm_done.sem, 1)

            def top(g, n):
                dve.wait_ge(s_ready.sem, s.sr + GSTEPS * g + n + 1)
                nc.vector.tensor_reduce(small2[:, n % 4, 0:2], bank[n % 2][:, :].rearrange("p (q k) -> p q k", q=2),
                                        AX.X, ALU.max, negate=True).then_inc(max_done.sem, 1)

            def low_part(g, n):
                half, x, b = place(n)
                dve.wait_ge(o_hi_done.sem, s.oh + GSTEPS * g + n + 1)
                v = slice(b * SEQ, (b + 1) * SEQ)
                nc.vector.scalar_tensor_tensor(o2_lo[:, half, x, v], bank[4 + n % 2][:, 0:SEQ], bv2[:, x:x + 1],
                                               o2_hi[:, half, x, v].bitcast(F32), ALU.add, ALU.subtract)\
                  .then_inc(o_lo_done.sem, 1)

            def copy(g, n):
                i = GSTEPS * g + n
                dve.wait_ge(pt_ready.sem, s.pr + i + 1)
                if real(i - 2, s.n):
                    dve.wait_ge(pv_done.sem, s.pv + i - 1)
                nc.vector.tensor_copy(pt2[:, n % 2, :, :], bank[2][:, :].rearrange("p (k q) -> p k q", k=2))\
                  .then_inc(pt_copied.sem, 1)

            def add(g, n):
                half, m = wo_place(2 + n // 2)
                dve.wait_ge(wo_done.sem, s.wd + 8 * g - 6 + n // 2 + 1)
                nc.vector.tensor_tensor(xT[:, m, at(half)], bank[6 + m % 2][:, :], xT[:, m, at(half)], ALU.add)\
                  .then_inc(out_read.sem, 1)

            def split(hi_sem, count, hi_part, lo_part, src, lo_sem):
                dve.wait_ge(hi_sem, count)
                nc.vector.tensor_tensor(lo_part, src, hi_part.bitcast(F32), ALU.subtract).then_inc(lo_sem, 1)

            def split_wv(g, ks):
                for k in ks:
                    split(hi.sem, s.hi0 + KT * g + k + 1, w_hi[:, k, :], w_lo[:, k, :], nat[:, k, :], lo.sem)

            def body(g):
                for n in range(GSTEPS):
                    i = GSTEPS * g + n
                    if n == 2 and real(g, GROUPS2):
                        if real(g - 1, GROUPS2):
                            dve.wait_ge(o_lo_done.sem, s.ol + GSTEPS * g)
                        nc.vector.tensor_scalar(bv2[:, :], cols2[:, 2, bass.ds(GRP2 * g, GRP2)], 0.0, None, ALU.add)\
                          .then_inc(bias_in.sem, 1)
                        dve.wait_ge(bias_in.sem, s.bv + g + 1)
                    if real(i + 1, s.n):
                        norm(g + (n + 1) // GSTEPS, (n + 1) % GSTEPS)
                    if n == 8 and real(g, GROUPS2 - 1):
                        split_wv(g + 1, (2, 3))
                    if real(i + 2, s.n):
                        top(g + (n + 2) // GSTEPS, (n + 2) % GSTEPS)
                    if real(i - 2, s.n):
                        low_part(g + (n - 2) // GSTEPS, (n - 2) % GSTEPS)
                    if real(i, s.n):
                        copy(g, n)
                    if n % 2 == 0 and real(8 * g - 6 + n // 2, s.o):
                        add(g, n)
                    if n == 7 and real(g, GROUPS2 - 1):
                        split_wv(g + 1, (0, 1))
                    if n in WO_SPLIT and real(g, GROUPS2):
                        m = WO_SPLIT.index(n)
                        split(wo_hi_done.sem, s.wh + KT * g + m + 1, wo_hi[:, m, :], wo_lo[:, m, :], wo_nat[:, m, :],
                              wo_lo_done.sem)

            if opening:
                split_wv(0, range(KT))
                return
            groups(dve, body)

        def pool_att2(pool, s):
            def scale_qk(g, e):
                q = 8 * g + e
                pool.wait_ge(qk_in[e % 2].sem, s.qi[e % 2] + 64 * g + 16 * (e // 2 + 1))
                half, _, _ = place(2 * e)
                v = qk_raw[:, e % 2, :, :]
                nc.gpsimd.tensor_tensor(v, v, rms[:, :, at(half)], ALU.mult).then_inc(qk_scaled.sem, 1)

            def split_qk(g, e):
                pool.wait_ge(qk_hi_done.sem, s.qh + 8 * g + e + 1)
                nc.gpsimd.tensor_tensor(qk_lo[:, e % 2, :, :], qk_raw[:, e % 2, :, :], qk_hi[:, e % 2, :, :].bitcast(F32),
                                        ALU.subtract).then_inc(qk_lo_done.sem, 1)

            def body(g):
                for e in range(8):
                    if real(8 * g + e + 1, s.q):
                        scale_qk(g + (e + 1) // 8, (e + 1) % 8)
                    if real(8 * g + e, s.q):
                        split_qk(g, e)

            groups(pool, body)

        def sp_adapters_up(sp):
            sp.wait_ge(cleared.sem, 3)
            for n, name in enumerate(("B1", "B3")):
                sp.dma_start(b13[:, n, 0:F0], t[f"L2_ffn_lora_{name}"].rearrange("o r -> r o"), allow_slow_non_contiguous=True)\
                  .then_inc(adapters_in[0].sem, 16)
                adapters_in[0].count += 16

        def sp_adapters(sp):
            for n, dst, src in ((0, a13[:, 0, :], t["L2_ffn_lora_A1"]), (0, a13[:, 1, :], t["L2_ffn_lora_A3"]),
                                (1, a2[:, :], t["L2_ffn_lora_A2"]), (1, b2[:, :], t["L2_ffn_lora_B2"].rearrange("o r -> r o"))):
                sp.dma_start(dst, src, allow_slow_non_contiguous=True).then_inc(adapters_in[n].sem, 16)
                adapters_in[n].count += 16

        def pool_adapters(pool):
            nc.gpsimd.memset(b13[:, :, :], 0.0).then_inc(cleared.sem, 1)

        def dve_adapters(dve, n):
            a = (a13, a2)[n]
            v = a[:, :, :] if n == 0 else a[:, :]
            dve.wait_ge(adapters_in[n].sem, adapters_in[n].count)
            nc.vector.tensor_scalar(v, v, LORA, None, ALU.mult).then_inc(adapters_scaled.sem, 1)

        def rhs_xn(k, half, rows):
            return xn_hi[:, k, at(half)], xn_lo[:, k, at(half)]

        def rhs_out(m):
            return lambda k, half, rows: (m.hi[:, k, at(half)], m.lo[:, k, at(half)])

        def dest(x, c, b=None, factor=1.0):
            return lambda half: (x[:, c, at(half)], b, factor)

        def qkv0():
            found = []
            for x, name in ((at_k, "wk"), (at_q, "wq"), (at_v, "wv")):
                for c in range(QC):
                    found.append(rows_chunk(t[f"L0_attn_{name}"], c * P, tile=len(found), to=dest(x, c)))
            return found

        def qkv1():
            w = t["L1_attn_w_qkv"]
            k, v = (rows_chunk(w, D + n * P, tile=tile, to=dest(x, 0, bias1[:, QC + n:QC + n + 1]))
                    for n, x, tile in ((0, heads1.k, 0), (1, heads1.v, QC + 1)))
            found = [k]
            for c in range(QC):
                q = rows_chunk(w, 0, tile=1 + c, to=dest(heads1.q, c, bias1[:, c:c + 1]))
                q["loads"] = [(slot(slice(kv * HD, (kv + 1) * HD), slice(0, D)),
                               w[(kv * QC + c) * HD:(kv * QC + c + 1) * HD, :]) for kv in range(KV1)]
                found.append(q)
            return found + [v]

        def qkv3():
            w = t["L3_attn_wq_w"]
            q = [rows_chunk(w, c * P, tile=1 + c, to=dest(heads1.q, c, bias3[:, c:c + 1])) for c in range(QC)]
            kv = []
            for n, x, tile, name in ((0, heads1.k, 0, "wk"), (1, heads1.v, QC + 1, "wv")):
                c = rows_chunk(w, 0, tile=tile, to=dest(x, 0, bias3[:, QC + n:QC + n + 1]))
                c["loads"] = [(slot(slice(r * HD, (r + 1) * HD), slice(0, D)), t[f"L3_attn_{name}_w"]) for r in range(DUP)]
                kv.append(c)
            return [kv[0]] + q + [kv[1]]

        def wo(w, b=None, by_key_head=False):
            found = []
            for m in range(KT):
                c = rows_chunk(w, m * P, tile=m)
                if b is not None:
                    c["bias"] = b[:, QC + 2 + m:QC + 3 + m]
                if by_key_head:
                    src = w[m * P:(m + 1) * P, :].rearrange("p (v c d) -> p c v d", c=QC, d=HD)
                    c["loads"] = [(lambda j, n=n: nat[:, j, n * P:(n + 1) * P].rearrange("p (v d) -> p v d", d=HD),
                                   src[:, n, :, :]) for n in range(QC)]
                found.append(c)
            return found

        start = plan_start()
        tables_gate = plan_tables(slice(0, GROUPS_UP), "gate", hot, 0, D, F0, sgf0[:, :, :, :].rearrange("p a b c -> p (a b c)"))
        norms = [plan_norm()]
        tables_up = plan_tables(slice(32, 32 + GROUPS_UP), "up", hot, D, D, F0, tables_gate.tmp)
        tables_down = plan_tables(ROWS_DOWN, "down", hot_d, 0, F0, D, tmp_down, zero_d, scale_d)
        up0 = plan_up(F0, "dequant", PACK, t["L0_ffn_gate_qweight"], t["L0_ffn_up_qweight"], (h0_hi, h0_lo), sgf0)
        down0 = plan_proj(packed_down_chunks(t["L0_ffn_down_qweight"], F0), "dequant", KT, h_of((h0_hi, h0_lo)), "dve")
        in0 = plan_proj(qkv0(), "turn", 3 * QC, rhs_xn, "act")
        split0 = plan_split(plan_heads(in0, heads0, (C_COS0, C_SIN0, C_ROT0)))
        att0 = plan_att(heads0, split0)
        wo0 = plan_proj(wo(t["L0_attn_wo"]), "turn", KT, rhs_out(heads0), "dve")

        norms.append(plan_norm())
        up1 = plan_up(F0, "turn", 1, t["L1_ffn_W_gate"], t["L1_ffn_W_up"], (h1_hi, h1_lo), sgf1)
        down1 = plan_proj(down_chunks(t["L1_ffn_W_down"], F0), "turn", KT, h_of((h1_hi, h1_lo)), "dve")
        in1 = plan_proj(qkv1(), "turn", QC + 2, rhs_xn, "act")
        split1 = plan_split(plan_heads(in1, heads1, (C_COS1, C_SIN1, C_ROT1)))
        att1 = plan_att(heads1, split1)
        wo1 = plan_proj(wo(t["L1_attn_w_o"], bias1, True), "turn", KT, rhs_out(heads1), "dve")

        norms.append(plan_norm())
        up2 = plan_up(F0, "turn", 1, t["L2_ffn_w1"], t["L2_ffn_w3"], (h2_hi, h2_lo), sgf2, adapters=True)
        down2 = plan_proj(down_chunks(t["L2_ffn_w2"], F0, adapter=(a2, b2)), "turn", KT, h_of((h2_hi, h2_lo)), "dve")
        qk2 = plan_qk2()
        rms2 = plan_rms()
        att2 = plan_att2()

        norms.append(plan_norm())
        up3 = plan_up(F3, "scaled", 1, t["L3_ffn_w1"], t["L3_ffn_w3"], (h3_hi, h3_lo), sgf3, scales=wscale)
        down3 = plan_proj(down_chunks(t["L3_ffn_w2"], F3, scales=wscale2), "scaled", KT, h_of((h3_hi, h3_lo)), "dve")
        in3 = plan_proj(qkv3(), "turn", QC + 2, rhs_xn, "act")
        split3 = plan_split(plan_heads(in3, heads1, None))
        att3 = plan_att(heads1, split3)
        wo3 = plan_proj(wo(t["L3_attn_wo_w"], bias3), "turn", KT, rhs_out(heads1), "dve")
        end = plan_end()

        for n, first in enumerate((up0, up1, up2, up3)):
            first.norm = norms[n]

        block = ctx.enter_context(nc.Block())

        @block.sync
        def _(sp):
            sp.wait_ge(begun, 1)
            sp_start(sp)
            sp_up(sp, up0, True)
            sp_columns(sp)
            sp_up(sp, up0)
            sp_proj(sp, down0, True)
            sp_proj(sp, down0)
            sp_proj(sp, in0, True)
            sp_proj(sp, in0)
            sp_units(sp, att0)
            sp_proj(sp, wo0, True)
            sp_proj(sp, wo0)
            sp_up(sp, up1, True)
            sp_up(sp, up1)
            sp_adapters_up(sp)
            sp_proj(sp, down1, True)
            sp_proj(sp, down1)
            sp_proj(sp, in1, True)
            sp_proj(sp, in1)
            sp_att(sp, att1)
            sp_proj(sp, wo1, True)
            sp_proj(sp, wo1)
            join(sp, "wo1")
            sp_adapters(sp)
            sp_up(sp, up2, True)
            sp_up(sp, up2)
            sp_proj(sp, down2, True)
            sp_proj(sp, down2)
            sp_qk2(sp, qk2, True)
            sp_qk2(sp, qk2)
            join(sp, "qk2")
            sp_att2(sp, att2)
            sp_up(sp, up3, True)
            sp_up(sp, up3)
            sp_proj(sp, down3, True)
            sp_proj(sp, down3)
            sp_proj(sp, in3, True)
            sp_proj(sp, in3)
            sp_att(sp, att3)
            sp_proj(sp, wo3, True)
            sp_proj(sp, wo3)
            sp_end(sp, end)

        @block.tensor
        def _(pe):
            pe.wait_ge(begun, 1)
            pe_start(pe, start)
            barrier(pe, "start")
            pe_norm(pe, norms[0])
            pe.wait_ge(step_b.sem, tables_up.done)
            pe_up(pe, up0, True)
            pe_up(pe, up0)
            pe.wait_ge(step_b.sem, tables_down.done)
            pe_proj(pe, down0, True)
            barrier(pe, "up0")
            pe_proj(pe, down0)
            pe_proj(pe, in0, True)
            barrier(pe, "down0")
            pe_proj(pe, in0)
            barrier(pe, "in0")
            barrier(pe, "prep0")
            pe_att(pe, att0)
            pe_proj(pe, wo0, True)
            barrier(pe, "att0")
            pe_proj(pe, wo0)
            pe_up(pe, up1, True)
            barrier(pe, "wo0")
            pe_norm(pe, norms[1])
            pe_up(pe, up1)
            pe_proj(pe, down1, True)
            barrier(pe, "up1")
            pe_proj(pe, down1)
            pe_proj(pe, in1, True)
            barrier(pe, "down1")
            pe_proj(pe, in1)
            barrier(pe, "in1")
            barrier(pe, "prep1")
            pe_att(pe, att1)
            pe_proj(pe, wo1, True)
            barrier(pe, "att1")
            pe_proj(pe, wo1)
            barrier(pe, "wo1")
            pe_norm(pe, norms[2])
            pe_up(pe, up2, True)
            pe_up(pe, up2)
            pe_proj(pe, down2, True)
            barrier(pe, "up2")
            pe_proj(pe, down2)
            pe_qk2(pe, qk2, True)
            barrier(pe, "down2")
            pe_qk2(pe, qk2)
            barrier(pe, "qk2")
            pe_rms(pe, rms2)
            barrier(pe, "rms2")
            pe_att2(pe, att2)
            pe_up(pe, up3, True)
            barrier(pe, "att2")
            pe_norm(pe, norms[3])
            pe_up(pe, up3)
            pe_proj(pe, down3, True)
            barrier(pe, "up3")
            pe_proj(pe, down3)
            pe_proj(pe, in3, True)
            barrier(pe, "down3")
            pe_proj(pe, in3)
            barrier(pe, "in3")
            barrier(pe, "prep3")
            pe_att(pe, att3)
            pe_proj(pe, wo3, True)
            barrier(pe, "att3")
            pe_proj(pe, wo3)
            barrier(pe, "wo3")
            pe_end(pe, end)
            barrier(pe, "end")

        @block.scalar
        def _(act):
            act.wait_ge(begun, 1)
            act_start(act, start)
            barrier(act, "start")
            act_norm(act, norms[0])
            act_up(act, up0, True)
            act_up(act, up0)
            act_proj(act, down0, True)
            barrier(act, "up0")
            act_proj(act, down0)
            act_proj(act, in0, True)
            barrier(act, "down0")
            act_proj(act, in0)
            barrier(act, "in0")
            act_split(act, split0, split0.late)
            barrier(act, "prep0")
            act_att(act, att0)
            act_proj(act, wo0, True)
            barrier(act, "att0")
            act_proj(act, wo0)
            act.wait_ge(cols_in.sem, cols_in.count)
            act_up(act, up1, True)
            barrier(act, "wo0")
            act_norm(act, norms[1])
            act_up(act, up1)
            act_proj(act, down1, True)
            barrier(act, "up1")
            act_proj(act, down1)
            act_proj(act, in1, True)
            barrier(act, "down1")
            act_proj(act, in1)
            barrier(act, "in1")
            act_split(act, split1, split1.late)
            barrier(act, "prep1")
            act_att(act, att1)
            act_proj(act, wo1, True)
            barrier(act, "att1")
            act_proj(act, wo1)
            barrier(act, "wo1")
            act_norm(act, norms[2], lambda: act_up(act, up2, True))
            act_up(act, up2)
            act_proj(act, down2, True)
            barrier(act, "up2")
            act_proj(act, down2)
            act_qk2(act, qk2, True)
            barrier(act, "down2")
            act_qk2(act, qk2)
            barrier(act, "qk2")
            act_rms(act, rms2)
            act_att2(act, att2, True)
            act_rms_spread(act, rms2)
            barrier(act, "rms2")
            act_att2(act, att2)
            act_up(act, up3, True)
            barrier(act, "att2")
            act_norm(act, norms[3])
            act_up(act, up3)
            act_proj(act, down3, True)
            barrier(act, "up3")
            act_proj(act, down3)
            act_proj(act, in3, True)
            barrier(act, "down3")
            act_proj(act, in3)
            barrier(act, "in3")
            act_split(act, split3, split3.late)
            barrier(act, "prep3")
            act_att(act, att3)
            act_proj(act, wo3, True)
            barrier(act, "att3")
            act_proj(act, wo3)
            barrier(act, "wo3")
            barrier(act, "end")

        @block.vector
        def _(dve):
            dve.wait_ge(begun, 1)
            dve_start(dve)
            barrier(dve, "start")
            dve_norm(dve, norms[0], lambda: dve_tables(dve, tables_up))
            dve_up(dve, up0, True)
            dve_tables(dve, tables_down)
            dve_up(dve, up0)
            dve_proj(dve, down0, True)
            barrier(dve, "up0")
            dve_proj(dve, down0)
            dve_proj(dve, in0, True)
            barrier(dve, "down0")
            dve_proj(dve, in0)
            barrier(dve, "in0")
            dve_split(dve, split0, split0.late)
            barrier(dve, "prep0")
            dve_att(dve, att0)
            dve_proj(dve, wo0, True)
            barrier(dve, "att0")
            dve_proj(dve, wo0)
            dve_up(dve, up1, True)
            barrier(dve, "wo0")
            dve_norm(dve, norms[1])
            dve_up(dve, up1)
            dve_proj(dve, down1, True)
            barrier(dve, "up1")
            dve_proj(dve, down1)
            dve_proj(dve, in1, True)
            barrier(dve, "down1")
            dve_proj(dve, in1)
            barrier(dve, "in1")
            dve_split(dve, split1, split1.late)
            barrier(dve, "prep1")
            dve_att(dve, att1)
            dve_proj(dve, wo1, True)
            barrier(dve, "att1")
            dve_proj(dve, wo1)
            barrier(dve, "wo1")
            dve_norm(dve, norms[2], lambda: dve_adapters(dve, 0), lambda: dve_up(dve, up2, True))
            dve_adapters(dve, 1)
            dve_up(dve, up2)
            dve_proj(dve, down2, True)
            barrier(dve, "up2")
            dve_proj(dve, down2)
            dve_qk2(dve, qk2, True)
            barrier(dve, "down2")
            dve_qk2(dve, qk2)
            barrier(dve, "qk2")
            dve_rms(dve, rms2)
            dve_att2(dve, att2, True)
            dve_rms_spread(dve, rms2)
            barrier(dve, "rms2")
            dve_att2(dve, att2)
            dve_up(dve, up3, True)
            barrier(dve, "att2")
            dve_norm(dve, norms[3])
            dve_up(dve, up3)
            dve_proj(dve, down3, True)
            barrier(dve, "up3")
            dve_proj(dve, down3)
            dve_proj(dve, in3, True)
            barrier(dve, "down3")
            dve_proj(dve, in3)
            barrier(dve, "in3")
            dve_split(dve, split3, split3.late)
            barrier(dve, "prep3")
            dve_att(dve, att3)
            dve_proj(dve, wo3, True)
            barrier(dve, "att3")
            dve_proj(dve, wo3)
            barrier(dve, "wo3")
            dve_end(dve, end)
            barrier(dve, "end")

        @block.gpsimd
        def _(pool):
            for x in signals:
                pool.sem_inc(x.sem, 1)
            pool.sem_inc(begun, 1)
            barrier(pool, "start")
            pool_norm(pool, norms[0])
            pool_up(pool, up0, True)
            pool_up(pool, up0)
            barrier(pool, "up0")
            pool_proj(pool, down0)
            barrier(pool, "down0")
            pool_proj(pool, in0)
            barrier(pool, "in0")
            pool_split(pool, split0, split0.late)
            barrier(pool, "prep0")
            pool_units(pool, att0)
            barrier(pool, "att0")
            pool_proj(pool, wo0)
            barrier(pool, "wo0")
            pool_norm(pool, norms[1])
            pool_adapters(pool)
            pool_up(pool, up1)
            barrier(pool, "up1")
            pool_proj(pool, down1)
            barrier(pool, "down1")
            pool_proj(pool, in1)
            barrier(pool, "in1")
            pool_split(pool, split1, split1.late)
            barrier(pool, "prep1")
            barrier(pool, "att1")
            pool_proj(pool, wo1)
            barrier(pool, "wo1")
            pool_norm(pool, norms[2])
            pool_up(pool, up2)
            barrier(pool, "up2")
            pool_proj(pool, down2)
            barrier(pool, "down2")
            pool_qk2(pool, qk2)
            barrier(pool, "qk2")
            barrier(pool, "rms2")
            pool_att2(pool, att2)
            pool_up(pool, up3, True)
            barrier(pool, "att2")
            pool_norm(pool, norms[3])
            pool_up(pool, up3)
            pool_proj(pool, down3, True)
            barrier(pool, "up3")
            pool_proj(pool, down3)
            barrier(pool, "down3")
            pool_proj(pool, in3)
            barrier(pool, "in3")
            pool_split(pool, split3, split3.late)
            barrier(pool, "prep3")
            barrier(pool, "att3")
            pool_proj(pool, wo3)
            barrier(pool, "wo3")
            barrier(pool, "end")


def kernel(**inputs):
    import concourse.bacc as bacc
    from concourse.bass_utils import run_bass_kernel_spmd

    nc = bacc.Bacc("TRN2", target_bir_lowering=False, num_devices=1)
    arrays, t = {}, {}
    cst, shift = constants()
    for name, a in (*inputs.items(), ("cst", cst), ("shift", shift)):
        arrays[f"in_{name}"] = a = np.ascontiguousarray(a)
        t[name] = nc.dram_tensor(f"in_{name}", a.shape, mybir.dt.from_np(a.dtype), kind="ExternalInput").ap()
    out = nc.dram_tensor("out", (BATCH, SEQ, D), F32, kind="ExternalOutput").ap()
    build(nc, t, out)
    return run_bass_kernel_spmd(nc, [arrays], core_ids=[0]).results[0]["out"]
```
